# Optimizing a Trainium2 kernel written in Bass

```python
import numpy as np
import jax
import jax.numpy as jnp

def _softmax(x, axis=-1):
    return jax.nn.softmax(x, axis=axis)

def _gelu(x):
    return jax.nn.gelu(x, approximate=True)

def _silu(x):
    return jax.nn.silu(x)

def _sigmoid(x):
    return jax.nn.sigmoid(x)

def _layernorm(x, axis=-1, eps=1e-05):
    m = jnp.mean(x, axis=axis, keepdims=True)
    v = jnp.var(x, axis=axis, keepdims=True)
    return (x - m) / jnp.sqrt(v + eps)

def _scatter_add(tgt, idx, src, axis=0):
    return tgt.at[idx].add(src)

def _segment_sum(src, seg, n):
    return jax.ops.segment_sum(src, seg, n)
kernel_name = 'mk_flamingo_gated_d2_seqx_r8_92971e'

def setup_inputs(seed: int=0):
    np.random.seed(seed)
    _w = jnp.asarray

    def _rec_inputs():
        import jax
        import jax.numpy as jnp
        _rk = jax.random.key(seed)
        x = -0.0002928 + 1 * jax.random.normal(jax.random.fold_in(_rk, 1), (16, 128, 256), jnp.float32)
        _lenS = 128 - jax.random.randint(jax.random.fold_in(_rk, 7), (16,), 0, max(1, 128 // 4) + 1, jnp.int32)
        _lenS2 = 128 - jax.random.randint(jax.random.fold_in(_rk, 8), (16,), 0, max(1, 128 // 4) + 1, jnp.int32)
        fside_S2_0 = -0.00337071 + 1.01897 * jax.random.normal(jax.random.fold_in(_rk, 11), (128,), jnp.float32)
        _ctx_2048P = jax.random.normal(jax.random.fold_in(_rk, 12), (16, 16, 256), jnp.float32)
        _ctx_2048c = jax.random.dirichlet(jax.random.fold_in(_rk, 512), 0.3 * jnp.ones((16,), jnp.float32), (16, 128))
        _ctx_2048t = jnp.einsum('bsk,bkd->bsd', _ctx_2048c, _ctx_2048P)
        _ctx_2048t = _ctx_2048t * jax.lax.rsqrt(jnp.mean(jnp.square(_ctx_2048t)) + 1e-12) * 0.953939
        ctx_2048 = 0.000675642 + 1.00031 * (_ctx_2048t + 0.3 * jax.random.normal(jax.random.fold_in(_rk, 612), (16, 128, 256), jnp.float32))
        _g = jax.random.normal(jax.random.fold_in(_rk, 9001), (2, 2), jnp.float32)
        _g = jnp.sign(_g) * jnp.maximum(jnp.abs(_g), 1.0) + (_g == 0) * 1.0
        g_xattn = _g[0]
        g_ffn = _g[1]
        return (x, fside_S2_0, ctx_2048, g_xattn, g_ffn)
    x, fside_S2_0, ctx_2048, g_xattn, g_ffn = _rec_inputs()

    def _L0_xattn_setup():
        import jax, jax.numpy as jnp
        import numpy as np
        key = jax.random.key(seed)
        ks = jax.random.split(key, 5)
        B, D, L, NH = (2, 128, 256, 8)
        H = D // NH
        return {'v': jax.random.normal(ks[0], (B, D, L), jnp.float32), 'k': jax.random.normal(ks[1], (H, L), jnp.float32) * 0.1, 'bias': jax.random.normal(ks[2], (D,), jnp.float32), 'x1': jax.random.normal(ks[3], (B, D, L), jnp.float32), 'x2': jax.random.normal(ks[4], (B, D, L), jnp.float32), 'num_heads': NH}
    _L0_xattn_all = _L0_xattn_setup()
    _L0_xattn_in = {k: v for k, v in _L0_xattn_all.items() if k in ('k',)}
    del _L0_xattn_all

    def _L0_ffn_setup():
        import jax, jax.numpy as jnp
        import numpy as np
        B, S, H = (2, 128, 256)
        E, K = (8, 2)
        F = 176
        FS = 704
        NORM_TOPK = False

        def _swiglu(x, wg, wu, wd):
            return jax.nn.silu(x @ wg) * (x @ wu) @ wd
        key = jax.random.key(seed)
        ks = jax.random.split(key, 9)
        s = 0.02
        return {'hidden_states': jax.random.normal(ks[0], (B, S, H), dtype=jnp.float32), 'Wr': jax.random.normal(ks[1], (H, E), dtype=jnp.float32) * s, 'Wg': jax.random.normal(ks[2], (E, H, F), dtype=jnp.float32) * s, 'Wu': jax.random.normal(ks[3], (E, H, F), dtype=jnp.float32) * s, 'Wd': jax.random.normal(ks[4], (E, F, H), dtype=jnp.float32) * s, 'Sg': jax.random.normal(ks[5], (H, FS), dtype=jnp.float32) * s, 'Su': jax.random.normal(ks[6], (H, FS), dtype=jnp.float32) * s, 'Sd': jax.random.normal(ks[7], (FS, H), dtype=jnp.float32) * s, 'Wsg': jax.random.normal(ks[8], (H, 1), dtype=jnp.float32) * s}
    _L0_ffn_all = _L0_ffn_setup()
    _L0_ffn_in = {k: v for k, v in _L0_ffn_all.items() if k in ('Wr', 'Wg', 'Wu', 'Wd', 'Sg', 'Su', 'Sd', 'Wsg')}
    del _L0_ffn_all

    def _L1_xattn_setup():
        import math
        import jax, jax.numpy as jnp
        import numpy as np
        HEADS = 16
        MASKED_BIAS = -10000.0

        def _mha(q, k, v):
            B, Sq, D = q.shape
            Sk = k.shape[-2]
            hd = D // HEADS
            qh = q.reshape(B, Sq, HEADS, hd).transpose(0, 2, 1, 3)
            kh = k.reshape(B, Sk, HEADS, hd).transpose(0, 2, 1, 3)
            vh = v.reshape(B, Sk, HEADS, hd).transpose(0, 2, 1, 3)
            scores = jnp.einsum('bhqd,bhkd->bhqk', qh, kh) / math.sqrt(hd)
            qi = jnp.arange(Sq)[:, None] + (Sk - Sq)
            ki = jnp.arange(Sk)[None, :]
            causal = ki <= qi
            scores = jnp.where(causal[None, None], scores, jnp.asarray(MASKED_BIAS, scores.dtype))
            attn = jax.nn.softmax(scores, axis=-1)
            out = jnp.einsum('bhqk,bhkd->bhqd', attn, vh)
            return out.transpose(0, 2, 1, 3).reshape(B, Sq, D)
        key = jax.random.key(seed)
        kq, kk, kv = jax.random.split(key, 3)
        B, S, D = (4, 128, 256)
        q = jax.random.normal(kq, (B, S, D), dtype=jnp.float32)
        k = jax.random.normal(kk, (B, S, D), dtype=jnp.float32)
        v = jax.random.normal(kv, (B, S, D), dtype=jnp.float32)
        return {'q': q, 'k': k, 'v': v}
    _L1_xattn_all = _L1_xattn_setup()
    _L1_xattn_in = {k: v for k, v in _L1_xattn_all.items() if k in ()}
    del _L1_xattn_all

    def _L1_ffn_setup():
        import jax, jax.numpy as jnp
        import numpy as np
        NUM_EXPERTS = 8
        TOP_K = 2
        LORA_ALPHA = 2.0
        LORA_RANK = 16
        D_MODEL = 256
        D_HIDDEN = 704
        key = jax.random.key(seed)
        ks = jax.random.split(key, 11)
        B, S, D, H, E, R = (2, 128, D_MODEL, D_HIDDEN, NUM_EXPERTS, LORA_RANK)
        sd = 1.0 / np.sqrt(D)
        sh = 1.0 / np.sqrt(H)
        x = jax.random.normal(ks[0], (B, S, D), jnp.float32)
        gate_w = jax.random.normal(ks[1], (E, D), jnp.float32) * sd
        w_up = jax.random.normal(ks[2], (H, D), jnp.float32) * sd
        w_gate = jax.random.normal(ks[3], (H, D), jnp.float32) * sd
        w_down = jax.random.normal(ks[4], (D, H), jnp.float32) * sh
        up_A = jax.random.normal(ks[5], (E, R, D), jnp.float32) * sd
        up_B = jax.random.normal(ks[6], (E, H, R), jnp.float32) * 0.02
        gate_A = jax.random.normal(ks[7], (E, R, D), jnp.float32) * sd
        gate_B = jax.random.normal(ks[8], (E, H, R), jnp.float32) * 0.02
        down_A = jax.random.normal(ks[9], (E, R, H), jnp.float32) * sh
        down_B = jax.random.normal(ks[10], (E, D, R), jnp.float32) * 0.02
        return {'x': x, 'gate_w': gate_w, 'w_up': w_up, 'w_gate': w_gate, 'w_down': w_down, 'up_A': up_A, 'up_B': up_B, 'gate_A': gate_A, 'gate_B': gate_B, 'down_A': down_A, 'down_B': down_B}
    _L1_ffn_all = _L1_ffn_setup()
    _L1_ffn_in = {k: v for k, v in _L1_ffn_all.items() if k in ('gate_w', 'w_up', 'w_gate', 'w_down', 'up_A', 'up_B', 'gate_A', 'gate_B', 'down_A', 'down_B')}
    del _L1_ffn_all
    return {'x': x, 'fside_S2_0': fside_S2_0, 'ctx_2048': ctx_2048, 'g_xattn': g_xattn, 'g_ffn': g_ffn, 'L0_xattn_k': _L0_xattn_in['k'], 'L0_ffn_Wr': _L0_ffn_in['Wr'], 'L0_ffn_Wg': _L0_ffn_in['Wg'], 'L0_ffn_Wu': _L0_ffn_in['Wu'], 'L0_ffn_Wd': _L0_ffn_in['Wd'], 'L0_ffn_Sg': _L0_ffn_in['Sg'], 'L0_ffn_Su': _L0_ffn_in['Su'], 'L0_ffn_Sd': _L0_ffn_in['Sd'], 'L0_ffn_Wsg': _L0_ffn_in['Wsg'], 'L1_ffn_gate_w': _L1_ffn_in['gate_w'], 'L1_ffn_w_up': _L1_ffn_in['w_up'], 'L1_ffn_w_gate': _L1_ffn_in['w_gate'], 'L1_ffn_w_down': _L1_ffn_in['w_down'], 'L1_ffn_up_A': _L1_ffn_in['up_A'], 'L1_ffn_up_B': _L1_ffn_in['up_B'], 'L1_ffn_gate_A': _L1_ffn_in['gate_A'], 'L1_ffn_gate_B': _L1_ffn_in['gate_B'], 'L1_ffn_down_A': _L1_ffn_in['down_A'], 'L1_ffn_down_B': _L1_ffn_in['down_B']}

def reference(x, fside_S2_0, ctx_2048, g_xattn, g_ffn, L0_xattn_k, L0_ffn_Wr, L0_ffn_Wg, L0_ffn_Wu, L0_ffn_Wd, L0_ffn_Sg, L0_ffn_Su, L0_ffn_Sd, L0_ffn_Wsg, L1_ffn_gate_w, L1_ffn_w_up, L1_ffn_w_gate, L1_ffn_w_down, L1_ffn_up_A, L1_ffn_up_B, L1_ffn_gate_A, L1_ffn_gate_B, L1_ffn_down_A, L1_ffn_down_B):
    import jax
    import jax.numpy as jnp

    def _L0_xattn_ref(v, k, bias, x1, x2, num_heads):
        import jax, jax.numpy as jnp
        import numpy as np
        B, D, L = v.shape
        H = D // num_heads
        fft_size = 2 * L
        vr = v.reshape(B, H, num_heads, L)
        x1r = x1.reshape(B, H, num_heads, L)
        x2r = x2.reshape(B, H, num_heads, L)
        kv = vr[:, :, :, None, :] * x2r[:, :, None, :, :]
        k_f = jnp.fft.rfft(k.astype(jnp.float32), n=fft_size)
        y = jnp.fft.irfft(jnp.fft.rfft(kv, n=fft_size) * k_f[None, :, None, None, :], n=fft_size)[..., :L]
        skip = bias.astype(jnp.float32).reshape(H, num_heads)[None, :, :, None, None]
        y = y + kv * skip
        out = jnp.einsum('bhijl,bhil->bhjl', y, x1r)
        return out.reshape(B, D, L)

    def _L0_ffn_ref(hidden_states, Wr, Wg, Wu, Wd, Sg, Su, Sd, Wsg):
        import jax, jax.numpy as jnp
        import numpy as np
        B, S, H = (2, 128, 256)
        E, K = (8, 2)
        F = 176
        FS = 704
        NORM_TOPK = False

        def _swiglu(x, wg, wu, wd):
            return jax.nn.silu(x @ wg) * (x @ wu) @ wd
        b, s, h = hidden_states.shape
        x = hidden_states.reshape(-1, h)
        router_logits = x @ Wr
        probs = jax.nn.softmax(router_logits.astype(jnp.float32), axis=-1)
        routing_weights, selected = jax.lax.top_k(probs, K)
        if NORM_TOPK:
            routing_weights = routing_weights / routing_weights.sum(-1, keepdims=True)
        routing_weights = routing_weights.astype(x.dtype)
        C = jnp.einsum('tk,tke->te', routing_weights, jax.nn.one_hot(selected, E, dtype=x.dtype))
        expert_out = jax.vmap(lambda wg, wu, wd: _swiglu(x, wg, wu, wd))(Wg, Wu, Wd)
        moe_out = jnp.einsum('te,eth->th', C, expert_out)
        shared = _swiglu(x, Sg, Su, Sd)
        shared = jax.nn.sigmoid(x @ Wsg) * shared
        out = (moe_out + shared).reshape(b, s, h)
        return out

    def _L1_xattn_ref(q, k, v):
        import math
        import jax, jax.numpy as jnp
        import numpy as np
        HEADS = 16
        MASKED_BIAS = -10000.0

        def _mha(q, k, v):
            B, Sq, D = q.shape
            Sk = k.shape[-2]
            hd = D // HEADS
            qh = q.reshape(B, Sq, HEADS, hd).transpose(0, 2, 1, 3)
            kh = k.reshape(B, Sk, HEADS, hd).transpose(0, 2, 1, 3)
            vh = v.reshape(B, Sk, HEADS, hd).transpose(0, 2, 1, 3)
            scores = jnp.einsum('bhqd,bhkd->bhqk', qh, kh) / math.sqrt(hd)
            qi = jnp.arange(Sq)[:, None] + (Sk - Sq)
            ki = jnp.arange(Sk)[None, :]
            causal = ki <= qi
            scores = jnp.where(causal[None, None], scores, jnp.asarray(MASKED_BIAS, scores.dtype))
            attn = jax.nn.softmax(scores, axis=-1)
            out = jnp.einsum('bhqk,bhkd->bhqd', attn, vh)
            return out.transpose(0, 2, 1, 3).reshape(B, Sq, D)
        return _mha(q, k, v)

    def _L1_ffn_ref(x, gate_w, w_up, w_gate, w_down, up_A, up_B, gate_A, gate_B, down_A, down_B):
        import jax, jax.numpy as jnp
        import numpy as np
        NUM_EXPERTS = 8
        TOP_K = 2
        LORA_ALPHA = 2.0
        LORA_RANK = 16
        D_MODEL = 256
        D_HIDDEN = 704
        B, S, D = x.shape
        H = w_up.shape[0]
        gate_logits = jnp.einsum('bsd,ed->bse', x, gate_w)
        topw, sel = jax.lax.top_k(gate_logits, TOP_K)
        topw = jax.nn.softmax(topw.astype(jnp.float32), axis=1).astype(x.dtype)
        xt = x.reshape(-1, D)
        wf = topw.reshape(-1, TOP_K)
        sf = sel.reshape(-1, TOP_K)
        base_up = xt @ w_up.T
        base_gate = xt @ w_gate.T
        mixed_h = jnp.zeros((xt.shape[0], H), x.dtype)
        lora_down = jnp.zeros_like(xt)
        for e in range(NUM_EXPERTS):
            c = jnp.sum(jnp.where(sf == e, wf, 0.0), axis=1)
            lo_up = LORA_ALPHA * (xt @ up_A[e].T @ up_B[e].T)
            lo_gate = LORA_ALPHA * (xt @ gate_A[e].T @ gate_B[e].T)
            h_e = jax.nn.silu(base_up + lo_up) * (base_gate + lo_gate)
            ch = c[:, None] * h_e
            mixed_h = mixed_h + ch
            lora_down = lora_down + LORA_ALPHA * (ch @ down_A[e].T @ down_B[e].T)
        out = mixed_h @ w_down.T + lora_down
        return out.reshape(B, S, D)
    x = x + jnp.tanh(g_xattn[0]) * _L0_xattn_ref(_layernorm(x, axis=-1), L0_xattn_k, fside_S2_0, ctx_2048, ctx_2048, 8)
    x = x + jnp.tanh(g_ffn[0]) * _L0_ffn_ref(_layernorm(x, axis=-1), L0_ffn_Wr, L0_ffn_Wg, L0_ffn_Wu, L0_ffn_Wd, L0_ffn_Sg, L0_ffn_Su, L0_ffn_Sd, L0_ffn_Wsg)
    x = x + jnp.tanh(g_xattn[1]) * _L1_xattn_ref(_layernorm(x, axis=-1), ctx_2048, ctx_2048)
    x = x + jnp.tanh(g_ffn[1]) * _L1_ffn_ref(_layernorm(x, axis=-1), L1_ffn_gate_w, L1_ffn_w_up, L1_ffn_w_gate, L1_ffn_w_down, L1_ffn_up_A, L1_ffn_up_B, L1_ffn_gate_A, L1_ffn_gate_B, L1_ffn_down_A, L1_ffn_down_B)
    return x

_drawn_inputs = setup_inputs


def setup_inputs(seed=0):
    import zlib

    import numpy as np

    out = dict(_drawn_inputs(seed))
    spreads = {'g_ffn': (-1.0, 0.6)}
    factors = {'L0_ffn_Wr': 8.0,
     'L0_ffn_Wg': 8.0,
     'L0_ffn_Wu': 8.0,
     'L0_ffn_Wd': 8.0,
     'L0_ffn_Sg': 8.0,
     'L0_ffn_Su': 8.0,
     'L0_ffn_Sd': 8.0,
     'L0_ffn_Wsg': 8.0,
     'L1_ffn_gate_w': 8.0,
     'L1_ffn_w_up': 8.0,
     'L1_ffn_w_gate': 8.0,
     'L1_ffn_w_down': 8.0,
     'L1_ffn_up_A': 8.0,
     'L1_ffn_up_B': 8.0,
     'L1_ffn_gate_A': 8.0,
     'L1_ffn_gate_B': 8.0,
     'L1_ffn_down_A': 8.0,
     'L1_ffn_down_B': 8.0}
    for name, (base, spread) in spreads.items():
        noise = np.random.default_rng([zlib.crc32(name.encode()), seed]).standard_normal(out[name].shape)
        drawn = base * np.exp(spread * noise) if base else spread * noise
        out[name] = jnp.asarray(drawn.astype(out[name].dtype))
    for name, factor in factors.items():
        out[name] = (out[name] * factor).astype(out[name].dtype)
    return out
```

```python
from contextlib import ExitStack

import concourse.bass as bass
from concourse import mybir

F32 = mybir.dt.float32
F32R = mybir.dt.float32r
BF16 = mybir.dt.bfloat16
ALU = mybir.AluOpType
ACT = mybir.ActivationFunctionType
AX_X = mybir.AxisListType.X

P = 128
B = 16
D = 256
DT = D // P
G = 4
BG = B // G
NT = BG * P
NH0, I0 = 16, 8
HALF = I0 // 2
E = 8
RANK = 16
F0, FS = 176, 704
EJ = E * F0 // P
SJ = -(-FS // P)
TAIL = FS - (SJ - 1) * P
J0 = EJ + SJ
W0T = 4 * P + D
W1T = 4 * P + 2 * P + D + P
W1X = 4 * P + D
W1N = W1X + SJ * W1T
W1K = 8
W1C = W1N // W1K
NR = E + 2
HEADS, HD = 16, 16
HH = P // HD
VA = HD + 1
EPS = 1e-5
MASKED = -10000.0
FAR = -1e30
LORA_ALPHA = 2.0
TURN_AT = (2, 4, 6, 7)
PHASES = 4


class Count:

    def __init__(self, sem):
        self.sem, self.base, self.n = sem, 0, 0

    def mark(self, ins):
        ins.then_inc(self.sem, 1)
        self.n += 1

    def value(self):
        return self.base + self.n

    def enter(self, g, per, start):
        self.base, self.n = g * per + start, 0

    def leave(self, per, rounds, start):
        assert self.n == per, (self.n, per)
        self.base, self.n = start + per * rounds, 0


def flamingo_kernel(nc, x, ctx_nat, ctx_t, ctx_one, filt, bias, gates, w0, wr, w1, gw, ramp_in, out):
    es = ExitStack()
    with es:
        sb = lambda name, shape, dt=F32: es.enter_context(nc.sbuf_tensor(name, shape, dt))
        sem = lambda name: es.enter_context(nc.semaphore(name))
        bank = [es.enter_context(nc.psum_tensor(f"bank{i}", [P, 1024], F32)) for i in range(4)]

        X = sb("X", [P, B, D])
        ident = sb("ident", [P, P])
        identb = sb("identb", [P, P], BF16)
        ones_blk = sb("ones_blk", [P, NH0, I0])
        neg = sb("neg", [P, 4, P], BF16)
        bias_c = sb("bias_c", [P, 1])
        gate_in = sb("gate_in", [P, 4])
        gate = sb("gate", [P, 4])
        ramp = sb("ramp", [P, E])
        wr_sb = sb("wr_sb", [P, DT, NR])
        gw_sb = sb("gw_sb", [P, DT, E])
        st = sb("st", [P, BG, 6])
        mv = sb("mv", [P, BG, 2])
        ve = sb("ve", [P, BG])
        scrap = sb("scrap", [P, 1])
        sd = sb("sd", [P, BG])
        rs = sb("rs", [P, BG])
        nb = sb("nb", [P, BG])
        small = sb("small", [P, 384])
        A1 = sb("A1", [P, 17792])
        R1 = sb("R1", [P, 2 * J0 * W0T + 4 * NT + 4 * NT], F32R)

        def carve(t, sizes):
            views, at = [], 0
            for n in sizes:
                views.append(t[:, at:at + n])
                at += n
            return views

        (toep, ctxN, ctxT, vN, vT, kv_, zr_, z4, stg_) = carve(
            A1, [NH0 * 2 * P, BG * D, BG * D, BG * D, BG * D, 1024, 1024, 8 * HALF * P, 2 * W0T])
        toep = toep.rearrange("p (h c) -> p h c", h=NH0)
        ctxN = ctxN.rearrange("p (b d) -> p b d", b=BG)
        vN = vN.rearrange("p (b d) -> p b d", b=BG)
        ctxT = ctxT.rearrange("p (q t) -> p q t", t=P)
        vT = vT.rearrange("p (q t) -> p q t", t=P)
        kv = kv_.rearrange("p (u q i j) -> p u q i j", u=2, q=8, i=I0)
        zr = zr_.rearrange("p (u q i j) -> p u q i j", u=2, q=8, i=I0)
        z4 = z4.rearrange("p (q i t) -> p q i t", q=8, i=HALF)
        stg = stg_.rearrange("p (u n) -> p u n", u=2)
        yb = [bank[0][:, 0:512], bank[0][:, 512:1024]]
        TV, WB, OB = bank[1], bank[2], bank[3]

        nW0 = J0 * W0T
        w0H = R1[:, 0:nW0].rearrange("p (j n) -> p j n", j=J0)
        w0L = R1[:, nW0:2 * nW0].rearrange("p (j n) -> p j n", j=J0)
        r_at = 2 * nW0
        xH = R1[:, r_at:r_at + DT * NT].rearrange("p (k t) -> p k t", k=DT)
        xL = R1[:, r_at + 2 * NT:r_at + 4 * NT].rearrange("p (k t) -> p k t", k=DT)
        hH = R1[:, r_at + 4 * NT:r_at + 6 * NT].rearrange("p (u t) -> p u t", u=2)
        hL = R1[:, r_at + 6 * NT:r_at + 8 * NT].rearrange("p (u t) -> p u t", u=2)

        xn, xT = (A1[:, at:at + BG * D] for at in (NH0 * 2 * P, NH0 * 2 * P + 2 * BG * D))
        xn = xn.rearrange("p (b d) -> p b d", b=BG)
        spread = A1[:, NH0 * 2 * P:NH0 * 2 * P + 2 * NT].rearrange("p (r b t) -> p r b t", r=2, b=BG)
        xT = xT.rearrange("p (k t) -> p k t", k=DT)
        b_silu, b_scaled = (A1[:, i * 2 * NT:(i + 1) * 2 * NT].rearrange("p (u t) -> p u t", u=2) for i in range(2))
        b_h, b_comb = (A1[:, i * 2 * NT:(i + 1) * 2 * NT].rearrange("p (u t) -> p u t", u=2) for i in (2, 3))
        G_, U_ = [bank[0][:, 0:512], bank[1][:, 0:512]], [bank[0][:, 512:1024], bank[1][:, 512:1024]]
        TP, DN = bank[2], bank[3]
        (lg, es_, eq, rk, oh1, oh2, l2) = carve(small, [BG * NR, BG * (E + 1), BG * E, BG * E, BG * E, BG * E, BG * E])
        m1, m2, den, rcp = carve(small[:, 40 + 36 + 160:], [BG, BG, 2 * BG, 2 * BG])
        lg = lg.rearrange("p (b e) -> p b e", b=BG)
        es_ = es_.rearrange("p (b e) -> p b e", b=BG)
        eq, rk, oh1, oh2, l2 = (v.rearrange("p (b e) -> p b e", b=BG) for v in (eq, rk, oh1, oh2, l2))

        E_, PT_ = (A1[:, i * 2048:(i + 1) * 2048].rearrange("p (u h k) -> p u h k", u=2, h=HH) for i in range(2))
        qT = A1[:, 4096:5120].rearrange("p (b k t) -> p b k t", b=BG, k=DT)
        qn = A1[:, 5120:6144].rearrange("p (b d) -> p b d", b=BG)
        kbd_ = A1[:, 7168:15360]
        kbd = kbd_.rearrange("p (r b k h t) -> p r b k h t", r=2, b=2, k=DT, h=HH)
        va = A1[:, 15360:15360 + BG * HEADS * VA].rearrange("p (r b h e) -> p r b h e", r=2, b=2, h=HEADS)
        stg1 = [A1[:, 6144:6144 + W1C], A1[:, 16448:16448 + W1C]]
        otmp = A1[:, 16448 + W1C:16448 + W1C + D].rearrange("p (h e) -> p h e", h=HEADS)
        (mx_, r16) = carve(small, [2 * HH, HEADS])
        mx = mx_.rearrange("p (u h) -> p u h", u=2)
        S_, PTP, O_, TQ = bank[0:2], bank[2], bank[3][:, 0:HEADS * VA], bank[3][:, 512:512 + D]
        w1H, w1L = R1[:, 0:W1N], R1[:, W1N:2 * W1N]

        (dx_, dxT_, dspread_, dcb_, dM_, dz_, dsilu_, dscaled_, dc1_, dc2_, dw_) = carve(
            A1, [1024, 1024, 2048, 1024, 1536, 2048, 1024, 1024, 1024, 1024, 1536])
        dxn = dx_.rearrange("p (b d) -> p b d", b=BG)
        dxT = dxT_.rearrange("p (k t) -> p k t", k=DT)
        dspread = dspread_.rearrange("p (m r b t) -> p m r b t", m=2, r=2, b=BG)
        dcb = dcb_.rearrange("p (r t) -> p r t", r=2)
        dM = dM_.rearrange("p (r t) -> p r t", r=3)
        dz = dz_.rearrange("p (r t) -> p r t", r=4)
        dsilu, dscaled, dc1, dc2 = (v.rearrange("p (u t) -> p u t", u=2) for v in (dsilu_, dscaled_, dc1_, dc2_))
        dw = dw_.rearrange("p (r t) -> p r t", r=3)
        cT = A1[0:2 * BG, 15360:15360 + P]
        d_at = 2 * W1N
        dzH = R1[:, d_at:d_at + 4 * NT].rearrange("p (r t) -> p r t", r=4)
        dzL = R1[:, d_at + 4 * NT:d_at + 8 * NT].rearrange("p (r t) -> p r t", r=4)
        dsH, dsL, dcH, dcL = (R1[:, d_at + i * NT:d_at + (i + 2) * NT].rearrange("p (u t) -> p u t", u=2)
                              for i in (8, 10, 12, 14))
        dwH, dwL = R1[:, d_at + 16 * NT:d_at + 17 * NT], R1[:, d_at + 17 * NT:d_at + 18 * NT]
        assert d_at + 18 * NT <= r_at
        mneg, mtop, msum, mrcp = (small[0:2 * BG, 300 + i:301 + i] for i in range(4))

        def w1_tile(j, at, n):
            a0 = W1X + j * W1T + at
            return w1H[:, a0:a0 + n], w1L[:, a0:a0 + n]

        EV = [(0, 0)]
        for j in range(1, SJ):
            EV += [(j, 0), (j - 1, 1)]
        EV.append((SJ - 1, 1))
        NE = len(EV)
        at_ev = {ev: i for i, ev in enumerate(EV)}

        consts_ready = sem("consts_ready")
        x0_loaded, xrest_loaded = sem("x0_loaded"), sem("xrest_loaded")
        small_loaded, toep_loaded = sem("small_loaded"), sem("toep_loaded")
        ctxN_loaded, ctxT_loaded = sem("ctxN_loaded"), sem("ctxT_loaded")
        stg_loaded = [sem("stg_loaded0"), sem("stg_loaded1")]
        wH_ready, wL_ready = sem("wH_ready"), sem("wL_ready")
        gate_ready = sem("gate_ready")
        dve_step = sem("dve_step")
        ve_ready, sd_ready, ln_ready, vN_ready = sem("ve_ready"), sem("sd_ready"), sem("ln_ready"), sem("vN_ready")
        vtp_ready, vT_ready, bvx_ready, w_ready, t_done = (
            sem("vtp_ready"), sem("vT_ready"), sem("bvx_ready"), sem("w_ready"), sem("t_done"))
        kv_ready, y_ready, z_ready, z4_ready, o_ready, a_done = (
            sem("kv_ready"), sem("y_ready"), sem("z_ready"), sem("z4_ready"), sem("o_ready"), sem("a_done"))
        xturned, xT_ready, xH_ready, xL_ready = sem("xturned"), sem("xT_ready"), sem("xH_ready"), sem("xL_ready")
        logits_ready, expin_ready, exp_ready, spread_ready, spread_turned, comb_ready = (
            sem("logits_ready"), sem("expin_ready"), sem("exp_ready"), sem("spread_ready"), sem("spread_turned"),
            sem("comb_ready"))
        gu_ready, silu_ready, scaled_ready, h_ready, hH_ready, hL_ready, down_done, b_done = (
            sem("gu_ready"), sem("silu_ready"), sem("scaled_ready"), sem("h_ready"), sem("hH_ready"), sem("hL_ready"),
            sem("down_done"), sem("b_done"))
        kbd_zeroed, qT_turned, qT_ready = sem("kbd_zeroed"), sem("qT_turned"), sem("qT_ready")
        kbd_loaded = [sem("kbd_loaded0"), sem("kbd_loaded1")]
        va_loaded = [sem("va_loaded0"), sem("va_loaded1")]
        stg1_loaded = [sem("stg1_loaded0"), sem("stg1_loaded1")]
        w1H_ready, w1L_ready = sem("w1H_ready"), sem("w1L_ready")
        scores_ready, shifted, exp_done, p_turned, pT_ready, pv_done, o_read, c_done = (
            sem("scores_ready"), sem("shifted"), sem("exp_done"), sem("p_turned"), sem("pT_ready"), sem("pv_done"),
            sem("o_read"), sem("c_done"))
        d_logits, tops_ready, tops_turned, topmax_ready, cexp_ready, c_ready, c_back, dspread_ready = (
            sem("d_logits"), sem("tops_ready"), sem("tops_turned"), sem("topmax_ready"), sem("cexp_ready"),
            sem("c_ready"), sem("c_back"), sem("dspread_ready"))
        dturned, dcb_ready, dM_ready, dMD_ready, z_psum, zm_ready, zH_ready, zL_ready = (
            sem("dturned"), sem("dcb_ready"), sem("dM_ready"), sem("dMD_ready"), sem("z_psum"), sem("zm_ready"),
            sem("zH_ready"), sem("zL_ready"))
        ev_ready, dsilu_ready, dscaled_ready, ch_ready, sum_ready = (
            sem("ev_ready"), sem("dsilu_ready"), sem("dscaled_ready"), sem("ch_ready"), sem("sum_ready"))
        cH_ready, cL_ready, sH_ready, sL_ready, ddown_done = (
            sem("cH_ready"), sem("cL_ready"), sem("sH_ready"), sem("sL_ready"), sem("ddown_done"))
        w_mixed, w_sum, wsH_ready, wsL_ready, dn_ready, d_done = (
            sem("w_mixed"), sem("w_sum"), sem("wsH_ready"), sem("wsL_ready"), sem("dn_ready"), sem("d_done"))
        out_stored = sem("out_stored")

        block = es.enter_context(nc.Block())
        CH = 4

        @block.sync
        def _(sp):
            sp.dma_start(X[:, 0:BG, :], x[0:BG].rearrange("b p d -> p b d")).then_inc(x0_loaded, 16)
            sp.dma_start(ctxN, ctx_nat[0:BG].rearrange("b p d -> p b d")).then_inc(ctxN_loaded, 16)
            sp.dma_start(ctxT, ctx_t[0].rearrange("p q t -> p q t")).then_inc(ctxT_loaded, 16)
            sp.dma_start(bias_c[:], bias.rearrange("(p a) -> p a", a=1)).then_inc(small_loaded, 16)
            sp.dma_start(gate_in[:], gates.partition_broadcast(P)).then_inc(small_loaded, 16)
            sp.dma_start(ramp[:], ramp_in.partition_broadcast(P)).then_inc(small_loaded, 16)
            sp.dma_start(toep, filt).then_inc(toep_loaded, 16)
            sp.dma_start(X[:, BG:B, :], x[BG:B].rearrange("b p d -> p b d")).then_inc(xrest_loaded, 16)
            sp.dma_start(wr_sb[:], wr.rearrange("p (k n) -> p k n", k=DT)).then_inc(small_loaded, 16)
            sp.dma_start(gw_sb[:], gw.rearrange("p (k n) -> p k n", k=DT)).then_inc(small_loaded, 16)

            def weights(c, first=False):
                u = c[1] % 2
                n = c[0] * CH + c[1]
                if not first:
                    sp.wait_ge(wL_ready, n - 1)
                sp.dma_start(stg[:, u, :], w0[n]).then_inc(stg_loaded[u], 16)

            weights((0, 0), True)
            weights((0, 1), True)

            def loads(g, n_chunks, more):
                for c in range(n_chunks):
                    weights((g, c + 2))
                if more:
                    sp.wait_ge(t_done, g + 1)
                    sp.dma_start(ctxN, ctx_nat[bass.ds((g + 1) * BG, BG)].rearrange("b p d -> p b d")
                                 ).then_inc(ctxN_loaded, 16)
                    sp.wait_ge(z_ready, 1 + NH0 * (g + 1))
                    sp.dma_start(ctxT, ctx_t[bass.ds(g + 1, 1)].rearrange("a p q t -> (a p) q t")
                                 ).then_inc(ctxT_loaded, 16)
            with sp.Fori(0, G - 1) as g:
                loads(g, CH, True)
            loads(G - 1, J0 - CH * (G - 1) - 2, False)
            sp.wait_ge(a_done, 1 + 2 * G)
            if PHASES == 2:
                sp.wait_ge(b_done, 1 + 2 * G)

            def keys(g, r):
                src = ctx_t[bass.ds(g, 1)].rearrange("a p (k b) t -> (a p) b k t", k=DT)
                for h in range(HH):
                    for b in range(2):
                        sp.dma_start(kbd[h * HD:(h + 1) * HD, r, b, :, h, :],
                                     src[h * HD:(h + 1) * HD, 2 * r + b, :, :]).then_inc(kbd_loaded[r], 16)

            def values(g, r):
                sp.dma_start(va[:, r], ctx_one[bass.ds(g * BG + 2 * r, 2)].rearrange("b p h e -> p b h e")
                             ).then_inc(va_loaded[r], 16)

            def weights1(g, r):
                if not isinstance(g, int) or g > 0:
                    sp.wait_ge(w1L_ready, 2 * g + r - 1)
                sp.dma_start(stg1[r], w1[bass.ds(2 * g + r, 1)].rearrange("a p n -> (a p) n")
                             ).then_inc(stg1_loaded[r], 16)

            if PHASES > 2:
                sp.wait_ge(kbd_zeroed, J0 - 1)
                for r in range(2):
                    keys(0, r)
                    values(0, r)
                sp.wait_ge(b_done, 1 + 2 * G)
                for r in range(2):
                    weights1(0, r)
                with sp.Fori(0, G - 1) as g:
                    for r in range(2):
                        sp.wait_ge(scores_ready, 8 * g + 4 * r + 4)
                        keys(g + 1, r)
                        weights1(g + 1, r)
                        sp.wait_ge(pv_done, 1 + 8 * g + 4 * r + 4)
                        values(g + 1, r)
                sp.wait_ge(c_done, B)
            if PHASES > 3:
                with sp.Fori(0, G) as g:
                    sp.wait_ge(d_done, 1 + 2 * (g + 1))
                    sp.dma_start(out[bass.ds(g * BG, BG)].rearrange("b p d -> p b d"), X[:, bass.ds(g * BG, BG), :]
                                 ).then_inc(out_stored, 16)
                sp.wait_ge(out_stored, 16 * G)
            else:
                sp.dma_start(out.rearrange("b p d -> p b d"), X[:]).then_inc(out_stored, 16)
                sp.wait_ge(out_stored, 16)

        @block.gpsimd
        def _(pool):
            for counted in (y_ready, z_ready, o_ready, a_done, h_ready, down_done, b_done,
                            o_read, pv_done, dscaled_ready, w_mixed, dn_ready, zL_ready, d_done):
                pool.sem_inc(counted, 1)
            c = Count(consts_ready)
            c.mark(nc.gpsimd.memset(ident[:], 0.0))
            c.mark(nc.gpsimd.memset(ones_blk[:], 1.0))
            c.mark(nc.gpsimd.memset(neg[:], 0.0))
            pool.wait_ge(consts_ready, 3)
            c.mark(nc.gpsimd.affine_select(out=ident[:], in_=ident[:], compare_op=ALU.not_equal, fill=1.0, base=0,
                                           pattern=[[-1, P]], channel_multiplier=1))
            c.mark(nc.gpsimd.affine_select(out=ones_blk[:], in_=ones_blk[:], compare_op=ALU.is_ge, fill=0.0, base=0,
                                           pattern=[[-I0, NH0], [0, I0]], channel_multiplier=1))
            c.mark(nc.gpsimd.affine_select(out=neg[:], in_=neg[:], compare_op=ALU.is_ge, fill=FAR, base=0,
                                           pattern=[[0, 4], [-1, P]], channel_multiplier=1))
            pool.wait_ge(consts_ready, 6)
            c.mark(nc.gpsimd.affine_select(out=ones_blk[:], in_=ones_blk[:], compare_op=ALU.is_ge, fill=0.0,
                                           base=I0 - 1, pattern=[[I0, NH0], [0, I0]], channel_multiplier=-1))
            c.mark(nc.gpsimd.tensor_copy(identb[:], ident[:]))

            def split_low(g, c):
                n = g * CH + c
                pool.wait_ge(wH_ready, n + 1)
                nc.gpsimd.tensor_tensor(w0L[:, bass.ds(n, 1), :], stg[:, c % 2:c % 2 + 1, :],
                                        w0H[:, bass.ds(n, 1), :].bitcast(F32), ALU.subtract).then_inc(wL_ready, 1)
            with pool.Fori(0, G - 1) as g:
                for c in range(CH):
                    split_low(g, c)
            for c in range(J0 - CH * (G - 1)):
                split_low(G - 1, c)

            def b_scale(g, j):
                pr = TAIL if j == J0 - 1 else P
                pool.wait_ge(silu_ready, J0 * g + j + 1)
                if j == 0:
                    pool.wait_ge(comb_ready, g + 1)
                if j >= 2:
                    pool.wait_ge(h_ready, 1 + J0 * g + j - 1)
                else:
                    pool.wait_ge(h_ready, 1 + J0 * g)
                nc.gpsimd.tensor_tensor(b_scaled[0:pr, j % 2], b_silu[0:pr, j % 2],
                                        b_comb[0:pr, 0 if j < EJ else 1], ALU.mult).then_inc(scaled_ready, 1)
            if PHASES > 1:
                with pool.Fori(0, G - 1) as g:
                    for j in range(J0):
                        b_scale(g, j)
                for j in range(J0):
                    b_scale(G - 1, j)
                    if j < J0 - 1 and PHASES > 2:
                        nc.gpsimd.memset(kbd_[:, j * 512:(j + 1) * 512], 0.0).then_inc(kbd_zeroed, 1)

            def split_low1(g, r):
                n = 2 * g + r
                pool.wait_ge(w1H_ready, n + 1)
                dst = bass.ds(n * W1C, W1C)
                nc.gpsimd.tensor_tensor(w1L[:, dst], stg1[r], w1H[:, dst].bitcast(F32), ALU.subtract
                                        ).then_inc(w1L_ready, 1)
            if PHASES > 2:
                with pool.Fori(0, G) as g:
                    for r in range(2):
                        split_low1(g, r)

            def d_scale(g, i):
                j, k = EV[i]
                pr = TAIL if j == SJ - 1 else P
                pool.wait_ge(dsilu_ready, NE * g + i + 1)
                if i >= 2:
                    pool.wait_ge(ch_ready, NE * g + i - 1)
                nc.gpsimd.tensor_tensor(dscaled[0:pr, i % 2], dsilu[0:pr, i % 2], dcb[0:pr, k], ALU.mult
                                        ).then_inc(dscaled_ready, 1)

            if PHASES > 3:
                with pool.Fori(0, G) as g:
                    pool.wait_ge(dM_ready, g + 1)
                    nc.gpsimd.tensor_tensor(dM[:, 2], dM[:, 1], dM[:, 0], ALU.subtract).then_inc(dMD_ready, 1)
                    for r in range(4):
                        pool.wait_ge(zH_ready, 4 * g + r + 1)
                        nc.gpsimd.tensor_tensor(dzL[:, r], dz[:, r], dzH[:, r].bitcast(F32), ALU.subtract
                                                ).then_inc(zL_ready, 1)
                    pool.wait_ge(dcb_ready, g + 1)
                    for i in range(NE):
                        d_scale(g, i)

        @block.scalar
        def _(act):
            act.wait_ge(small_loaded, 80)
            nc.scalar.activation(gate[:], gate_in[:], ACT.Tanh).then_inc(gate_ready, 1)

            def normed(g, dst, phase=0):
                act.wait_ge(ve_ready, G * phase + g + 1)
                nc.scalar.activation(sd[:], ve[:], ACT.Sqrt).then_inc(sd_ready, 1)
                act.wait_ge(ln_ready, G * phase + g + 1)
                for b in range(BG):
                    nc.scalar.activation(dst[:, b:b + 1, :], X[:, bass.ds(g * BG + b, 1), :], ACT.Identity,
                                         bias=nb[:, b:b + 1], scale=rs[:, b:b + 1]).then_inc(vN_ready, 1)

            def a_prep(g, first=False):
                if not first:
                    act.wait_ge(w_ready, g)
                normed(g, vN)

            def a_turned(g, first=False):
                act.wait_ge(vtp_ready, g + 1)
                if not first:
                    act.wait_ge(kv_ready, NH0 * g)
                for k in range(DT):
                    nc.scalar.activation(vT[:, k * BG:(k + 1) * BG, :], TV[:, k * NT:(k + 1) * NT], ACT.Copy
                                         ).then_inc(vT_ready, 1)

            def split_high(g, c):
                n = g * CH + c
                act.wait_ge(stg_loaded[c % 2], (g * (CH // 2) + c // 2 + 1) * 16)
                nc.scalar.activation(w0H[:, bass.ds(n, 1), :], stg[:, c % 2:c % 2 + 1, :], ACT.Copy).then_inc(wH_ready, 1)

            a_prep(0, True)
            a_turned(0, True)
            with act.Fori(0, G - 1) as g:
                a_prep(g + 1)
                for c in range(CH):
                    split_high(g, c)
                a_turned(g + 1)
            def b_norm(g):
                if isinstance(g, int) and g == 0:
                    act.wait_ge(t_done, G)
                else:
                    act.wait_ge(spread_turned, g)
                normed(g, xn, 1)

            def b_turned(g):
                act.wait_ge(xturned, g + 1)
                act.wait_ge(xL_ready, 2 * g)
                nc.scalar.activation(xT, TP[:].rearrange("p (k t) -> p k t", k=DT), ACT.Copy).then_inc(xT_ready, 1)

            def b_exp(g):
                act.wait_ge(expin_ready, g + 1)
                nc.scalar.activation(es_, es_, ACT.Exp).then_inc(exp_ready, 1)

            def b_enter(g):
                act.wait_ge(gu_ready, J0 * g)
                act.wait_ge(xT_ready, g + 1)
                for k in range(DT):
                    nc.scalar.activation(xH[:, k], xT[:, k], ACT.Copy).then_inc(xH_ready, 1)
                act.wait_ge(spread_turned, g + 1)
                act.wait_ge(scaled_ready, J0 * g)
                nc.scalar.activation(b_comb, TP[:].rearrange("p (r t) -> p r t", r=2), ACT.Copy).then_inc(comb_ready, 1)

            def b_silu_of(g, j):
                pr = TAIL if j == J0 - 1 else P
                act.wait_ge(gu_ready, J0 * g + j + 1)
                if j >= 2:
                    act.wait_ge(scaled_ready, J0 * g + j - 1)
                nc.scalar.activation(b_silu[0:pr, j % 2], G_[j % 2][0:pr], ACT.Silu).then_inc(silu_ready, 1)

            def b_high(g, j):
                pr = TAIL if j == J0 - 1 else P
                act.wait_ge(h_ready, 1 + J0 * g + j + 1)
                if j >= 2:
                    act.wait_ge(down_done, 1 + J0 * g + j - 1)
                else:
                    act.wait_ge(down_done, 1 + J0 * g)
                nc.scalar.activation(hH[0:pr, j % 2], b_h[0:pr, j % 2], ACT.Copy).then_inc(hH_ready, 1)

            def b_tiles(g, more):
                for j in range(J0):
                    b_silu_of(g, j)
                    if j >= 1:
                        b_high(g, j - 1)
                    if more and j == 2:
                        b_norm(g + 1)
                    if more and j == 6:
                        b_turned(g + 1)
                    if more and j == 9:
                        b_exp(g + 1)
                    if not more and j == 9 and PHASES > 2:
                        normed(0, qn, 2)
                b_high(g, J0 - 1)

            for c in range(J0 - CH * (G - 1)):
                split_high(G - 1, c)
                if PHASES > 1:
                    if c == 1:
                        b_norm(0)
                    if c == 2:
                        b_turned(0)
                    if c == 4:
                        b_exp(0)
            if PHASES > 1:
                act.wait_ge(a_done, 1 + 2 * G)
                b_enter(0)
                with act.Fori(0, G - 1) as g:
                    b_tiles(g, True)
                    b_enter(g + 1)
                b_tiles(G - 1, False)

            def c_high(g, r):
                n = 2 * g + r
                act.wait_ge(stg1_loaded[r], 16 * (g + 1))
                nc.scalar.activation(w1H[:, bass.ds(n * W1C, W1C)], stg1[r], ACT.Copy).then_inc(w1H_ready, 1)

            def c_exp(g, k):
                n = 8 * g + k
                act.wait_ge(shifted, n + 1)
                nc.scalar.activation(E_[:, k % 2], E_[:, k % 2], ACT.Exp).then_inc(exp_done, 1)

            def c_evac(g, k):
                n = 8 * g + k
                act.wait_ge(p_turned, n + 1)
                if isinstance(n, int) and n < 2:
                    pass
                else:
                    act.wait_ge(pv_done, 1 + n - 1)
                nc.scalar.activation(PT_[:, k % 2], PTP[:].rearrange("p (h k) -> p h k", h=HH), ACT.Copy
                                     ).then_inc(pT_ready, 1)

            def c_take_q(g, b):
                act.wait_ge(qT_turned, BG * g + b + 1)
                act.wait_ge(scores_ready, 8 * (g - 1) + 2 * b + 2)
                nc.scalar.activation(qT[:, b], TQ.rearrange("p (k t) -> p k t", k=DT), ACT.Copy).then_inc(qT_ready, 1)

            def c_steps(g, more):
                if more:
                    act.wait_ge(qT_turned, BG * (g + 1))
                    normed(g + 1, qn, 2)
                for k in range(8):
                    if k < 7 or more:
                        c_evac(g + (k + 1) // 8, (k + 1) % 8)
                    if k < 6 or more:
                        c_exp(g + (k + 2) // 8, (k + 2) % 8)
                    if more and k in TURN_AT:
                        c_take_q(g + 1, TURN_AT.index(k))
                    if k in (3, 6):
                        c_high(g, k // 4)

            if PHASES > 2:
                act.wait_ge(qT_turned, BG)
                act.wait_ge(b_done, 1 + 2 * G)
                for b in range(BG):
                    nc.scalar.activation(qT[:, b], bank[2][:, b * D:(b + 1) * D].rearrange("p (k t) -> p k t", k=DT),
                                         ACT.Copy).then_inc(qT_ready, 1)
                c_exp(0, 0)
                c_exp(0, 1)
                c_evac(0, 0)
                c_first = True
                with act.Fori(0, G - 1) as g:
                    c_steps(g, True)
                c_steps(G - 1, False)

            def d_prep(g):
                act.wait_ge(xturned, G + g)
                normed(g, dxn, 3)
                act.wait_ge(xturned, G + g + 1)
                act.wait_ge(xL_ready, 2 * (G + g))
                nc.scalar.activation(dxT, bank[0][:].rearrange("p (k t) -> p k t", k=DT), ACT.Copy
                                     ).then_inc(xT_ready, 1)
                act.wait_ge(xT_ready, G + g + 1)
                for k in range(DT):
                    nc.scalar.activation(xH[:, k], dxT[:, k], ACT.Copy).then_inc(xH_ready, 1)
                act.wait_ge(topmax_ready, g + 1)
                nc.scalar.activation(cT, bank[1][0:2 * BG, 64:64 + P], ACT.Exp, bias=mneg, accum_out=msum
                                     ).then_inc(cexp_ready, 1)
                act.wait_ge(c_ready, g + 1)
                nc.scalar.activation(cT, cT, ACT.Copy, scale=mrcp).then_inc(cexp_ready, 1)
                act.wait_ge(dturned, 2 * g + 1)
                act.wait_ge(dscaled_ready, 1 + NE * g)
                nc.scalar.activation(dcb, bank[0][:].rearrange("p (r t) -> p r t", r=2), ACT.Copy
                                     ).then_inc(dcb_ready, 1)
                act.wait_ge(dturned, 2 * g + 2)
                act.wait_ge(w_mixed, 1 + 2 * g)
                nc.scalar.activation(dM[:, 0:2], bank[1][:].rearrange("p (r t) -> p r t", r=2), ACT.Copy
                                     ).then_inc(dM_ready, 1)
                act.wait_ge(dn_ready, 1 + g)
                for r in range(4):
                    act.wait_ge(zm_ready, 4 * g + r + 1)
                    nc.scalar.activation(dzH[:, r], dz[:, r], ACT.Copy).then_inc(zH_ready, 1)

            def d_silu(g, i):
                j, k = EV[i]
                pr = TAIL if j == SJ - 1 else P
                act.wait_ge(ev_ready, NE * g + i + 1)
                if i >= 2:
                    act.wait_ge(dscaled_ready, 1 + NE * g + i - 1)
                nc.scalar.activation(dsilu[0:pr, i % 2], U_[j % 2][0:pr], ACT.Silu).then_inc(dsilu_ready, 1)

            def d_high(g, i):
                j, k = EV[i]
                pr = TAIL if j == SJ - 1 else P
                if j >= 2:
                    act.wait_ge(ddown_done, SJ * g + j - 1)
                if k == 0:
                    act.wait_ge(ch_ready, NE * g + i + 1)
                    nc.scalar.activation(dcH[0:pr, j % 2], dc1[0:pr, j % 2], ACT.Copy).then_inc(cH_ready, 1)
                else:
                    act.wait_ge(sum_ready, SJ * g + j + 1)
                    nc.scalar.activation(dsH[0:pr, j % 2], dc2[0:pr, j % 2], ACT.Copy).then_inc(sH_ready, 1)

            if PHASES > 3:
                act.wait_ge(c_done, B)
                with act.Fori(0, G) as g:
                    d_prep(g)
                    for i in range(NE):
                        d_silu(g, i)
                        if i >= 1:
                            d_high(g, i - 1)
                    d_high(g, NE - 1)
                    act.wait_ge(w_sum, g + 1)
                    nc.scalar.activation(dwH, dw[:, 2], ACT.Copy).then_inc(wsH_ready, 1)

        @block.vector
        def _(dve):
            step = Count(dve_step)

            def link(ins):
                step.mark(ins)
                dve.wait_ge(dve_step, step.value())

            def stats(g, gain, phase=0):
                for b in range(BG):
                    step.mark(nc.vector.bn_stats(st[:, b, :], X[:, bass.ds(g * BG + b, 1), :]))
                dve.wait_ge(dve_step, step.value())
                step.mark(nc.vector.memset(scrap[:], 0.0))
                for b in range(BG):
                    step.mark(nc.vector.bn_aggr(mv[:, b, :], st[:, b, :]))
                dve.wait_ge(dve_step, step.value())
                nc.vector.tensor_scalar(ve[:], mv[:, :, 1], EPS, None, ALU.add).then_inc(ve_ready, 1)
                dve.wait_ge(sd_ready, G * phase + g + 1)
                link(nc.vector.reciprocal(rs[:], sd[:]))
                if gain is not None:
                    link(nc.vector.tensor_scalar(rs[:], rs[:], gain, None, ALU.mult))
                nc.vector.scalar_tensor_tensor(out=nb[:], in0=mv[:, :, 0], scalar=-1.0, in1=rs[:],
                                               op0=ALU.mult, op1=ALU.mult).then_inc(ln_ready, 1)

            def a_kv(g, h):
                u = h % 2
                t0 = h * I0
                if h >= 2:
                    dve.wait_ge(y_ready, 1 + NH0 * g + h - 1)
                else:
                    dve.wait_ge(y_ready, 1 + NH0 * g)
                nc.vector.tensor_tensor(
                    kv[:, u], vT[:, :, t0:t0 + I0].unsqueeze(3).to_broadcast([P, 8, I0, I0]),
                    ctxT[:, :, t0:t0 + I0].unsqueeze(2).to_broadcast([P, 8, I0, I0]), ALU.mult).then_inc(kv_ready, 1)

            def a_z(g, h):
                u = h % 2
                t0 = h * I0
                dve.wait_ge(y_ready, 1 + NH0 * g + h + 1)
                nc.vector.tensor_tensor(
                    zr[:, u], yb[u].rearrange("p (q i j) -> p q i j", q=8, i=I0),
                    ctxT[:, :, t0:t0 + I0].unsqueeze(3).to_broadcast([P, 8, I0, I0]), ALU.mult).then_inc(z_ready, 1)

            def a_add(g, h):
                u = h % 2
                dve.wait_ge(z_ready, 1 + NH0 * g + h + 1)
                if h == 0:
                    dve.wait_ge(o_ready, 1 + 2 * g)
                nc.vector.tensor_tensor(z4[:, :, :, h * I0:(h + 1) * I0], zr[:, u, :, 0:HALF, :],
                                        zr[:, u, :, HALF:, :], ALU.add).then_inc(z4_ready, 1)

            def a_bias(g):
                dve.wait_ge(vtp_ready, g + 1)
                dve.wait_ge(ctxN_loaded, 16 * (g + 1))
                nc.vector.scalar_tensor_tensor(out=vN, in0=vN, scalar=bias_c[:, 0:1], in1=ctxN,
                                               op0=ALU.mult, op1=ALU.mult).then_inc(bvx_ready, 1)

            def a_skip(g):
                dve.wait_ge(w_ready, g + 1)
                Xg = X[:, bass.ds(g * BG, BG), :]
                link(nc.vector.tensor_tensor(vN, WB[:].rearrange("p (b d) -> p b d", b=BG), ctxN, ALU.mult))
                nc.vector.tensor_tensor(Xg, Xg, vN, ALU.add).then_inc(t_done, 1)

            def a_finish(g):
                for k in range(2):
                    dve.wait_ge(o_ready, 1 + 2 * g + 1 + k)
                    if k == 0:
                        dve.wait_ge(t_done, g + 1)
                    Xg = X[:, bass.ds(g * BG + 2 * k, 2), :]
                    nc.vector.tensor_tensor(Xg, Xg, OB[:, k * 512:(k + 1) * 512].rearrange("p (b d) -> p b d", b=2),
                                            ALU.add).then_inc(a_done, 1)

            def a_next(g):
                a_skip(g)
                dve.wait_ge(vT_ready, 2 * g + 2)
                dve.wait_ge(ctxT_loaded, 16 * (g + 1))
                a_kv(g, 0)
                a_kv(g, 1)

            def a_heads(g, more):
                for h in range(NH0):
                    a_z(g, h)
                    if h + 2 < NH0:
                        a_kv(g, h + 2)
                    a_add(g, h)
                    if more and h == 4:
                        stats(g + 1, gate[:, 0:1])
                    if more and h == 11:
                        a_bias(g + 1)
                    if not more and PHASES > 1:
                        if h == 3:
                            stats(0, None, 1)
                        if h == 10:
                            route(0)

            def top2(lg, dst1, dst2):
                def first_max(src, mx, dst):
                    wide = lambda v: v.unsqueeze(2).to_broadcast([P, BG, E])
                    order = ramp[:].unsqueeze(1).to_broadcast([P, BG, E])
                    link(nc.vector.tensor_reduce(mx, src, AX_X, ALU.max))
                    link(nc.vector.tensor_tensor(eq, src, wide(mx), ALU.is_equal))
                    link(nc.vector.tensor_tensor(eq, eq, order, ALU.mult))
                    link(nc.vector.tensor_reduce(rk[:, :, 0], eq, AX_X, ALU.max))
                    link(nc.vector.tensor_tensor(dst, order, wide(rk[:, :, 0]), ALU.is_equal))
                first_max(lg, m1, dst1)
                link(nc.vector.scalar_tensor_tensor(out=l2, in0=dst1, scalar=FAR, in1=lg, op0=ALU.mult, op1=ALU.add))
                first_max(l2, m2, dst2)

            def route(g):
                dve.wait_ge(logits_ready, g + 1)
                link(nc.vector.tensor_copy(lg, TP[:, 0:BG * NR].rearrange("p (b e) -> p b e", b=BG)))
                top2(lg[:, :, 0:E], oh1, oh2)
                step.mark(nc.vector.tensor_tensor(es_[:, :, 0:E], lg[:, :, 0:E],
                                                  m1.unsqueeze(2).to_broadcast([P, BG, E]), ALU.subtract))
                nc.vector.tensor_scalar(es_[:, :, E], lg[:, :, E], -1.0, None, ALU.mult).then_inc(expin_ready, 1)
                link(nc.vector.tensor_tensor(oh1, oh1, oh2, ALU.add))
                dve.wait_ge(exp_ready, g + 1)
                step.mark(nc.vector.tensor_reduce(den[:, 0:BG], es_[:, :, 0:E], AX_X, ALU.add))
                link(nc.vector.tensor_scalar(den[:, BG:], es_[:, :, E], 1.0, None, ALU.add))
                link(nc.vector.reciprocal(rcp, den))
                link(nc.vector.tensor_tensor(oh1, oh1, es_[:, :, 0:E], ALU.mult))
                link(nc.vector.tensor_tensor(oh1, oh1, rcp[:, 0:BG].unsqueeze(2).to_broadcast([P, BG, E]), ALU.mult))
                step.mark(nc.vector.tensor_copy(spread[:, 0].rearrange("p b (e r) -> p b e r", e=E),
                                                oh1.unsqueeze(3).to_broadcast([P, BG, E, RANK])))
                nc.vector.tensor_copy(spread[:, 1], rcp[:, BG:].unsqueeze(2).to_broadcast([P, BG, P])
                                      ).then_inc(spread_ready, 1)
            N_ROUTE = 1 + 11 + 1 + 1 + 1 + 1 + 1 + 1 + 1 + 1

            def b_low_x(g):
                for k in range(DT):
                    dve.wait_ge(xH_ready, 2 * g + k + 1)
                    nc.vector.tensor_tensor(xL[:, k], xT[:, k], xH[:, k].bitcast(F32), ALU.subtract
                                            ).then_inc(xL_ready, 1)

            def b_hidden(g, j):
                pr = TAIL if j == J0 - 1 else P
                dve.wait_ge(scaled_ready, J0 * g + j + 1)
                if j >= 2:
                    dve.wait_ge(hL_ready, J0 * g + j - 1)
                nc.vector.tensor_tensor(b_h[0:pr, j % 2], b_scaled[0:pr, j % 2], U_[j % 2][0:pr], ALU.mult
                                        ).then_inc(h_ready, 1)

            def b_low(g, j):
                pr = TAIL if j == J0 - 1 else P
                dve.wait_ge(hH_ready, J0 * g + j + 1)
                nc.vector.tensor_tensor(hL[0:pr, j % 2], b_h[0:pr, j % 2], hH[0:pr, j % 2].bitcast(F32), ALU.subtract
                                        ).then_inc(hL_ready, 1)

            def b_tiles(g, more):
                for j in range(J0):
                    b_hidden(g, j)
                    if j >= 1:
                        b_low(g, j - 1)
                    if more and j == 2:
                        stats(g + 1, None, 1)
                    if more and j == 9:
                        route(g + 1)
                    if not more and j == 9 and PHASES > 2:
                        stats(0, HD ** -0.5, 2)
                b_low(g, J0 - 1)

            def b_finish(g):
                dve.wait_ge(down_done, 1 + J0 * (g + 1))
                for k in range(2):
                    Xg = X[:, bass.ds(g * BG + 2 * k, 2), :]
                    nc.vector.scalar_tensor_tensor(
                        out=Xg, in0=DN[:, k * 512:(k + 1) * 512].rearrange("p (b d) -> p b d", b=2),
                        scalar=gate[:, 2:3], in1=Xg, op0=ALU.mult, op1=ALU.add).then_inc(b_done, 1)

            def c_shift(g, k):
                n = 8 * g + k
                u = k % 2
                dve.wait_ge(scores_ready, n + 1)
                S = S_[u][:].rearrange("p (h k) -> p h k", h=HH)
                link(nc.vector.tensor_reduce(mx[:, u], S, AX_X, ALU.max))
                link(nc.vector.tensor_scalar(mx[:, u], mx[:, u], MASKED, None, ALU.max))
                if not (isinstance(n, int) and n < 2):
                    dve.wait_ge(p_turned, n - 1)
                nc.vector.scalar_tensor_tensor(out=E_[:, u], in0=S, scalar=MASKED,
                                               in1=mx[:, u].unsqueeze(2).to_broadcast([P, HH, P]),
                                               op0=ALU.max, op1=ALU.subtract).then_inc(shifted, 1)

            def c_finish(g, b):
                t = BG * g + b
                dve.wait_ge(pv_done, 1 + 2 * t + 2)
                O = O_.rearrange("p (h e) -> p h e", h=HEADS)
                link(nc.vector.reciprocal(r16, O[:, :, HD]))
                nc.vector.scalar_tensor_tensor(out=otmp, in0=O[:, :, 0:HD], scalar=gate[:, 1:2],
                                               in1=r16.unsqueeze(2).to_broadcast([P, HEADS, HD]),
                                               op0=ALU.mult, op1=ALU.mult).then_inc(o_read, 1)
                dve.wait_ge(o_read, 1 + t + 1)
                Xt = X[:, bass.ds(t, 1), :]
                nc.vector.tensor_tensor(Xt, Xt, otmp.rearrange("p h e -> p (h e)").unsqueeze(1), ALU.add
                                        ).then_inc(c_done, 1)

            def c_steps(g, more):
                if more:
                    stats(g + 1, HD ** -0.5, 2)
                for k in range(8):
                    if k < 6 or more:
                        c_shift(g + (k + 2) // 8, (k + 2) % 8)
                    if k % 2:
                        c_finish(g, k // 2)

            def d_prep(g):
                stats(g, None, 3)
                for k in range(DT):
                    dve.wait_ge(xH_ready, 2 * (G + g) + k + 1)
                    nc.vector.tensor_tensor(xL[:, k], dxT[:, k], xH[:, k].bitcast(F32), ALU.subtract
                                            ).then_inc(xL_ready, 1)
                dve.wait_ge(d_logits, g + 1)
                link(nc.vector.tensor_copy(lg[:, :, 0:E], bank[1][:, 0:BG * E].rearrange("p (b e) -> p b e", b=BG)))
                top2(lg[:, :, 0:E], oh1, oh2)
                nc.vector.tensor_scalar(dspread[:, 1, 0].rearrange("p b (e r) -> p b e r", e=E),
                                        oh1.unsqueeze(3).to_broadcast([P, BG, E, RANK]), LORA_ALPHA, None, ALU.mult
                                        ).then_inc(tops_ready, 1)
                step.mark(nc.vector.tensor_scalar(dspread[:, 1, 1].rearrange("p b (e r) -> p b e r", e=E),
                                                  oh2.unsqueeze(3).to_broadcast([P, BG, E, RANK]), LORA_ALPHA, None,
                                                  ALU.mult))
                dve.wait_ge(tops_turned, g + 1)
                link(nc.vector.tensor_reduce(mtop, bank[1][0:2 * BG, 64:64 + P], AX_X, ALU.max))
                nc.vector.tensor_scalar(mneg, mtop, -1.0, None, ALU.mult).then_inc(topmax_ready, 1)
                dve.wait_ge(cexp_ready, 2 * g + 1)
                nc.vector.reciprocal(mrcp, msum).then_inc(c_ready, 1)
                dve.wait_ge(c_back, g + 1)
                nc.vector.tensor_copy(dspread[:, 0].rearrange("p r b t -> p (r b) t"),
                                      bank[1][:, 256:256 + 2 * BG].unsqueeze(2).to_broadcast([P, 2 * BG, P])
                                      ).then_inc(dspread_ready, 1)
                dve.wait_ge(dM_ready, g + 1)
                dve.wait_ge(dMD_ready, g + 1)
                dve.wait_ge(zL_ready, 1 + 4 * g)
                for r in range(4):
                    dve.wait_ge(z_psum, 2 * g + r // 2 + 1)
                    nc.vector.tensor_tensor(dz[:, r], bank[2][:, (r // 2) * 512:(r // 2 + 1) * 512],
                                            dM[:, 0 if r % 2 == 0 else 2], ALU.mult).then_inc(zm_ready, 1)

            def d_hidden(g, i):
                j, k = EV[i]
                pr = TAIL if j == SJ - 1 else P
                dst = (dc1, dc2)[k]
                dve.wait_ge(dscaled_ready, 1 + NE * g + i + 1)
                if j >= 2:
                    if k == 0:
                        dve.wait_ge(cL_ready, SJ * g + j - 1)
                        dve.wait_ge(sum_ready, SJ * g + j - 1)
                    else:
                        dve.wait_ge(sL_ready, SJ * g + j - 1)
                nc.vector.tensor_tensor(dst[0:pr, j % 2], dscaled[0:pr, i % 2], G_[j % 2][0:pr], ALU.mult
                                        ).then_inc(ch_ready, 1)
                if k == 1:
                    dve.wait_ge(ch_ready, NE * g + i + 1)
                    nc.vector.tensor_tensor(dc2[0:pr, j % 2], dc2[0:pr, j % 2], dc1[0:pr, j % 2], ALU.add
                                            ).then_inc(sum_ready, 1)

            def d_low(g, i):
                j, k = EV[i]
                pr = TAIL if j == SJ - 1 else P
                if k == 0:
                    dve.wait_ge(cH_ready, SJ * g + j + 1)
                    nc.vector.tensor_tensor(dcL[0:pr, j % 2], dc1[0:pr, j % 2], dcH[0:pr, j % 2].bitcast(F32),
                                            ALU.subtract).then_inc(cL_ready, 1)
                else:
                    dve.wait_ge(sH_ready, SJ * g + j + 1)
                    nc.vector.tensor_tensor(dsL[0:pr, j % 2], dc2[0:pr, j % 2], dsH[0:pr, j % 2].bitcast(F32),
                                            ALU.subtract).then_inc(sL_ready, 1)

            def d_mix(g):
                dve.wait_ge(ddown_done, SJ * (g + 1))
                nc.vector.tensor_tensor(dw[:, 0], bank[2][:, 0:512], dM[:, 1], ALU.mult).then_inc(w_mixed, 1)
                nc.vector.tensor_tensor(dw[:, 1], bank[2][:, 512:1024], dM[:, 2], ALU.mult).then_inc(w_mixed, 1)
                dve.wait_ge(w_mixed, 1 + 2 * g + 2)
                nc.vector.tensor_tensor(dw[:, 2], dw[:, 0], dw[:, 1], ALU.subtract).then_inc(w_sum, 1)
                dve.wait_ge(wsH_ready, g + 1)
                nc.vector.tensor_tensor(dwL, dw[:, 2], dwH.bitcast(F32), ALU.subtract).then_inc(wsL_ready, 1)
                dve.wait_ge(dn_ready, 1 + g + 1)
                for k in range(2):
                    Xg = X[:, bass.ds(g * BG + 2 * k, 2), :]
                    nc.vector.scalar_tensor_tensor(
                        out=Xg, in0=DN[:, k * 512:(k + 1) * 512].rearrange("p (b d) -> p b d", b=2),
                        scalar=gate[:, 3:4], in1=Xg, op0=ALU.mult, op1=ALU.add).then_inc(d_done, 1)

            dve.wait_ge(x0_loaded, 16)
            dve.wait_ge(gate_ready, 1)
            stats(0, gate[:, 0:1])
            dve.wait_ge(xrest_loaded, 16)
            a_bias(0)
            a_next(0)
            per = 2 * BG + 3 + 1
            start = step.value()
            with dve.Fori(0, G - 1) as g:
                step.enter(g, per, start)
                a_heads(g, True)
                a_next(g + 1)
                a_finish(g)
            step.leave(per, G - 1, start)
            a_heads(G - 1, False)
            a_finish(G - 1)
            if PHASES > 1:
                b_low_x(0)
                per = 2 * BG + 2 + N_ROUTE
                start = step.value()
                with dve.Fori(0, G - 1) as g:
                    step.enter(g, per, start)
                    b_tiles(g, True)
                    b_low_x(g + 1)
                    b_finish(g)
                step.leave(per, G - 1, start)
                b_tiles(G - 1, False)
                b_finish(G - 1)
            if PHASES > 2:
                c_shift(0, 0)
                c_shift(0, 1)
                per = 2 * BG + 3 + 2 * 8 + BG
                start = step.value()
                with dve.Fori(0, G - 1) as g:
                    step.enter(g, per, start)
                    c_steps(g, True)
                step.leave(per, G - 1, start)
                c_steps(G - 1, False)
            if PHASES > 3:
                per = 2 * BG + 2 + 1 + 11 + 1 + 1
                start = step.value()
                with dve.Fori(0, G) as g:
                    step.enter(g, per, start)
                    d_prep(g)
                    for i in range(NE):
                        d_hidden(g, i)
                        if i >= 1:
                            d_low(g, i - 1)
                    d_low(g, NE - 1)
                    d_mix(g)
                step.leave(per, G, start)

        @block.tensor
        def _(pe):
            pe.wait_ge(consts_ready, 8)

            def a_turn(g):
                pe.wait_ge(vN_ready, BG * (g + 1))
                pe.wait_ge(vT_ready, 2 * g)
                for k in range(DT):
                    for b in range(BG):
                        mm = nc.tensor.transpose(TV[:, (k * BG + b) * P:(k * BG + b + 1) * P],
                                                 vN[:, b, k * P:(k + 1) * P], ident[:])
                mm.then_inc(vtp_ready, 1)

            def a_block_sums(g):
                pe.wait_ge(bvx_ready, g + 1)
                pe.wait_ge(t_done, g)
                ob = ones_blk[:].rearrange("p a b -> p (a b)")
                for k in range(2):
                    mm = nc.tensor.matmul(WB[:, k * 512:(k + 1) * 512], ob, vN[:, 2 * k:2 * k + 2, :],
                                          start=True, stop=True)
                mm.then_inc(w_ready, 1)

            def a_conv(g, h):
                u = h % 2
                pe.wait_ge(kv_ready, NH0 * g + h + 1)
                if h >= 2:
                    pe.wait_ge(z_ready, 1 + NH0 * g + h - 1)
                else:
                    pe.wait_ge(z_ready, 1 + NH0 * g)
                y = yb[u]
                n = BG * I0 * I0
                diag, off = toep[:, h, 0:P], toep[:, h, P:2 * P]
                kv0 = kv[:, u, 0:BG].rearrange("p q i j -> p (q i j)")
                kv1 = kv[:, u, BG:2 * BG].rearrange("p q i j -> p (q i j)")
                nc.tensor.matmul(y[:, 0:n], diag, kv0, start=True, stop=False, skip_group_check=True)
                nc.tensor.matmul(y[:, n:2 * n], diag, kv1, start=False, stop=False, skip_group_check=True)
                nc.tensor.matmul(y[:, n:2 * n], off, kv0, start=False, stop=True, skip_group_check=True
                                 ).then_inc(y_ready, 1)

            def a_sum(g):
                pe.wait_ge(z4_ready, NH0 * (g + 1))
                pe.wait_ge(a_done, 1 + 2 * g)
                for b in range(BG):
                    for k in range(DT):
                        for i in range(HALF):
                            mm = nc.tensor.matmul(OB[:, b * D + k * P:b * D + (k + 1) * P], z4[:, k * BG + b, i, :],
                                                  ident[:], start=(i == 0), stop=(i == HALF - 1),
                                                  skip_group_check=True)
                    if b % 2:
                        mm.then_inc(o_ready, 1)

            a_turn(0)
            a_block_sums(0)
            pe.wait_ge(toep_loaded, 16)
            with pe.Fori(0, G - 1) as g:
                for h in range(NH0):
                    a_conv(g, h)
                    if h == 8:
                        a_turn(g + 1)
                a_block_sums(g + 1)
                a_sum(g)
            def b_turn(g):
                pe.wait_ge(vN_ready, BG * (G + g + 1))
                if isinstance(g, int) and g == 0:
                    pe.wait_ge(t_done, G)
                else:
                    pe.wait_ge(comb_ready, g)
                for k in range(DT):
                    for b in range(BG):
                        mm = nc.tensor.transpose(TP[:, (k * BG + b) * P:(k * BG + b + 1) * P],
                                                 xn[:, b, k * P:(k + 1) * P], ident[:])
                mm.then_inc(xturned, 1)

            def b_logits(g):
                pe.wait_ge(xT_ready, g + 1)
                for b in range(BG):
                    for k in range(DT):
                        mm = nc.tensor.matmul(TP[:, b * NR:(b + 1) * NR], xT[:, k, b * P:(b + 1) * P], wr_sb[:, k],
                                              start=(k == 0), stop=(k == DT - 1), skip_group_check=True)
                mm.then_inc(logits_ready, 1)

            def b_spread(g):
                pe.wait_ge(spread_ready, g + 1)
                for r in range(2):
                    for b in range(BG):
                        mm = nc.tensor.transpose(TP[:, (r * BG + b) * P:(r * BG + b + 1) * P], spread[:, r, b],
                                                 ident[:])
                mm.then_inc(spread_turned, 1)

            def b_gate_up(g, j):
                pr = TAIL if j == J0 - 1 else P
                if j == 0:
                    pe.wait_ge(xL_ready, 2 * (g + 1))
                if j >= 2:
                    pe.wait_ge(h_ready, 1 + J0 * g + j - 1)
                else:
                    pe.wait_ge(h_ready, 1 + J0 * g)
                for at, dst in ((0, G_[j % 2]), (2 * P, U_[j % 2])):
                    n = 0
                    for wX, mX in ((w0H, xH), (w0L, xH), (w0H, xL)):
                        for k in range(DT):
                            mm = nc.tensor.matmul(dst[0:pr], wX[:, j, at + k * P:at + k * P + pr], mX[:, k],
                                                  start=(n == 0), stop=(n == 5))
                            n += 1
                mm.then_inc(gu_ready, 1)

            def b_down(g, j):
                pr = TAIL if j == J0 - 1 else P
                if j == 0:
                    pe.wait_ge(b_done, 1 + 2 * g)
                pe.wait_ge(hL_ready, J0 * g + j + 1)
                for b in range(BG):
                    n = 0
                    for hX, wX in ((hH, w0H), (hH, w0L), (hL, w0H)):
                        mm = nc.tensor.matmul(DN[:, b * D:(b + 1) * D], hX[0:pr, j % 2, b * P:(b + 1) * P],
                                              wX[0:pr, j, 4 * P:], start=(j == 0 and n == 0 and b % 2 == 0),
                                              stop=(j == J0 - 1 and n == 2), skip_group_check=True)
                        n += 1
                mm.then_inc(down_done, 1)

            def b_tiles(g, more):
                for j in range(J0):
                    b_gate_up(g, j)
                    if j >= 2:
                        b_down(g, j - 2)
                    if more and j == 4:
                        b_turn(g + 1)
                    if more and j == 7:
                        b_logits(g + 1)
                    if more and j == 12:
                        b_spread(g + 1)
                    if not more and j == 12 and PHASES > 2:
                        pe.wait_ge(vN_ready, BG * (2 * G + 1))
                        for b in range(BG):
                            for k in range(DT):
                                mm = nc.tensor.transpose(bank[2][:, b * D + k * P:b * D + (k + 1) * P],
                                                         qn[:, b, k * P:(k + 1) * P], ident[:])
                            mm.then_inc(qT_turned, 1)
                b_down(g, J0 - 2)
                b_down(g, J0 - 1)

            def c_scores(g, k):
                n = 8 * g + k
                r, b, kk = k // 4, k // 2, k % 2
                pe.wait_ge(qT_ready, BG * g + b + 1)
                pe.wait_ge(kbd_loaded[r], 16 * 2 * HH * (g + 1))
                if not (isinstance(n, int) and n < 2):
                    pe.wait_ge(shifted, n - 1)
                for c in range(2):
                    S = S_[k % 2][:, c * 512:(c + 1) * 512]
                    nc.tensor.matmul(S, qT[:, b, kk], kbd[:, r, b % 2, kk, 4 * c:4 * c + 4, :], start=True, stop=False)
                    mm = nc.tensor.matmul(S, identb[:], neg[:], start=False, stop=True)
                mm.then_inc(scores_ready, 1)

            def c_turn_p(g, k):
                n = 8 * g + k
                pe.wait_ge(exp_done, n + 1)
                pe.wait_ge(pT_ready, n)
                for h in range(HH):
                    mm = nc.tensor.transpose(PTP[:, h * P:(h + 1) * P], E_[:, k % 2, h], ident[:])
                mm.then_inc(p_turned, 1)

            def c_values(g, k):
                n = 8 * g + k
                r, b, kk = k // 4, k // 2, k % 2
                pe.wait_ge(pT_ready, n + 1)
                pe.wait_ge(va_loaded[r], 16 * (g + 1))
                if kk == 0:
                    pe.wait_ge(o_read, 1 + BG * g + b)
                for h in range(HH):
                    head = kk * HH + h
                    mm = nc.tensor.matmul(O_[:, head * VA:(head + 1) * VA], PT_[:, k % 2, h], va[:, r, b % 2, head],
                                          start=True, stop=True, skip_group_check=True)
                mm.then_inc(pv_done, 1)

            def c_turn_q(g, b):
                pe.wait_ge(vN_ready, BG * (2 * G + g) + b + 1)
                pe.wait_ge(qT_ready, BG * g + b)
                for k in range(DT):
                    mm = nc.tensor.transpose(TQ[:, k * P:(k + 1) * P], qn[:, b, k * P:(k + 1) * P], ident[:])
                mm.then_inc(qT_turned, 1)

            def c_steps(g, more):
                for k in range(8):
                    if k < 6 or more:
                        c_scores(g + (k + 2) // 8, (k + 2) % 8)
                    if k < 7 or more:
                        c_turn_p(g + (k + 1) // 8, (k + 1) % 8)
                    c_values(g, k)
                    if more and k in TURN_AT:
                        c_turn_q(g + 1, TURN_AT.index(k))

            def three(dst, pairs, start=True, stop=True, skip=False):
                prods = [(a[0], m[0]) for a, m in pairs] + [(a[1], m[0]) for a, m in pairs] + [
                    (a[0], m[1]) for a, m in pairs]
                for n, (a, m) in enumerate(prods):
                    mm = nc.tensor.matmul(dst, a, m, start=start and n == 0, stop=stop and n == len(prods) - 1,
                                          skip_group_check=skip)
                return mm

            def d_prep(g):
                pe.wait_ge(vN_ready, BG * (3 * G + g + 1))
                for k in range(DT):
                    for b in range(BG):
                        mm = nc.tensor.transpose(bank[0][:, (k * BG + b) * P:(k * BG + b + 1) * P],
                                                 dxn[:, b, k * P:(k + 1) * P], ident[:])
                mm.then_inc(xturned, 1)
                pe.wait_ge(xT_ready, G + g + 1)
                for b in range(BG):
                    for k in range(DT):
                        mm = nc.tensor.matmul(bank[1][:, b * E:(b + 1) * E], dxT[:, k, b * P:(b + 1) * P], gw_sb[:, k],
                                              start=(k == 0), stop=(k == DT - 1), skip_group_check=True)
                mm.then_inc(d_logits, 1)
                pe.wait_ge(tops_ready, g + 1)
                tops = small[:, 236:236 + 2 * BG]
                nc.tensor.transpose(bank[1][0:2 * BG, 64:64 + P], tops, ident[:]).then_inc(tops_turned, 1)
                pe.wait_ge(xL_ready, 2 * (G + g + 1))
                pe.wait_ge(w_mixed, 1 + 2 * g)
                for r in range(2):
                    a = [((w1H[:, r * D + k * P:r * D + (k + 1) * P], w1L[:, r * D + k * P:r * D + (k + 1) * P]),
                          (xH[:, k], xL[:, k])) for k in range(DT)]
                    three(bank[2][:, r * 512:(r + 1) * 512], a).then_inc(z_psum, 1)
                pe.wait_ge(cexp_ready, 2 * g + 2)
                nc.tensor.matmul(bank[1][:, 256:256 + 2 * BG], cT, ident[0:2 * BG, 0:2 * BG], start=True, stop=True,
                                 skip_group_check=True).then_inc(c_back, 1)
                pe.wait_ge(dspread_ready, g + 1)
                for m in range(2):
                    for r in range(2):
                        for b in range(BG):
                            mm = nc.tensor.transpose(bank[m][:, (r * BG + b) * P:(r * BG + b + 1) * P],
                                                     dspread[:, m, r, b], ident[:])
                    mm.then_inc(dturned, 1)

            def d_base(g, j):
                pr = TAIL if j == SJ - 1 else P
                if j >= 2:
                    pe.wait_ge(ch_ready, NE * g + at_ev[(j - 2, 1)] + 1)
                elif j == 0:
                    pe.wait_ge(dcb_ready, g + 1)
                    pe.wait_ge(zL_ready, 1 + 4 * g + 4)
                    pe.wait_ge(dM_ready, g + 1)
                for at, dst, zr_ in ((0, U_[j % 2], 0), (2 * P, G_[j % 2], 2)):
                    a = [(tuple(w[:, 0:pr] for w in w1_tile(j, at + k * P, P)), (xH[:, k], xL[:, k]))
                         for k in range(DT)]
                    lora = tuple(w[:, 0:pr] for w in w1_tile(j, 4 * P + at // 2, P))
                    mm = three(dst[0:pr], a + [(lora, (dzH[:, zr_], dzL[:, zr_]))], skip=True)
                mm.then_inc(ev_ready, 1)

            def d_delta(g, j):
                pr = TAIL if j == SJ - 1 else P
                pe.wait_ge(ch_ready, NE * g + at_ev[(j, 0)] + 1)
                for at, dst, zr_ in ((0, U_[j % 2], 1), (P, G_[j % 2], 3)):
                    lora = tuple(w[:, 0:pr] for w in w1_tile(j, 4 * P + at, P))
                    mm = three(dst[0:pr], [(lora, (dzH[:, zr_], dzL[:, zr_]))], start=False, skip=True)
                mm.then_inc(ev_ready, 1)

            def d_down(g, j):
                pr = TAIL if j == SJ - 1 else P
                pe.wait_ge(cL_ready, SJ * g + j + 1)
                pe.wait_ge(sL_ready, SJ * g + j + 1)
                if j == 0:
                    pe.wait_ge(d_done, 1 + 2 * g)
                wd = tuple(w[0:pr] for w in w1_tile(j, 6 * P, D))
                wa = tuple(w[0:pr] for w in w1_tile(j, 6 * P + D, P))
                ends = dict(start=(j == 0), stop=(j == SJ - 1), skip=True)
                three(bank[2][:, 0:512], [(wa, (dsH[0:pr, j % 2], dsL[0:pr, j % 2]))], **ends)
                three(bank[2][:, 512:1024], [(wa, (dcH[0:pr, j % 2], dcL[0:pr, j % 2]))], **ends)
                for b in range(BG):
                    tok = slice(b * P, (b + 1) * P)
                    mm = three(DN[:, b * D:(b + 1) * D], [((dsH[0:pr, j % 2, tok], dsL[0:pr, j % 2, tok]), wd)],
                               start=(j == 0 and b % 2 == 0), stop=False, skip=True)
                mm.then_inc(ddown_done, 1)

            def d_adapt(g):
                pe.wait_ge(wsL_ready, g + 1)
                wb = (w1H[:, 2 * D:3 * D], w1L[:, 2 * D:3 * D])
                for b in range(BG):
                    tok = slice(b * P, (b + 1) * P)
                    mm = three(DN[:, b * D:(b + 1) * D], [((dwH[:, tok], dwL[:, tok]), wb)], start=False, skip=True)
                mm.then_inc(dn_ready, 1)

            for h in range(NH0):
                a_conv(G - 1, h)
                if PHASES > 1:
                    if h == 5:
                        b_turn(0)
                    if h == 8:
                        b_logits(0)
                    if h == 14:
                        b_spread(0)
            a_sum(G - 1)
            if PHASES > 1:
                pe.wait_ge(wL_ready, J0)
                with pe.Fori(0, G - 1) as g:
                    b_tiles(g, True)
                b_tiles(G - 1, False)
            if PHASES > 2:
                pe.wait_ge(b_done, 1 + 2 * G)
                c_scores(0, 0)
                c_scores(0, 1)
                c_turn_p(0, 0)
                with pe.Fori(0, G - 1) as g:
                    c_steps(g, True)
                c_steps(G - 1, False)
            if PHASES > 3:
                pe.wait_ge(c_done, B)
                pe.wait_ge(w1L_ready, W1K)
                with pe.Fori(0, G) as g:
                    d_prep(g)
                    for j in range(SJ + 2):
                        if j < SJ:
                            d_base(g, j)
                        if 1 <= j <= SJ:
                            d_delta(g, j - 1)
                        if j >= 2:
                            d_down(g, j - 2)
                    d_adapt(g)


def kernel(**inputs):
    import numpy as np
    import concourse.bacc as bacc
    from concourse.bass_utils import run_bass_kernel_spmd

    a = {k: np.asarray(v) for k, v in inputs.items()}

    def halves(w):
        return w.reshape(DT, P, -1).transpose(1, 0, 2)

    def padded(w, n, axis):
        pad = [(0, 0)] * w.ndim
        pad[axis] = (0, n - w.shape[axis])
        return np.pad(w, pad)

    def expert_cols(w):
        w = w.transpose(1, 0, 2).reshape(D, P, EJ).transpose(0, 2, 1)
        return halves(w.reshape(D, -1)).reshape(P, DT, EJ, P)

    def plain_cols(w):
        return halves(padded(w, SJ * P, 1)).reshape(P, DT, SJ, P)

    def rows(w):
        return padded(w, SJ * P, 0).reshape(SJ, P, -1).transpose(1, 0, 2)

    gate0 = np.concatenate([expert_cols(a["L0_ffn_Wg"]), plain_cols(a["L0_ffn_Sg"])], 2)
    up0 = np.concatenate([expert_cols(a["L0_ffn_Wu"]), plain_cols(a["L0_ffn_Su"])], 2)
    down0 = np.concatenate([a["L0_ffn_Wd"].reshape(P, EJ, D), rows(a["L0_ffn_Sd"])], 1)
    tiles = lambda w: w.transpose(2, 0, 1, 3).reshape(w.shape[2], P, -1)
    w0 = np.concatenate([tiles(gate0), tiles(up0), down0.transpose(1, 0, 2)], 2)
    wr = halves(padded(np.concatenate([a["L0_ffn_Wr"], a["L0_ffn_Wsg"]], 1), NR, 1)).reshape(P, -1)
    er_rows = lambda w: w.reshape(P, -1)
    up1, gate1 = plain_cols(a["L1_ffn_w_up"].T), plain_cols(a["L1_ffn_w_gate"].T)
    b_up = padded(er_rows(a["L1_ffn_up_B"].transpose(0, 2, 1)), SJ * P, 1).reshape(P, SJ, P).transpose(1, 0, 2)
    b_gate = padded(er_rows(a["L1_ffn_gate_B"].transpose(0, 2, 1)), SJ * P, 1).reshape(P, SJ, P).transpose(1, 0, 2)
    down1 = rows(a["L1_ffn_w_down"].T).transpose(1, 0, 2)
    a_down = rows(er_rows(a["L1_ffn_down_A"]).T).transpose(1, 0, 2)
    w1_tiles = np.concatenate([tiles(up1), tiles(gate1), b_up, b_gate, down1, a_down], 2)
    ab = np.concatenate([halves(er_rows(a["L1_ffn_up_A"]).T).reshape(P, -1),
                         halves(er_rows(a["L1_ffn_gate_A"]).T).reshape(P, -1),
                         er_rows(a["L1_ffn_down_B"].transpose(0, 2, 1))], 1)
    w1 = np.concatenate([ab, w1_tiles.transpose(1, 0, 2).reshape(P, -1)], 1).reshape(P, W1K, W1C).transpose(1, 0, 2)
    ctx_one = np.concatenate([a["ctx_2048"].reshape(B, P, HEADS, HD), np.ones((B, P, HEADS, 1), np.float32)], 3)
    gw = halves(a["L1_ffn_gate_w"].T).reshape(P, -1)
    filt = np.lib.stride_tricks.sliding_window_view(np.pad(a["L0_xattn_k"], ((0, 0), (P, 0))), 2 * P, 1)
    filt = filt[:, P:0:-1].transpose(1, 0, 2)
    ctx_t = a["ctx_2048"].reshape(G, BG, P, DT, P).transpose(0, 4, 3, 1, 2).reshape(G, P, DT * BG, P)
    arrays = {
        "x": a["x"], "ctx_nat": a["ctx_2048"], "ctx_t": ctx_t, "ctx_one": ctx_one, "filt": filt, "bias": a["fside_S2_0"],
        "gates": np.concatenate([a["g_xattn"], a["g_ffn"]]), "w0": w0, "wr": wr, "w1": w1, "gw": gw,
        "ramp": np.arange(E, 0, -1).astype(np.float32),
    }
    arrays = {k: np.ascontiguousarray(v) for k, v in arrays.items()}
    nc = bacc.Bacc("TRN2", target_bir_lowering=False, num_devices=1)
    args = [nc.dram_tensor("in_" + k, v.shape, mybir.dt.from_np(v.dtype), kind="ExternalInput").ap() for k, v in arrays.items()]
    out = nc.dram_tensor("out", (B, P, D), F32, kind="ExternalOutput").ap()
    flamingo_kernel(nc, *args, out)
    r = run_bass_kernel_spmd(nc, [{"in_" + k: v for k, v in arrays.items()}], core_ids=[0])
    return r.results[0]["out"]
```

```python
from contextlib import ExitStack

import concourse.bass as bass
from concourse import mybir

F32 = mybir.dt.float32
F32R = mybir.dt.float32r
BF16 = mybir.dt.bfloat16
I32 = mybir.dt.int32
ALU = mybir.AluOpType
ACT = mybir.ActivationFunctionType
AX_X = mybir.AxisListType.X

P = 128
B = 16
D = 256
DT = D // P
G = 4
BG = B // G
NT = BG * P
NH0, I0 = 16, 8
HALF = I0 // 2
E = 8
RANK = 16
F0, FS = 176, 704
EJ = E * F0 // P
SJ = -(-FS // P)
TAIL = FS - (SJ - 1) * P
J0 = EJ + SJ
W0T = 4 * P + D
W1T = 4 * P + 2 * P + D + P
W1X = 4 * P + D
W1N = W1X + SJ * W1T
W1K = 8
W1C = W1N // W1K
NR = E + 2
HEADS, HD = 16, 16
HH = P // HD
VA = HD + 1
EPS = 1e-5
MASKED = -10000.0
FAR = -1e30
LORA_ALPHA = 2.0
RSQRT_GUESS = 0x5F3759DF
TOEP_H = 4
TURN_AT = (2, 4, 6, 7)
PHASES = 4


class Count:

    def __init__(self, sem):
        self.sem, self.base, self.n = sem, 0, 0

    def mark(self, ins):
        ins.then_inc(self.sem, 1)
        self.n += 1

    def value(self):
        return self.base + self.n

    def enter(self, g, per, start):
        self.base, self.n = g * per + start, 0

    def leave(self, per, rounds, start):
        assert self.n == per, (self.n, per)
        self.base, self.n = start + per * rounds, 0


def flamingo_kernel(nc, x, ctx_nat, ctx_half, ctx_t, ctx_one, filt, bias, gates, w0, wr, w1, gw, ramp_in, out):
    es = ExitStack()
    with es:
        sb = lambda name, shape, dt=F32: es.enter_context(nc.sbuf_tensor(name, shape, dt))
        sem = lambda name: es.enter_context(nc.semaphore(name))
        bank = [es.enter_context(nc.psum_tensor(f"bank{i}", [P, 1024], F32)) for i in range(4)]

        X = sb("X", [P, B, D])
        ident = sb("ident", [P, P])
        identb = sb("identb", [P, P], BF16)
        ones_blk = sb("ones_blk", [P, NH0, I0])
        neg = sb("neg", [P, 4, P], BF16)
        bias_c = sb("bias_c", [P, 1])
        gate_in = sb("gate_in", [P, 4])
        gate = sb("gate", [P, 4])
        ramp = sb("ramp", [P, E])
        wr_sb = sb("wr_sb", [P, DT, NR])
        gw_sb = sb("gw_sb", [P, DT, E])
        st = sb("st", [P, BG, 6])
        mv = sb("mv", [P, BG, 2])
        ve = sb("ve", [P, BG])
        scrap = sb("scrap", [P, 1])
        sd = sb("sd", [P, BG])
        rs = sb("rs", [P, BG])
        nb = sb("nb", [P, BG])
        small = sb("small", [P, 384])
        A1 = sb("A1", [P, 17792])
        R1 = sb("R1", [P, 2 * J0 * W0T + 4 * NT + 4 * NT], F32R)

        def carve(t, sizes):
            views, at = [], 0
            for n in sizes:
                views.append(t[:, at:at + n])
                at += n
            return views

        (toep, ctxN, ctxT, vN, vT, kv_, zr_, z4, stg_) = carve(
            A1, [NH0 * 2 * P, BG * D, BG * D, BG * D, BG * D, 1024, 1024, 8 * HALF * P, 2 * W0T])
        toep = toep.rearrange("p (h c) -> p h c", h=NH0)
        ctxN = ctxN.rearrange("p (b d) -> p b d", b=BG)
        vN = vN.rearrange("p (b d) -> p b d", b=BG)
        ctxT = ctxT.rearrange("p (s q t) -> p s q t", s=2, q=8)
        vT = vT.rearrange("p (q t) -> p q t", t=P)
        kv = kv_.rearrange("p (u q i j) -> p u q i j", u=2, q=8, i=I0)
        zr = zr_.rearrange("p (u q i j) -> p u q i j", u=2, q=8, i=I0)
        z4 = z4.rearrange("p (q i t) -> p q i t", q=8, i=HALF)
        stg = stg_.rearrange("p (u n) -> p u n", u=2)
        yb = [bank[0][:, 0:512], bank[0][:, 512:1024]]
        TV, WB, OB = bank[1], bank[2], bank[3]

        nW0 = J0 * W0T
        w0H = R1[:, 0:nW0].rearrange("p (j n) -> p j n", j=J0)
        w0L = R1[:, nW0:2 * nW0].rearrange("p (j n) -> p j n", j=J0)
        r_at = 2 * nW0
        xH = R1[:, r_at:r_at + DT * NT].rearrange("p (k t) -> p k t", k=DT)
        xL = R1[:, r_at + 2 * NT:r_at + 4 * NT].rearrange("p (k t) -> p k t", k=DT)
        hH = R1[:, r_at + 4 * NT:r_at + 6 * NT].rearrange("p (u t) -> p u t", u=2)
        hL = R1[:, r_at + 6 * NT:r_at + 8 * NT].rearrange("p (u t) -> p u t", u=2)

        xn, xT = (A1[:, at:at + BG * D] for at in (NH0 * 2 * P, NH0 * 2 * P + 2 * BG * D))
        xn = xn.rearrange("p (b d) -> p b d", b=BG)
        spread = A1[:, NH0 * 2 * P:NH0 * 2 * P + 2 * NT].rearrange("p (r b t) -> p r b t", r=2, b=BG)
        xT = xT.rearrange("p (k t) -> p k t", k=DT)
        b_silu, b_scaled = (A1[:, i * 2 * NT:(i + 1) * 2 * NT].rearrange("p (u t) -> p u t", u=2) for i in range(2))
        b_h, b_comb = (A1[:, i * 2 * NT:(i + 1) * 2 * NT].rearrange("p (u t) -> p u t", u=2) for i in (2, 3))
        G_, U_ = [bank[0][:, 0:512], bank[1][:, 0:512]], [bank[0][:, 512:1024], bank[1][:, 512:1024]]
        TP, DN = bank[2], bank[3]
        (lg, es_, eq, rk, oh1, oh2, l2) = carve(small, [BG * NR, BG * (E + 1), BG * E, BG * E, BG * E, BG * E, BG * E])
        m1, m2, den, rcp = carve(small[:, 40 + 36 + 160:], [BG, BG, 2 * BG, 2 * BG])
        lg = lg.rearrange("p (b e) -> p b e", b=BG)
        es_ = es_.rearrange("p (b e) -> p b e", b=BG)
        eq, rk, oh1, oh2, l2 = (v.rearrange("p (b e) -> p b e", b=BG) for v in (eq, rk, oh1, oh2, l2))

        E_, PT_ = (A1[:, i * 2048:(i + 1) * 2048].rearrange("p (u h k) -> p u h k", u=2, h=HH) for i in range(2))
        qT = A1[:, 4096:5120].rearrange("p (b k t) -> p b k t", b=BG, k=DT)
        qn = A1[:, 5120:6144].rearrange("p (b d) -> p b d", b=BG)
        kbd_ = A1[:, 7168:15360]
        kbd = kbd_.rearrange("p (r b k h t) -> p r b k h t", r=2, b=2, k=DT, h=HH)
        va = A1[:, 15360:15360 + BG * HEADS * VA].rearrange("p (r b h e) -> p r b h e", r=2, b=2, h=HEADS)
        stg1 = [A1[:, 6144:6144 + W1C], A1[:, 16448:16448 + W1C]]
        otmp = A1[:, 16448 + W1C:16448 + W1C + D].rearrange("p (h e) -> p h e", h=HEADS)
        (mx_, r16) = carve(small, [2 * HH, HEADS])
        mx = mx_.rearrange("p (u h) -> p u h", u=2)
        S_, PTP, O_, TQ = bank[0:2], bank[2], bank[3][:, 0:HEADS * VA], bank[3][:, 512:512 + D]
        w1H, w1L = R1[:, 0:W1N], R1[:, W1N:2 * W1N]

        (dsilu_, dxT_, dcb_, dM2_, dscaled_, dc1_, dc2_, dw_) = carve(
            A1, [2 * NT, G * DT * NT, G * 2 * NT, G * NT, 2 * NT, 2 * NT, 2 * NT, 3 * NT])
        dxT = dxT_.rearrange("p (g k t) -> p g k t", g=G, k=DT)
        dcb = dcb_.rearrange("p (g r t) -> p g r t", g=G, r=2)
        dM1 = R1[:, r_at + 4 * NT:r_at + 8 * NT].rearrange("p (g t) -> p g t", g=G)
        dM2 = dM2_.rearrange("p (g t) -> p g t", g=G)
        dMD = R1[:, 2 * W1N + 18 * NT:2 * W1N + 19 * NT]
        d_tmp = A1[:, 22 * NT:26 * NT]
        dxn = d_tmp.rearrange("p (u b d) -> p u b d", u=2, b=BG)
        dhot = d_tmp.bitcast(BF16).rearrange("p (r b t) -> p r b t", r=2, b=B)
        dsilu, dscaled, dc1, dc2 = (v.rearrange("p (u t) -> p u t", u=2) for v in (dsilu_, dscaled_, dc1_, dc2_))
        (dst_, dmv_, dvar, dtmp, drs, dnb, dlg_, deq_, dl2_, do1_, do2_, drk, dtop, dctok, cT_) = carve(
            A1[:, 31 * NT:], [B * 6, B * 2, B, B, B, B, B * E, B * E, B * E, B * E, B * E, B, 2 * B, 2 * B, P])
        dstat = dst_.rearrange("p (b s) -> p b s", b=B)
        dmv = dmv_.rearrange("p (b s) -> p b s", b=B)
        dlg, deq, dl2, do1, do2 = (v.rearrange("p (b e) -> p b e", b=B) for v in (dlg_, deq_, dl2_, do1_, do2_))
        cT = cT_[0:2 * B, :]
        d_at = 2 * W1N
        dzH = R1[:, d_at:d_at + 4 * NT].rearrange("p (r t) -> p r t", r=4)
        dzL = R1[:, d_at + 4 * NT:d_at + 8 * NT].rearrange("p (r t) -> p r t", r=4)
        dsH, dsL, dcH, dcL = (R1[:, d_at + i * NT:d_at + (i + 2) * NT].rearrange("p (u t) -> p u t", u=2)
                              for i in (8, 10, 12, 14))
        dwH, dwL = R1[:, d_at + 16 * NT:d_at + 17 * NT], R1[:, d_at + 17 * NT:d_at + 18 * NT]
        dw = dw_.rearrange("p (r t) -> p r t", r=3)
        dz = [dw[:, 0], dw[:, 1], dw[:, 2], dc1[:, 0]]
        assert d_at + 19 * NT <= r_at
        mneg, mtop, msum, mrcp = (small[0:2 * B, 300 + i:301 + i] for i in range(4))

        def w1_tile(j, at, n):
            a0 = W1X + j * W1T + at
            return w1H[:, a0:a0 + n], w1L[:, a0:a0 + n]

        EV = [(0, 0)]
        for j in range(1, SJ):
            EV += [(j, 0), (j - 1, 1)]
        EV.append((SJ - 1, 1))
        NE = len(EV)
        Z_ORDER = (0, 2, 1, 3)
        at_ev = {ev: i for i, ev in enumerate(EV)}

        consts_ready = sem("consts_ready")
        x0_loaded, xrest_loaded = sem("x0_loaded"), sem("xrest_loaded")
        gates_loaded, small_loaded, toep_loaded = sem("gates_loaded"), sem("small_loaded"), [sem("toep_loaded0"), sem("toep_loaded1")]
        ctxN_loaded = sem("ctxN_loaded")
        ctxT_loaded = [sem("ctxT_loaded0"), sem("ctxT_loaded1")]
        stg_loaded = [sem("stg_loaded0"), sem("stg_loaded1")]
        wH_ready, wL_ready = sem("wH_ready"), sem("wL_ready")
        gate_ready = sem("gate_ready")
        dve_step = sem("dve_step")
        ve_ready, sd_ready, ln_ready, vN_ready = sem("ve_ready"), sem("sd_ready"), sem("ln_ready"), sem("vN_ready")
        vtp_ready, vT_ready, bvx_ready, w_ready, t_done = (
            sem("vtp_ready"), sem("vT_ready"), sem("bvx_ready"), sem("w_ready"), sem("t_done"))
        kv_ready, y_ready, z_ready, z4_ready, o_ready, a_done = (
            sem("kv_ready"), sem("y_ready"), sem("z_ready"), sem("z4_ready"), sem("o_ready"), sem("a_done"))
        xturned, xT_ready, xH_ready, xL_ready = sem("xturned"), sem("xT_ready"), sem("xH_ready"), sem("xL_ready")
        logits_ready, expin_ready, exp_ready, spread_ready, spread_turned, comb_ready = (
            sem("logits_ready"), sem("expin_ready"), sem("exp_ready"), sem("spread_ready"), sem("spread_turned"),
            sem("comb_ready"))
        gu_ready, silu_ready, scaled_ready, h_ready, hH_ready, hL_ready, down_done, b_done = (
            sem("gu_ready"), sem("silu_ready"), sem("scaled_ready"), sem("h_ready"), sem("hH_ready"), sem("hL_ready"),
            sem("down_done"), sem("b_done"))
        kbd_zeroed, qT_turned, qT_ready = sem("kbd_zeroed"), sem("qT_turned"), sem("qT_ready")
        kbd_loaded = [sem("kbd_loaded0"), sem("kbd_loaded1")]
        va_loaded = [sem("va_loaded0"), sem("va_loaded1")]
        stg1_loaded = [sem("stg1_loaded0"), sem("stg1_loaded1")]
        w1H_ready, w1L_ready = sem("w1H_ready"), sem("w1L_ready")
        scores_ready, shifted, exp_done, p_turned, pT_ready, pv_done, o_read, c_done = (
            sem("scores_ready"), sem("shifted"), sem("exp_done"), sem("p_turned"), sem("pT_ready"), sem("pv_done"),
            sem("o_read"), sem("c_done"))
        d_logits, tops_ready, tops_turned, topmax_ready, cexp_ready, c_ready, c_back, ctok_ready = (
            sem("d_logits"), sem("tops_ready"), sem("tops_turned"), sem("topmax_ready"), sem("cexp_ready"),
            sem("c_ready"), sem("c_back"), sem("ctok_ready"))
        hot_ready = [sem("hot_ready0"), sem("hot_ready1")]
        dM_turned, dM_ready, dMD_ready = sem("dM_turned"), sem("dM_ready"), sem("dMD_ready")
        dcb_turned, dcb_ready = sem("dcb_turned"), sem("dcb_ready")
        z_psum, zm_ready, zH_ready, zL_ready = sem("z_psum"), sem("zm_ready"), sem("zH_ready"), sem("zL_ready")
        ev_ready, dsilu_ready, dscaled_ready, ch_ready, sum_ready = (
            sem("ev_ready"), sem("dsilu_ready"), sem("dscaled_ready"), sem("ch_ready"), sem("sum_ready"))
        cH_ready, cL_ready, sH_ready, sL_ready, ddown_done = (
            sem("cH_ready"), sem("cL_ready"), sem("sH_ready"), sem("sL_ready"), sem("ddown_done"))
        w_mixed, w_sum, wsH_ready, wsL_ready, dn_ready, d_done = (
            sem("w_mixed"), sem("w_sum"), sem("wsH_ready"), sem("wsL_ready"), sem("dn_ready"), sem("d_done"))
        out_stored = sem("out_stored")

        block = es.enter_context(nc.Block())
        SPLIT_AT = (2, 6, 10, 14)
        CH = len(SPLIT_AT)

        @block.sync
        def _(sp):
            sp.dma_start(X[:, 0:BG, :], x[0:BG].rearrange("b p d -> p b d")).then_inc(x0_loaded, 16)
            sp.dma_start(gate_in[:], gates.partition_broadcast(P)).then_inc(gates_loaded, 16)
            sp.dma_start(bias_c[:], bias.rearrange("(p a) -> p a", a=1)).then_inc(gates_loaded, 16)
            for s in range(2):
                sp.dma_start(ctxT[:, s], ctx_half[0, s]).then_inc(ctxT_loaded[s], 16)
            sp.dma_start(toep[:, 0:TOEP_H], filt[:, 0:TOEP_H]).then_inc(toep_loaded[0], 16)
            sp.dma_start(ctxN, ctx_nat[0:BG].rearrange("b p d -> p b d")).then_inc(ctxN_loaded, 16)
            sp.dma_start(toep[:, TOEP_H:], filt[:, TOEP_H:]).then_inc(toep_loaded[1], 16)
            sp.dma_start(X[:, BG:B, :], x[BG:B].rearrange("b p d -> p b d")).then_inc(xrest_loaded, 16)
            sp.dma_start(ramp[:], ramp_in.partition_broadcast(P)).then_inc(small_loaded, 16)
            sp.dma_start(wr_sb[:], wr.rearrange("p (k n) -> p k n", k=DT)).then_inc(small_loaded, 16)
            sp.dma_start(gw_sb[:], gw.rearrange("p (k n) -> p k n", k=DT)).then_inc(small_loaded, 16)

            def weights(c, first=False):
                u = c[1] % 2
                n = c[0] * CH + c[1]
                if not first:
                    sp.wait_ge(wL_ready, n - 1)
                sp.dma_start(stg[:, u, :], w0[n]).then_inc(stg_loaded[u], 16)

            weights((0, 0), True)
            weights((0, 1), True)

            def loads(g, n_chunks, more):
                if more:
                    sp.wait_ge(t_done, g + 1)
                    sp.dma_start(ctxN, ctx_nat[bass.ds((g + 1) * BG, BG)].rearrange("b p d -> p b d")
                                 ).then_inc(ctxN_loaded, 16)
                for c in range(n_chunks):
                    weights((g, c + 2))
                    if more and c % 2:
                        s = c // 2
                        sp.wait_ge(z_ready, 1 + NH0 * g + NH0 // 2 * (s + 1))
                        sp.dma_start(ctxT[:, s], ctx_half[bass.ds(g + 1, 1), s].rearrange("a p q t -> (a p) q t")
                                     ).then_inc(ctxT_loaded[s], 16)
            with sp.Fori(0, G - 1) as g:
                loads(g, CH, True)
            loads(G - 1, J0 - CH * (G - 1) - 2, False)
            sp.wait_ge(a_done, 1 + 2 * G)
            if PHASES == 2:
                sp.wait_ge(b_done, 1 + 2 * G)

            def keys(g, r):
                src = ctx_t[bass.ds(g, 1)].rearrange("a p (k b) t -> (a p) b k t", k=DT)
                for h in range(HH):
                    for b in range(2):
                        sp.dma_start(kbd[h * HD:(h + 1) * HD, r, b, :, h, :],
                                     src[h * HD:(h + 1) * HD, 2 * r + b, :, :]).then_inc(kbd_loaded[r], 16)

            def values(g, r):
                sp.dma_start(va[:, r], ctx_one[bass.ds(g * BG + 2 * r, 2)].rearrange("b p h e -> p b h e")
                             ).then_inc(va_loaded[r], 16)

            def weights1(g, r):
                if not isinstance(g, int) or g > 0:
                    sp.wait_ge(w1L_ready, 2 * g + r - 1)
                sp.dma_start(stg1[r], w1[bass.ds(2 * g + r, 1)].rearrange("a p n -> (a p) n")
                             ).then_inc(stg1_loaded[r], 16)

            if PHASES > 2:
                sp.wait_ge(kbd_zeroed, J0 - 1)
                for r in range(2):
                    keys(0, r)
                    values(0, r)
                sp.wait_ge(b_done, 1 + 2 * G)
                for r in range(2):
                    weights1(0, r)
                with sp.Fori(0, G - 1) as g:
                    for r in range(2):
                        sp.wait_ge(scores_ready, 8 * g + 4 * r + 4)
                        keys(g + 1, r)
                        weights1(g + 1, r)
                        sp.wait_ge(pv_done, 1 + 8 * g + 4 * r + 4)
                        values(g + 1, r)
                sp.wait_ge(c_done, B)
            if PHASES > 3:
                with sp.Fori(0, G) as g:
                    sp.wait_ge(d_done, 1 + 2 * (g + 1))
                    sp.dma_start(out[bass.ds(g * BG, BG)].rearrange("b p d -> p b d"), X[:, bass.ds(g * BG, BG), :]
                                 ).then_inc(out_stored, 16)
                sp.wait_ge(out_stored, 16 * G)
            else:
                sp.dma_start(out.rearrange("b p d -> p b d"), X[:]).then_inc(out_stored, 16)
                sp.wait_ge(out_stored, 16)

        @block.gpsimd
        def _(pool):
            for counted in (y_ready, z_ready, z4_ready, o_ready, a_done, h_ready, down_done, b_done,
                            o_read, pv_done, ch_ready, ddown_done, w_mixed, dn_ready, d_done):
                pool.sem_inc(counted, 1)
            c = Count(consts_ready)
            c.mark(nc.gpsimd.memset(ident[:], 0.0))
            c.mark(nc.gpsimd.memset(ones_blk[:], 1.0))
            c.mark(nc.gpsimd.memset(neg[:], 0.0))
            pool.wait_ge(consts_ready, 3)
            c.mark(nc.gpsimd.affine_select(out=ident[:], in_=ident[:], compare_op=ALU.not_equal, fill=1.0, base=0,
                                           pattern=[[-1, P]], channel_multiplier=1))
            c.mark(nc.gpsimd.affine_select(out=ones_blk[:], in_=ones_blk[:], compare_op=ALU.is_ge, fill=0.0, base=0,
                                           pattern=[[-I0, NH0], [0, I0]], channel_multiplier=1))
            c.mark(nc.gpsimd.affine_select(out=neg[:], in_=neg[:], compare_op=ALU.is_ge, fill=FAR, base=0,
                                           pattern=[[0, 4], [-1, P]], channel_multiplier=1))
            pool.wait_ge(consts_ready, 6)
            c.mark(nc.gpsimd.affine_select(out=ones_blk[:], in_=ones_blk[:], compare_op=ALU.is_ge, fill=0.0,
                                           base=I0 - 1, pattern=[[I0, NH0], [0, I0]], channel_multiplier=-1))
            c.mark(nc.gpsimd.tensor_copy(identb[:], ident[:]))

            def split_low(g, c):
                n = g * CH + c
                pool.wait_ge(wH_ready, n + 1)
                nc.gpsimd.tensor_tensor(w0L[:, bass.ds(n, 1), :], stg[:, c % 2:c % 2 + 1, :],
                                        w0H[:, bass.ds(n, 1), :].bitcast(F32), ALU.subtract).then_inc(wL_ready, 1)

            def a_add(g, h):
                u = h % 2
                pool.wait_ge(z_ready, 1 + NH0 * g + h + 1)
                if h == 0:
                    pool.wait_ge(o_ready, 1 + 2 * g)
                nc.gpsimd.tensor_tensor(z4[:, :, :, h * I0:(h + 1) * I0], zr[:, u, :, 0:HALF, :],
                                        zr[:, u, :, HALF:, :], ALU.add).then_inc(z4_ready, 1)

            def a_adds(g):
                for h in range(NH0):
                    a_add(g, h)
                    if h in SPLIT_AT:
                        split_low(g, SPLIT_AT.index(h))
            with pool.Fori(0, G - 1) as g:
                a_adds(g)
            a_adds(G - 1)
            for c in range(CH, J0 - CH * (G - 1)):
                split_low(G - 1, c)

            if PHASES > 2:
                pool.wait_ge(h_ready, 1 + J0 * (G - 1))
                for j in range(J0 - 1):
                    nc.gpsimd.memset(kbd_[:, j * 512:(j + 1) * 512], 0.0).then_inc(kbd_zeroed, 1)

            def split_low1(g, r):
                n = 2 * g + r
                pool.wait_ge(w1H_ready, n + 1)
                dst = bass.ds(n * W1C, W1C)
                nc.gpsimd.tensor_tensor(w1L[:, dst], stg1[r], w1H[:, dst].bitcast(F32), ALU.subtract
                                        ).then_inc(w1L_ready, 1)
            if PHASES > 2:
                with pool.Fori(0, G) as g:
                    for r in range(2):
                        split_low1(g, r)

            if PHASES > 3:
                def d_difference(g):
                    nc.gpsimd.tensor_tensor(dMD, dM2[:, bass.ds(g, 1)], dM1[:, bass.ds(g, 1)].bitcast(F32),
                                            ALU.subtract).then_inc(dMD_ready, 1)
                pool.wait_ge(dM_ready, 2 * G)
                d_difference(0)
                with pool.Fori(0, G - 1) as g:
                    pool.wait_ge(zm_ready, 4 * (g + 1))
                    d_difference(g + 1)

        @block.scalar
        def _(act):
            act.wait_ge(gates_loaded, 32)
            nc.scalar.activation(gate[:], gate_in[:], ACT.Tanh).then_inc(gate_ready, 1)

            def normed(g, dst, phase=0):
                act.wait_ge(ln_ready, G * phase + g + 1)
                for b in range(BG):
                    nc.scalar.activation(dst[:, b:b + 1, :], X[:, bass.ds(g * BG + b, 1), :], ACT.Identity,
                                         bias=nb[:, b:b + 1], scale=rs[:, b:b + 1]).then_inc(vN_ready, 1)

            def a_prep(g, first=False):
                if not first:
                    act.wait_ge(w_ready, g)
                normed(g, vN)

            def a_turned(g, first=False):
                act.wait_ge(vtp_ready, g + 1)
                if not first:
                    act.wait_ge(kv_ready, NH0 * g)
                for k in range(DT):
                    nc.scalar.activation(vT[:, k * BG:(k + 1) * BG, :], TV[:, k * NT:(k + 1) * NT], ACT.Copy
                                         ).then_inc(vT_ready, 1)

            def split_high(g, c):
                n = g * CH + c
                act.wait_ge(stg_loaded[c % 2], (g * (CH // 2) + c // 2 + 1) * 16)
                nc.scalar.activation(w0H[:, bass.ds(n, 1), :], stg[:, c % 2:c % 2 + 1, :], ACT.Copy).then_inc(wH_ready, 1)

            a_prep(0, True)
            a_turned(0, True)
            with act.Fori(0, G - 1) as g:
                split_high(g, 0)
                split_high(g, 1)
                a_prep(g + 1)
                for c in range(2, CH):
                    split_high(g, c)
                a_turned(g + 1)

            def norm_one(g, b, dst, phase):
                if b == 0:
                    act.wait_ge(ln_ready, G * phase + g + 1)
                nc.scalar.activation(dst[:, b:b + 1, :], X[:, bass.ds(g * BG + b, 1), :], ACT.Identity,
                                     bias=nb[:, b:b + 1], scale=rs[:, b:b + 1]).then_inc(vN_ready, 1)

            def b_norm(g, b):
                if b == 0:
                    if isinstance(g, int) and g == 0:
                        act.wait_ge(t_done, G)
                    else:
                        act.wait_ge(spread_turned, g)
                norm_one(g, b, xn, 1)

            def b_turned(g):
                act.wait_ge(xturned, g + 1)
                if not (isinstance(g, int) and g == 0):
                    act.wait_ge(xL_ready, 2 * g)
                nc.scalar.activation(xT, TP[:].rearrange("p (k t) -> p k t", k=DT), ACT.Copy).then_inc(xT_ready, 1)

            def b_exp(g):
                act.wait_ge(expin_ready, g + 1)
                nc.scalar.activation(es_, es_, ACT.Exp).then_inc(exp_ready, 1)

            def b_high_x(g):
                act.wait_ge(xT_ready, g + 1)
                for k in range(DT):
                    nc.scalar.activation(xH[:, k], xT[:, k], ACT.Copy).then_inc(xH_ready, 1)

            def b_take_comb(g):
                act.wait_ge(spread_turned, g + 1)
                nc.scalar.activation(b_comb, TP[:].rearrange("p (r t) -> p r t", r=2), ACT.Copy).then_inc(comb_ready, 1)

            def b_silu_of(g, j, first=False):
                pr = TAIL if j == J0 - 1 else P
                act.wait_ge(gu_ready, J0 * g + j + 1)
                if not first:
                    act.wait_ge(h_ready, 1 + J0 * g + j - 1)
                nc.scalar.activation(b_silu[0:pr, j % 2], G_[j % 2][0:pr], ACT.Silu).then_inc(silu_ready, 1)

            def b_high(g, j):
                pr = TAIL if j == J0 - 1 else P
                act.wait_ge(h_ready, 1 + J0 * g + j + 1)
                if j >= 2:
                    act.wait_ge(down_done, 1 + J0 * g + j - 1)
                else:
                    act.wait_ge(down_done, 1 + J0 * g)
                nc.scalar.activation(hH[0:pr, j % 2], b_h[0:pr, j % 2], ACT.Copy).then_inc(hH_ready, 1)

            def b_tiles(g, more):
                for j in range(1, J0):
                    b_silu_of(g, j)
                    if more and j == J0 - 1:
                        act.wait_ge(gu_ready, J0 * (g + 1))
                        b_high_x(g + 1)
                    b_high(g, j - 1)
                    if more and 6 <= j < 10:
                        b_norm(g + 1, j - 6)
                    if more and j == 11:
                        b_turned(g + 1)
                    if more and j == 14:
                        b_exp(g + 1)
                    if not more and 10 <= j < 14 and PHASES > 2:
                        norm_one(0, j - 10, qn, 2)
                if more:
                    act.wait_ge(scaled_ready, J0 * (g + 1))
                    b_take_comb(g + 1)
                b_high(g, J0 - 1)
                if more:
                    b_silu_of(g + 1, 0)

            for c in range(J0 - CH * (G - 1)):
                split_high(G - 1, c)
                if PHASES > 1:
                    if c == 1:
                        for b in range(BG):
                            b_norm(0, b)
                    if c == 2:
                        b_turned(0)
                    if c == 4:
                        b_exp(0)
            if PHASES > 1:
                act.wait_ge(a_done, 1 + 2 * G)
                b_high_x(0)
                b_take_comb(0)
                b_silu_of(0, 0, True)
                with act.Fori(0, G - 1) as g:
                    b_tiles(g, True)
                b_tiles(G - 1, False)

            def c_high(g, r):
                n = 2 * g + r
                act.wait_ge(stg1_loaded[r], 16 * (g + 1))
                nc.scalar.activation(w1H[:, bass.ds(n * W1C, W1C)], stg1[r], ACT.Copy).then_inc(w1H_ready, 1)

            def c_exp(g, k):
                n = 8 * g + k
                act.wait_ge(shifted, n + 1)
                nc.scalar.activation(E_[:, k % 2], E_[:, k % 2], ACT.Exp).then_inc(exp_done, 1)

            def c_evac(g, k):
                n = 8 * g + k
                act.wait_ge(p_turned, n + 1)
                if isinstance(n, int) and n < 2:
                    pass
                else:
                    act.wait_ge(pv_done, 1 + n - 1)
                nc.scalar.activation(PT_[:, k % 2], PTP[:].rearrange("p (h k) -> p h k", h=HH), ACT.Copy
                                     ).then_inc(pT_ready, 1)

            def c_take_q(g, b):
                act.wait_ge(qT_turned, BG * g + b + 1)
                act.wait_ge(scores_ready, 8 * (g - 1) + 2 * b + 2)
                nc.scalar.activation(qT[:, b], TQ.rearrange("p (k t) -> p k t", k=DT), ACT.Copy).then_inc(qT_ready, 1)

            def c_steps(g, more):
                if more:
                    act.wait_ge(qT_turned, BG * (g + 1))
                    normed(g + 1, qn, 2)
                for k in range(8):
                    if k < 7 or more:
                        c_evac(g + (k + 1) // 8, (k + 1) % 8)
                    if k < 6 or more:
                        c_exp(g + (k + 2) // 8, (k + 2) % 8)
                    if more and k in TURN_AT:
                        c_take_q(g + 1, TURN_AT.index(k))
                    if k in (3, 6):
                        c_high(g, k // 4)

            if PHASES > 2:
                act.wait_ge(qT_turned, BG)
                act.wait_ge(b_done, 1 + 2 * G)
                for b in range(BG):
                    nc.scalar.activation(qT[:, b], bank[2][:, b * D:(b + 1) * D].rearrange("p (k t) -> p k t", k=DT),
                                         ACT.Copy).then_inc(qT_ready, 1)
                c_exp(0, 0)
                c_exp(0, 1)
                c_evac(0, 0)
                c_first = True
                with act.Fori(0, G - 1) as g:
                    c_steps(g, True)
                c_steps(G - 1, False)

            def d_choose():
                for g in range(G):
                    act.wait_ge(ln_ready, 3 * G + (1 if g < G - 1 else 2))
                    if g >= 2:
                        act.wait_ge(xturned, G + g - 1)
                    for b in range(BG):
                        t = g * BG + b
                        nc.scalar.activation(dxn[:, g % 2, b], X[:, t], ACT.Identity, bias=dnb[:, t:t + 1],
                                             scale=drs[:, t:t + 1]).then_inc(vN_ready, 1)
                act.wait_ge(topmax_ready, 1)
                nc.scalar.activation(cT, bank[2][0:2 * B, 512:512 + P], ACT.Exp, bias=mneg, accum_out=msum
                                     ).then_inc(cexp_ready, 1)
                d_take_masks(0)
                act.wait_ge(c_ready, 1)
                nc.scalar.activation(cT, cT, ACT.Copy, scale=mrcp).then_inc(cexp_ready, 1)
                for g in range(1, G):
                    d_take_masks(g)
                d_high_x(0)
                d_high_z(0)

            def d_take_masks(g):
                act.wait_ge(dM_turned, g + 1)
                for r, dst in enumerate((dM1, dM2)):
                    nc.scalar.activation(dst[:, g], bank[g % 2][:, r * 512:(r + 1) * 512], ACT.Copy
                                         ).then_inc(dM_ready, 1)

            def d_high_x(g):
                for k in range(DT):
                    nc.scalar.activation(xH[:, k], dxT[:, bass.ds(g, 1), k], ACT.Copy).then_inc(xH_ready, 1)

            def d_high_z(g):
                for n, r in enumerate(Z_ORDER):
                    act.wait_ge(zm_ready, 4 * g + n + 1)
                    nc.scalar.activation(dzH[:, r], dz[r], ACT.Copy).then_inc(zH_ready, 1)

            def d_silu(g, j, k, first=False):
                i = at_ev[j, k]
                pr = TAIL if j == SJ - 1 else P
                act.wait_ge(ev_ready, NE * g + i + 1)
                if not first:
                    act.wait_ge(ch_ready, 1 + NE * g + i - 1)
                nc.scalar.activation(dsilu[0:pr, i % 2], U_[j % 2][0:pr], ACT.Silu).then_inc(dsilu_ready, 1)

            def d_high_first(g, j, first=False):
                pr = TAIL if j == SJ - 1 else P
                act.wait_ge(ch_ready, 1 + NE * g + at_ev[j, 0] + 1)
                if not first:
                    act.wait_ge(ddown_done, 1 + SJ * g + j - 1)
                nc.scalar.activation(dcH[0:pr, j % 2], dc1[0:pr, j % 2], ACT.Copy).then_inc(cH_ready, 1)

            def d_high_sum(g, j):
                pr = TAIL if j == SJ - 1 else P
                act.wait_ge(sum_ready, SJ * g + j + 1)
                nc.scalar.activation(dsH[0:pr, j % 2], dc2[0:pr, j % 2], ACT.Copy).then_inc(sH_ready, 1)

            def d_first(g, first=False):
                d_silu(g, 0, 0, first)
                d_high_first(g, 0, first)

            def d_tiles(g, more):
                for j in range(1, SJ):
                    d_silu(g, j, 0)
                    d_silu(g, j - 1, 1)
                    if more and j == SJ - 1:
                        act.wait_ge(ev_ready, NE * g + at_ev[SJ - 1, 0] + 1)
                        d_high_x(g + 1)
                    d_high_first(g, j)
                    d_high_sum(g, j - 1)
                d_silu(g, SJ - 1, 1)
                d_high_sum(g, SJ - 1)
                if more:
                    d_high_z(g + 1)
                act.wait_ge(w_sum, g + 1)
                act.wait_ge(dn_ready, 1 + g)
                nc.scalar.activation(dwH, dw[:, 2], ACT.Copy).then_inc(wsH_ready, 1)
                if more:
                    d_first(g + 1)

            if PHASES > 3:
                act.wait_ge(c_done, B)
                d_choose()
                d_first(0, True)
                with act.Fori(0, G - 1) as g:
                    d_tiles(g, True)
                d_tiles(G - 1, False)

        @block.vector
        def _(dve):
            step = Count(dve_step)

            def link(ins):
                step.mark(ins)
                dve.wait_ge(dve_step, step.value())

            def stats_parts(g, gain):
                def moments():
                    for b in range(BG):
                        step.mark(nc.vector.bn_stats(st[:, b, :], X[:, bass.ds(g * BG + b, 1), :]))
                return [moments] + shift_parts(st, mv, ve[:], sd[:], rs[:], nb[:], gain)

            def shift_parts(st, mv, ve, tmp, rs, nb, gain):
                def guess():
                    dve.wait_ge(dve_step, step.value())
                    step.mark(nc.vector.memset(scrap[:], 0.0))
                    for b in range(mv.shape[1]):
                        step.mark(nc.vector.bn_aggr(mv[:, b, :], st[:, b, :]))
                    dve.wait_ge(dve_step, step.value())
                    link(nc.vector.tensor_scalar(ve, mv[:, :, 1], EPS, None, ALU.add))
                    link(nc.vector.tensor_scalar(rs.bitcast(I32), ve.bitcast(I32), 1, None, ALU.logical_shift_right))
                    link(nc.vector.tensor_scalar(rs.bitcast(I32), rs.bitcast(I32), -1, RSQRT_GUESS, ALU.mult, ALU.add))

                def newton(last=False):
                    link(nc.vector.tensor_tensor(tmp, rs, rs, ALU.mult))
                    link(nc.vector.tensor_tensor(tmp, tmp, ve, ALU.mult))
                    link(nc.vector.tensor_scalar(tmp, tmp, -0.5, 1.5, ALU.mult, ALU.add))
                    if last and gain is not None:
                        link(nc.vector.scalar_tensor_tensor(out=rs, in0=rs, scalar=gain, in1=tmp,
                                                            op0=ALU.mult, op1=ALU.mult))
                    else:
                        link(nc.vector.tensor_tensor(rs, rs, tmp, ALU.mult))

                def shift():
                    newton(True)
                    nc.vector.scalar_tensor_tensor(out=nb, in0=mv[:, :, 0], scalar=-1.0, in1=rs,
                                                   op0=ALU.mult, op1=ALU.mult).then_inc(ln_ready, 1)
                return [guess, newton, newton, shift]

            def stats(g, gain):
                for part in stats_parts(g, gain):
                    part()

            def scale_shift(*args):
                for part in shift_parts(*args):
                    part()
            N_STATS = 2 * BG + 1 + 1 + 2 + 3 * 4

            def a_kv(g, h, first=False):
                u = h % 2
                t0 = h * I0
                c = ctxT[:, h // 8, :, t0 % 64:t0 % 64 + I0]
                if not first:
                    dve.wait_ge(y_ready, 1 + NH0 * g + h - 1)
                nc.vector.tensor_tensor(
                    kv[:, u], vT[:, :, t0:t0 + I0].unsqueeze(3).to_broadcast([P, 8, I0, I0]),
                    c.unsqueeze(2).to_broadcast([P, 8, I0, I0]), ALU.mult).then_inc(kv_ready, 1)

            def a_z(g, h, first=False):
                u = h % 2
                t0 = h * I0
                c = ctxT[:, h // 8, :, t0 % 64:t0 % 64 + I0]
                dve.wait_ge(y_ready, 1 + NH0 * g + h + 1)
                if not first:
                    dve.wait_ge(z4_ready, NH0 * g + h)
                nc.vector.tensor_tensor(
                    zr[:, u], yb[u].rearrange("p (q i j) -> p q i j", q=8, i=I0),
                    c.unsqueeze(3).to_broadcast([P, 8, I0, I0]), ALU.mult).then_inc(z_ready, 1)

            def a_bias(g):
                dve.wait_ge(vtp_ready, g + 1)
                dve.wait_ge(ctxN_loaded, 16 * (g + 1))
                nc.vector.scalar_tensor_tensor(out=vN, in0=vN, scalar=bias_c[:, 0:1], in1=ctxN,
                                               op0=ALU.mult, op1=ALU.mult).then_inc(bvx_ready, 1)

            def a_skip(g):
                dve.wait_ge(w_ready, g + 1)
                Xg = X[:, bass.ds(g * BG, BG), :]
                link(nc.vector.tensor_tensor(vN, WB[:].rearrange("p (b d) -> p b d", b=BG), ctxN, ALU.mult))
                nc.vector.tensor_tensor(Xg, Xg, vN, ALU.add).then_inc(t_done, 1)

            def a_finish(g):
                for k in range(2):
                    dve.wait_ge(o_ready, 1 + 2 * g + 1 + k)
                    if k == 0:
                        dve.wait_ge(t_done, g + 1)
                    Xg = X[:, bass.ds(g * BG + 2 * k, 2), :]
                    nc.vector.tensor_tensor(Xg, Xg, OB[:, k * 512:(k + 1) * 512].rearrange("p (b d) -> p b d", b=2),
                                            ALU.add).then_inc(a_done, 1)

            def a_heads(g, more):
                if more:
                    beside = dict(zip((2, 3, 4, 5, 6), stats_parts(g + 1, gate[:, 0:1])))
                elif PHASES > 1:
                    beside = dict(zip((2, 3, 4, 5, 6, 12, 13, 14, 15), stats_parts(0, None) + route_parts(0)))
                else:
                    beside = {}
                for h in range(2, NH0 + 2 if more else NH0):
                    if h < NH0:
                        a_z(g, h)
                    else:
                        a_z(g + 1, h - NH0)
                    if h + 2 < NH0:
                        if h + 2 == NH0 // 2:
                            dve.wait_ge(ctxT_loaded[1], 16 * (g + 1))
                        a_kv(g, h + 2)
                    elif more:
                        if h + 2 == NH0:
                            dve.wait_ge(vT_ready, 2 * (g + 2))
                            dve.wait_ge(ctxT_loaded[0], 16 * (g + 2))
                        a_kv(g + 1, h + 2 - NH0)
                    if h in beside:
                        beside[h]()
                    if more and h == 11:
                        a_bias(g + 1)
                    if more and h == 15:
                        a_skip(g + 1)

            def top2(lg, eq, rk, l2, m1, m2, dst1, dst2, found=None):
                n = lg.shape[1]

                def first_max(src, mx, dst, found=None):
                    wide = lambda v: v.unsqueeze(2).to_broadcast([P, n, E])
                    order = ramp[:].unsqueeze(1).to_broadcast([P, n, E])
                    if found is None:
                        link(nc.vector.tensor_reduce(mx, src, AX_X, ALU.max))
                    else:
                        nc.vector.tensor_reduce(mx, src, AX_X, ALU.max).then_inc(found, 1)
                        dve.wait_ge(found, 1)
                    link(nc.vector.tensor_tensor(eq, src, wide(mx), ALU.is_equal))
                    link(nc.vector.tensor_tensor(eq, eq, order, ALU.mult))
                    link(nc.vector.tensor_reduce(rk, eq, AX_X, ALU.max))
                    link(nc.vector.tensor_tensor(dst, order, wide(rk), ALU.is_equal))

                def second():
                    link(nc.vector.scalar_tensor_tensor(out=l2, in0=dst1, scalar=FAR, in1=lg,
                                                        op0=ALU.mult, op1=ALU.add))
                    first_max(l2, m2, dst2, found)
                return [lambda: first_max(lg, m1, dst1), second]

            def route_parts(g):
                tops = top2(lg[:, :, 0:E], eq, rk[:, :, 0], l2, m1, m2, oh1, oh2)

                def first():
                    dve.wait_ge(logits_ready, g + 1)
                    link(nc.vector.tensor_copy(lg, TP[:, 0:BG * NR].rearrange("p (b e) -> p b e", b=BG)))
                    tops[0]()
                    step.mark(nc.vector.tensor_tensor(es_[:, :, 0:E], lg[:, :, 0:E],
                                                      m1.unsqueeze(2).to_broadcast([P, BG, E]), ALU.subtract))
                    nc.vector.tensor_scalar(es_[:, :, E], lg[:, :, E], -1.0, None, ALU.mult).then_inc(expin_ready, 1)

                def second():
                    tops[1]()
                    link(nc.vector.tensor_tensor(oh1, oh1, oh2, ALU.add))

                def weigh():
                    dve.wait_ge(exp_ready, g + 1)
                    step.mark(nc.vector.tensor_reduce(den[:, 0:BG], es_[:, :, 0:E], AX_X, ALU.add))
                    link(nc.vector.tensor_scalar(den[:, BG:], es_[:, :, E], 1.0, None, ALU.add))
                    link(nc.vector.reciprocal(rcp, den))
                    link(nc.vector.tensor_tensor(oh1, oh1, es_[:, :, 0:E], ALU.mult))
                    link(nc.vector.tensor_tensor(oh1, oh1, rcp[:, 0:BG].unsqueeze(2).to_broadcast([P, BG, E]), ALU.mult))

                def spread_out():
                    step.mark(nc.vector.tensor_copy(spread[:, 0].rearrange("p b (e r) -> p b e r", e=E),
                                                    oh1.unsqueeze(3).to_broadcast([P, BG, E, RANK])))
                    nc.vector.tensor_copy(spread[:, 1], rcp[:, BG:].unsqueeze(2).to_broadcast([P, BG, P])
                                          ).then_inc(spread_ready, 1)
                return [first, second, weigh, spread_out]
            N_ROUTE = 1 + 11 + 1 + 1 + 1 + 1 + 1 + 1 + 1 + 1

            def b_low_x(g):
                for k in range(DT):
                    dve.wait_ge(xH_ready, 2 * g + k + 1)
                    nc.vector.tensor_tensor(xL[:, k], xT[:, k], xH[:, k].bitcast(F32), ALU.subtract
                                            ).then_inc(xL_ready, 1)

            def b_hidden(g, j):
                pr = TAIL if j == J0 - 1 else P
                dve.wait_ge(gu_ready, J0 * g + j + 1)
                if j == 0:
                    dve.wait_ge(comb_ready, g + 1)
                nc.vector.tensor_tensor(b_scaled[0:pr, j % 2], U_[j % 2][0:pr], b_comb[0:pr, 0 if j < EJ else 1],
                                        ALU.mult).then_inc(scaled_ready, 1)
                dve.wait_ge(silu_ready, J0 * g + j + 1)
                dve.wait_ge(scaled_ready, J0 * g + j + 1)
                nc.vector.tensor_tensor(b_h[0:pr, j % 2], b_silu[0:pr, j % 2], b_scaled[0:pr, j % 2], ALU.mult
                                        ).then_inc(h_ready, 1)

            def b_low(g, j):
                pr = TAIL if j == J0 - 1 else P
                dve.wait_ge(hH_ready, J0 * g + j + 1)
                nc.vector.tensor_tensor(hL[0:pr, j % 2], b_h[0:pr, j % 2], hH[0:pr, j % 2].bitcast(F32), ALU.subtract
                                        ).then_inc(hL_ready, 1)

            def b_tiles(g, more):
                if more:
                    beside = dict(zip((1, 2, 3, 4, 5, 12, 13, 14, 15), stats_parts(g + 1, None) + route_parts(g + 1)))
                elif PHASES > 2:
                    beside = dict(zip((5, 6, 7, 8, 9), stats_parts(0, HD ** -0.5)))
                else:
                    beside = {}
                for j in range(1, J0):
                    b_hidden(g, j)
                    if more and j == J0 - 1:
                        b_low_x(g + 1)
                    b_low(g, j - 1)
                    if j in beside:
                        beside[j]()
                b_low(g, J0 - 1)
                if more:
                    b_hidden(g + 1, 0)

            def b_finish(g):
                dve.wait_ge(down_done, 1 + J0 * (g + 1))
                for k in range(2):
                    Xg = X[:, bass.ds(g * BG + 2 * k, 2), :]
                    nc.vector.scalar_tensor_tensor(
                        out=Xg, in0=DN[:, k * 512:(k + 1) * 512].rearrange("p (b d) -> p b d", b=2),
                        scalar=gate[:, 2:3], in1=Xg, op0=ALU.mult, op1=ALU.add).then_inc(b_done, 1)

            def c_shift(g, k):
                n = 8 * g + k
                u = k % 2
                dve.wait_ge(scores_ready, n + 1)
                S = S_[u][:].rearrange("p (h k) -> p h k", h=HH)
                link(nc.vector.tensor_reduce(mx[:, u], S, AX_X, ALU.max))
                link(nc.vector.tensor_scalar(mx[:, u], mx[:, u], MASKED, None, ALU.max))
                if not (isinstance(n, int) and n < 2):
                    dve.wait_ge(p_turned, n - 1)
                nc.vector.scalar_tensor_tensor(out=E_[:, u], in0=S, scalar=MASKED,
                                               in1=mx[:, u].unsqueeze(2).to_broadcast([P, HH, P]),
                                               op0=ALU.max, op1=ALU.subtract).then_inc(shifted, 1)

            def c_finish(g, b):
                t = BG * g + b
                dve.wait_ge(pv_done, 1 + 2 * t + 2)
                O = O_.rearrange("p (h e) -> p h e", h=HEADS)
                link(nc.vector.reciprocal(r16, O[:, :, HD]))
                nc.vector.scalar_tensor_tensor(out=otmp, in0=O[:, :, 0:HD], scalar=gate[:, 1:2],
                                               in1=r16.unsqueeze(2).to_broadcast([P, HEADS, HD]),
                                               op0=ALU.mult, op1=ALU.mult).then_inc(o_read, 1)
                dve.wait_ge(o_read, 1 + t + 1)
                Xt = X[:, bass.ds(t, 1), :]
                nc.vector.tensor_tensor(Xt, Xt, otmp.rearrange("p h e -> p (h e)").unsqueeze(1), ALU.add
                                        ).then_inc(c_done, 1)

            def c_steps(g, more):
                if more:
                    stats(g + 1, HD ** -0.5)
                for k in range(8):
                    if k < 6 or more:
                        c_shift(g + (k + 2) // 8, (k + 2) % 8)
                    if k % 2:
                        c_finish(g, k // 2)

            def d_stats(g):
                for b in range(g * BG, (g + 1) * BG):
                    step.mark(nc.vector.bn_stats(dstat[:, b, :], X[:, b]))

            def d_choose():
                n = B - BG
                for g in range(G):
                    d_stats(g)
                    if g == G - 2:
                        scale_shift(dstat[:, 0:n], dmv[:, 0:n], dvar[:, 0:n], dtmp[:, 0:n], drs[:, 0:n], dnb[:, 0:n],
                                    None)
                scale_shift(dstat[:, n:], dmv[:, n:], dvar[:, n:], dtmp[:, n:], drs[:, n:], dnb[:, n:], None)
                for g in range(G):
                    dve.wait_ge(xturned, G + g + 1)
                    nc.vector.tensor_copy(dxT[:, g], bank[g % 2][:].rearrange("p (k t) -> p k t", k=DT)
                                          ).then_inc(xT_ready, 1)
                dve.wait_ge(d_logits, G)
                link(nc.vector.tensor_copy(dlg, bank[2][:, 0:B * E].rearrange("p (b e) -> p b e", b=B)))
                for part in top2(dlg, deq, drk, dl2, dtop[:, 0:B], dtop[:, B:], do1, do2, tops_ready):
                    part()
                for r, hot in enumerate((do1, do2)):
                    ins = nc.vector.tensor_scalar(dhot[:, r].rearrange("p b (e r) -> p b e r", e=E),
                                                  hot.unsqueeze(3).to_broadcast([P, B, E, RANK]), LORA_ALPHA, None,
                                                  ALU.mult)
                    ins.then_inc(hot_ready[r], 1)
                    if r == 0:
                        dve.wait_ge(tops_turned, 1)
                        link(nc.vector.tensor_reduce(mtop, bank[2][0:2 * B, 512:512 + P], AX_X, ALU.max))
                        nc.vector.tensor_scalar(mneg, mtop, -1.0, None, ALU.mult).then_inc(topmax_ready, 1)
                dve.wait_ge(cexp_ready, 1)
                nc.vector.reciprocal(mrcp, msum).then_inc(c_ready, 1)
                dve.wait_ge(c_back, 1)
                nc.vector.tensor_copy(dctok, bank[2][:, 512 + P:512 + P + 2 * B]).then_inc(ctok_ready, 1)
                for g in range(G):
                    dve.wait_ge(dcb_turned, g + 1)
                    nc.vector.tensor_copy(dcb[:, g], bank[3 - g % 2][:].rearrange("p (r t) -> p r t", r=2)
                                          ).then_inc(dcb_ready, 1)
                    if g == 0:
                        d_low_x(0)
                d_split_z(0)

            def d_low_x(g):
                for k in range(DT):
                    dve.wait_ge(xH_ready, 2 * (G + g) + k + 1)
                    nc.vector.tensor_tensor(xL[:, k], dxT[:, bass.ds(g, 1), k], xH[:, k].bitcast(F32), ALU.subtract
                                            ).then_inc(xL_ready, 1)

            def d_split_z(g):
                dve.wait_ge(dMD_ready, g + 1)
                for n, r in enumerate(Z_ORDER):
                    dve.wait_ge(z_psum, 2 * g + n % 2 + 1)
                    m = (dM1[:, bass.ds(g, 1)] if r % 2 == 0 else dMD).bitcast(F32)
                    nc.vector.tensor_tensor(dz[r], (U_, G_)[r // 2][0], m, ALU.mult).then_inc(zm_ready, 1)
                for n, r in enumerate(Z_ORDER):
                    dve.wait_ge(zH_ready, 4 * g + n + 1)
                    nc.vector.tensor_tensor(dzL[:, r], dz[r], dzH[:, r].bitcast(F32), ALU.subtract
                                            ).then_inc(zL_ready, 1)

            def d_rows(g, j, k):
                i = at_ev[j, k]
                pr = TAIL if j == SJ - 1 else P
                dst = (dc1, dc2)[k]
                dve.wait_ge(ev_ready, NE * g + i + 1)
                nc.vector.tensor_tensor(dscaled[0:pr, i % 2], G_[j % 2][0:pr], dcb[0:pr, bass.ds(g, 1), k], ALU.mult
                                        ).then_inc(dscaled_ready, 1)
                dve.wait_ge(dsilu_ready, NE * g + i + 1)
                dve.wait_ge(dscaled_ready, NE * g + i + 1)
                nc.vector.tensor_tensor(dst[0:pr, j % 2], dscaled[0:pr, i % 2], dsilu[0:pr, i % 2], ALU.mult
                                        ).then_inc(ch_ready, 1)
                if k == 1:
                    dve.wait_ge(ch_ready, 1 + NE * g + i + 1)
                    nc.vector.tensor_tensor(dc2[0:pr, j % 2], dc2[0:pr, j % 2], dc1[0:pr, j % 2], ALU.add
                                            ).then_inc(sum_ready, 1)

            def d_low_first(g, j):
                pr = TAIL if j == SJ - 1 else P
                dve.wait_ge(cH_ready, SJ * g + j + 1)
                nc.vector.tensor_tensor(dcL[0:pr, j % 2], dc1[0:pr, j % 2], dcH[0:pr, j % 2].bitcast(F32),
                                        ALU.subtract).then_inc(cL_ready, 1)

            def d_low_sum(g, j):
                pr = TAIL if j == SJ - 1 else P
                dve.wait_ge(sH_ready, SJ * g + j + 1)
                nc.vector.tensor_tensor(dsL[0:pr, j % 2], dc2[0:pr, j % 2], dsH[0:pr, j % 2].bitcast(F32),
                                        ALU.subtract).then_inc(sL_ready, 1)

            def d_mix(g):
                dve.wait_ge(ddown_done, 1 + SJ * (g + 1))
                nc.vector.tensor_tensor(dw[:, 1], bank[2][:, 512:1024], dM1[:, bass.ds(g, 1)].bitcast(F32), ALU.mult
                                        ).then_inc(w_mixed, 1)
                nc.vector.tensor_copy(dw[:, 2], bank[2][:, 512:1024]).then_inc(w_mixed, 1)
                dve.wait_ge(w_mixed, 1 + 4 * g + 2)
                nc.vector.tensor_tensor(dw[:, 0], bank[2][:, 0:512], dw[:, 2], ALU.subtract).then_inc(w_mixed, 1)
                dve.wait_ge(w_mixed, 1 + 4 * g + 3)
                nc.vector.tensor_tensor(dw[:, 0], dw[:, 0], dM2[:, bass.ds(g, 1)], ALU.mult).then_inc(w_mixed, 1)
                dve.wait_ge(w_mixed, 1 + 4 * g + 4)
                nc.vector.tensor_tensor(dw[:, 2], dw[:, 0], dw[:, 1], ALU.add).then_inc(w_sum, 1)
                dve.wait_ge(wsH_ready, g + 1)
                nc.vector.tensor_tensor(dwL, dw[:, 2], dwH.bitcast(F32), ALU.subtract).then_inc(wsL_ready, 1)

            def d_finish(g):
                dve.wait_ge(dn_ready, 1 + g + 1)
                for k in range(2):
                    Xg = X[:, bass.ds(g * BG + 2 * k, 2), :]
                    nc.vector.scalar_tensor_tensor(
                        out=Xg, in0=DN[:, k * 512:(k + 1) * 512].rearrange("p (b d) -> p b d", b=2),
                        scalar=gate[:, 3:4], in1=Xg, op0=ALU.mult, op1=ALU.add).then_inc(d_done, 1)

            def d_first(g):
                d_rows(g, 0, 0)
                d_low_first(g, 0)

            def d_tiles(g, more):
                for j in range(1, SJ):
                    d_rows(g, j, 0)
                    d_rows(g, j - 1, 1)
                    if more and j == SJ - 1:
                        d_low_x(g + 1)
                    d_low_first(g, j)
                    d_low_sum(g, j - 1)
                d_rows(g, SJ - 1, 1)
                d_low_sum(g, SJ - 1)
                if more:
                    dve.wait_ge(dn_ready, 1 + g)
                    d_split_z(g + 1)
                    dve.wait_ge(zL_ready, 4 * (g + 2))
                d_mix(g)
                if more:
                    d_first(g + 1)
                d_finish(g)

            dve.wait_ge(x0_loaded, 16)
            dve.wait_ge(gate_ready, 1)
            stats(0, gate[:, 0:1])
            a_bias(0)
            dve.wait_ge(vT_ready, 2)
            dve.wait_ge(ctxT_loaded[0], 16)
            for h in range(2):
                a_kv(0, h, True)
            a_skip(0)
            for h in range(2):
                a_z(0, h, True)
                a_kv(0, h + 2)
            per = N_STATS + 1
            start = step.value()
            dve.wait_ge(xrest_loaded, 16)
            dve.wait_ge(small_loaded, 16 * 3)
            with dve.Fori(0, G - 1) as g:
                step.enter(g, per, start)
                a_heads(g, True)
                a_finish(g)
            step.leave(per, G - 1, start)
            a_heads(G - 1, False)
            a_finish(G - 1)
            if PHASES > 1:
                b_low_x(0)
                b_hidden(0, 0)
                per = N_STATS + N_ROUTE
                start = step.value()
                with dve.Fori(0, G - 1) as g:
                    step.enter(g, per, start)
                    b_tiles(g, True)
                    b_finish(g)
                step.leave(per, G - 1, start)
                b_tiles(G - 1, False)
                b_finish(G - 1)
            if PHASES > 2:
                c_shift(0, 0)
                c_shift(0, 1)
                per = N_STATS + 2 * 8 + BG
                start = step.value()
                with dve.Fori(0, G - 1) as g:
                    step.enter(g, per, start)
                    c_steps(g, True)
                step.leave(per, G - 1, start)
                c_steps(G - 1, False)
            if PHASES > 3:
                dve.wait_ge(c_done, B)
                dve.wait_ge(w1L_ready, W1K)
                d_choose()
                d_first(0)
                with dve.Fori(0, G - 1) as g:
                    d_tiles(g, True)
                d_tiles(G - 1, False)

        @block.tensor
        def _(pe):
            pe.wait_ge(consts_ready, 8)

            def a_turn(g, first=False):
                pe.wait_ge(vN_ready, BG * (g + 1))
                if not first:
                    pe.wait_ge(vT_ready, 2 * g)
                for k in range(DT):
                    for b in range(BG):
                        mm = nc.tensor.transpose(TV[:, (k * BG + b) * P:(k * BG + b + 1) * P],
                                                 vN[:, b, k * P:(k + 1) * P], ident[:])
                mm.then_inc(vtp_ready, 1)

            def a_block_sums(g, first=False):
                pe.wait_ge(bvx_ready, g + 1)
                if not first:
                    pe.wait_ge(t_done, g)
                ob = ones_blk[:].rearrange("p a b -> p (a b)")
                for k in range(2):
                    mm = nc.tensor.matmul(WB[:, k * 512:(k + 1) * 512], ob, vN[:, 2 * k:2 * k + 2, :],
                                          start=True, stop=True)
                mm.then_inc(w_ready, 1)

            def a_conv(g, h):
                u = h % 2
                pe.wait_ge(toep_loaded[0 if h < TOEP_H else 1], 16)
                pe.wait_ge(kv_ready, NH0 * g + h + 1)
                if h >= 2:
                    pe.wait_ge(z_ready, 1 + NH0 * g + h - 1)
                else:
                    pe.wait_ge(z_ready, 1 + NH0 * g)
                y = yb[u]
                n = BG * I0 * I0
                diag, off = toep[:, h, 0:P], toep[:, h, P:2 * P]
                kv0 = kv[:, u, 0:BG].rearrange("p q i j -> p (q i j)")
                kv1 = kv[:, u, BG:2 * BG].rearrange("p q i j -> p (q i j)")
                nc.tensor.matmul(y[:, 0:n], diag, kv0, start=True, stop=False, skip_group_check=True)
                nc.tensor.matmul(y[:, n:2 * n], diag, kv1, start=False, stop=False, skip_group_check=True)
                nc.tensor.matmul(y[:, n:2 * n], off, kv0, start=False, stop=True, skip_group_check=True
                                 ).then_inc(y_ready, 1)

            def a_sum(g):
                pe.wait_ge(z4_ready, 1 + NH0 * (g + 1))
                pe.wait_ge(a_done, 1 + 2 * g)
                for b in range(BG):
                    for k in range(DT):
                        for i in range(HALF):
                            mm = nc.tensor.matmul(OB[:, b * D + k * P:b * D + (k + 1) * P], z4[:, k * BG + b, i, :],
                                                  ident[:], start=(i == 0), stop=(i == HALF - 1),
                                                  skip_group_check=True)
                    if b % 2:
                        mm.then_inc(o_ready, 1)

            a_turn(0, True)
            a_block_sums(0, True)
            a_conv(0, 0)
            a_conv(0, 1)
            with pe.Fori(0, G - 1) as g:
                for h in range(2, NH0):
                    a_conv(g, h)
                    if h == 10:
                        a_turn(g + 1)
                    if h == 13:
                        a_block_sums(g + 1)
                for h in range(2):
                    a_conv(g + 1, h)
                a_sum(g)

            def b_turn(g):
                pe.wait_ge(vN_ready, BG * (G + g + 1))
                if isinstance(g, int) and g == 0:
                    pe.wait_ge(t_done, G)
                else:
                    pe.wait_ge(comb_ready, g)
                for k in range(DT):
                    for b in range(BG):
                        mm = nc.tensor.transpose(TP[:, (k * BG + b) * P:(k * BG + b + 1) * P],
                                                 xn[:, b, k * P:(k + 1) * P], ident[:])
                mm.then_inc(xturned, 1)

            def b_logits(g):
                pe.wait_ge(xT_ready, g + 1)
                for b in range(BG):
                    for k in range(DT):
                        mm = nc.tensor.matmul(TP[:, b * NR:(b + 1) * NR], xT[:, k, b * P:(b + 1) * P], wr_sb[:, k],
                                              start=(k == 0), stop=(k == DT - 1), skip_group_check=True)
                mm.then_inc(logits_ready, 1)

            def b_spread(g):
                pe.wait_ge(spread_ready, g + 1)
                for r in range(2):
                    for b in range(BG):
                        mm = nc.tensor.transpose(TP[:, (r * BG + b) * P:(r * BG + b + 1) * P], spread[:, r, b],
                                                 ident[:])
                mm.then_inc(spread_turned, 1)

            def b_gate_up(g, j):
                pr = TAIL if j == J0 - 1 else P
                if j == 0:
                    pe.wait_ge(xL_ready, 2 * (g + 1))
                if j >= 2:
                    pe.wait_ge(silu_ready, J0 * g + j - 1)
                else:
                    pe.wait_ge(h_ready, 1 + J0 * g)
                for at, dst in ((0, G_[j % 2]), (2 * P, U_[j % 2])):
                    if j >= 2 and at:
                        pe.wait_ge(scaled_ready, J0 * g + j - 1)
                    n = 0
                    for wX, mX in ((w0H, xH), (w0L, xH), (w0H, xL)):
                        for k in range(DT):
                            mm = nc.tensor.matmul(dst[0:pr], wX[:, j, at + k * P:at + k * P + pr], mX[:, k],
                                                  start=(n == 0), stop=(n == 5))
                            n += 1
                mm.then_inc(gu_ready, 1)

            def b_down(g, j):
                pr = TAIL if j == J0 - 1 else P
                if j == 0:
                    pe.wait_ge(b_done, 1 + 2 * g)
                pe.wait_ge(hL_ready, J0 * g + j + 1)
                for b in range(BG):
                    n = 0
                    for hX, wX in ((hH, w0H), (hH, w0L), (hL, w0H)):
                        mm = nc.tensor.matmul(DN[:, b * D:(b + 1) * D], hX[0:pr, j % 2, b * P:(b + 1) * P],
                                              wX[0:pr, j, 4 * P:], start=(j == 0 and n == 0 and b % 2 == 0),
                                              stop=(j == J0 - 1 and n == 2), skip_group_check=True)
                        n += 1
                mm.then_inc(down_done, 1)

            def b_tiles(g, more):
                for j in range(1, J0):
                    b_gate_up(g, j)
                    if j >= 2:
                        b_down(g, j - 2)
                    if more and j == 10:
                        b_turn(g + 1)
                    if more and j == 12:
                        b_logits(g + 1)
                    if not more and j == 15 and PHASES > 2:
                        pe.wait_ge(vN_ready, BG * (2 * G + 1))
                        for b in range(BG):
                            for k in range(DT):
                                mm = nc.tensor.transpose(bank[2][:, b * D + k * P:b * D + (k + 1) * P],
                                                         qn[:, b, k * P:(k + 1) * P], ident[:])
                            mm.then_inc(qT_turned, 1)
                if more:
                    b_spread(g + 1)
                b_down(g, J0 - 2)
                if more:
                    b_gate_up(g + 1, 0)
                b_down(g, J0 - 1)

            def c_scores(g, k):
                n = 8 * g + k
                r, b, kk = k // 4, k // 2, k % 2
                pe.wait_ge(qT_ready, BG * g + b + 1)
                pe.wait_ge(kbd_loaded[r], 16 * 2 * HH * (g + 1))
                if not (isinstance(n, int) and n < 2):
                    pe.wait_ge(shifted, n - 1)
                for c in range(2):
                    S = S_[k % 2][:, c * 512:(c + 1) * 512]
                    nc.tensor.matmul(S, qT[:, b, kk], kbd[:, r, b % 2, kk, 4 * c:4 * c + 4, :], start=True, stop=False)
                    mm = nc.tensor.matmul(S, identb[:], neg[:], start=False, stop=True)
                mm.then_inc(scores_ready, 1)

            def c_turn_p(g, k):
                n = 8 * g + k
                pe.wait_ge(exp_done, n + 1)
                pe.wait_ge(pT_ready, n)
                for h in range(HH):
                    mm = nc.tensor.transpose(PTP[:, h * P:(h + 1) * P], E_[:, k % 2, h], ident[:])
                mm.then_inc(p_turned, 1)

            def c_values(g, k):
                n = 8 * g + k
                r, b, kk = k // 4, k // 2, k % 2
                pe.wait_ge(pT_ready, n + 1)
                pe.wait_ge(va_loaded[r], 16 * (g + 1))
                if kk == 0:
                    pe.wait_ge(o_read, 1 + BG * g + b)
                for h in range(HH):
                    head = kk * HH + h
                    mm = nc.tensor.matmul(O_[:, head * VA:(head + 1) * VA], PT_[:, k % 2, h], va[:, r, b % 2, head],
                                          start=True, stop=True, skip_group_check=True)
                mm.then_inc(pv_done, 1)

            def c_turn_q(g, b):
                pe.wait_ge(vN_ready, BG * (2 * G + g) + b + 1)
                pe.wait_ge(qT_ready, BG * g + b)
                for k in range(DT):
                    mm = nc.tensor.transpose(TQ[:, k * P:(k + 1) * P], qn[:, b, k * P:(k + 1) * P], ident[:])
                mm.then_inc(qT_turned, 1)

            def c_steps(g, more):
                for k in range(8):
                    if k < 6 or more:
                        c_scores(g + (k + 2) // 8, (k + 2) % 8)
                    if k < 7 or more:
                        c_turn_p(g + (k + 1) // 8, (k + 1) % 8)
                    c_values(g, k)
                    if more and k in TURN_AT:
                        c_turn_q(g + 1, TURN_AT.index(k))

            def three(dst, pairs, start=True, stop=True, skip=False):
                prods = [(a[0], m[0]) for a, m in pairs] + [(a[1], m[0]) for a, m in pairs] + [
                    (a[0], m[1]) for a, m in pairs]
                for n, (a, m) in enumerate(prods):
                    mm = nc.tensor.matmul(dst, a, m, start=start and n == 0, stop=stop and n == len(prods) - 1,
                                          skip_group_check=skip)
                return mm

            def d_turn(g):
                pe.wait_ge(vN_ready, BG * (3 * G + g + 1))
                if g >= 2:
                    pe.wait_ge(xT_ready, G + g - 1)
                for k in range(DT):
                    for b in range(BG):
                        mm = nc.tensor.transpose(bank[g % 2][:, (k * BG + b) * P:(k * BG + b + 1) * P],
                                                 dxn[:, g % 2, b, k * P:(k + 1) * P], ident[:])
                mm.then_inc(xturned, 1)

            def d_router(g):
                pe.wait_ge(xT_ready, G + g + 1)
                for b in range(BG):
                    t = g * BG + b
                    for k in range(DT):
                        mm = nc.tensor.matmul(bank[2][:, t * E:(t + 1) * E], dxT[:, g, k, b * P:(b + 1) * P],
                                              gw_sb[:, k], start=(k == 0), stop=(k == DT - 1), skip_group_check=True)
                mm.then_inc(d_logits, 1)

            def d_masks(g):
                for r in range(2):
                    pe.wait_ge(hot_ready[r], 1)
                    if r == 0 and g >= 2:
                        pe.wait_ge(dM_ready, 2 * (g - 1))
                    for b in range(BG):
                        mm = nc.tensor.matmul(bank[g % 2][:, (r * BG + b) * P:(r * BG + b + 1) * P],
                                              dhot[:, r, g * BG + b], identb[:], start=True, stop=True,
                                              skip_group_check=True)
                mm.then_inc(dM_turned, 1)

            def d_weights(g):
                if g >= 2:
                    pe.wait_ge(dcb_ready, g - 1)
                for r in range(2):
                    for b in range(BG):
                        q = r * B + g * BG + b
                        mm = nc.tensor.matmul(bank[3 - g % 2][:, (r * BG + b) * P:(r * BG + b + 1) * P],
                                              dctok[:, q:q + 1].to_broadcast([P, P]), ident[:], start=True, stop=True,
                                              skip_group_check=True)
                mm.then_inc(dcb_turned, 1)

            def d_choose():
                d_turn(0)
                for g in range(G):
                    if g < G - 1:
                        d_turn(g + 1)
                    d_router(g)
                pe.wait_ge(tops_ready, 1)
                nc.tensor.transpose(bank[2][0:2 * B, 512:512 + P], dtop, ident[:]).then_inc(tops_turned, 1)
                d_masks(0)
                d_masks(1)
                pe.wait_ge(cexp_ready, 2)
                nc.tensor.matmul(bank[2][:, 512 + P:512 + P + 2 * B], cT, ident[0:2 * B, 0:2 * B], start=True,
                                 stop=True, skip_group_check=True).then_inc(c_back, 1)
                d_masks(2)
                d_masks(3)
                pe.wait_ge(ctok_ready, 1)
                for g in range(G):
                    d_weights(g)

            def d_adapters_in(g):
                pe.wait_ge(xL_ready, 2 * (G + g + 1))
                for r, dst in enumerate((U_[0], G_[0])):
                    a = [((w1H[:, r * D + k * P:r * D + (k + 1) * P], w1L[:, r * D + k * P:r * D + (k + 1) * P]),
                          (xH[:, k], xL[:, k])) for k in range(DT)]
                    three(dst, a).then_inc(z_psum, 1)

            def d_base(g, j):
                pr = TAIL if j == SJ - 1 else P
                if j >= 2:
                    pe.wait_ge(dsilu_ready, NE * g + at_ev[j - 2, 1] + 1)
                else:
                    pe.wait_ge(zm_ready, 4 * (g + 1))
                if j == 0:
                    pe.wait_ge(zL_ready, 4 * g + 2)
                for at, dst, zr_ in ((0, U_[j % 2], 0), (2 * P, G_[j % 2], 2)):
                    if j >= 2 and zr_ == 2:
                        pe.wait_ge(dscaled_ready, NE * g + at_ev[j - 2, 1] + 1)
                    a = [(tuple(w[:, 0:pr] for w in w1_tile(j, at + k * P, P)), (xH[:, k], xL[:, k]))
                         for k in range(DT)]
                    lora = tuple(w[:, 0:pr] for w in w1_tile(j, 4 * P + at // 2, P))
                    mm = three(dst[0:pr], a + [(lora, (dzH[:, zr_], dzL[:, zr_]))], skip=True)
                mm.then_inc(ev_ready, 1)

            def d_delta(g, j):
                pr = TAIL if j == SJ - 1 else P
                if j == 0:
                    pe.wait_ge(zL_ready, 4 * (g + 1))
                pe.wait_ge(dsilu_ready, NE * g + at_ev[j, 0] + 1)
                pe.wait_ge(dscaled_ready, NE * g + at_ev[j, 0] + 1)
                for at, dst, zr_ in ((0, U_[j % 2], 1), (P, G_[j % 2], 3)):
                    lora = tuple(w[:, 0:pr] for w in w1_tile(j, 4 * P + at, P))
                    mm = three(dst[0:pr], [(lora, (dzH[:, zr_], dzL[:, zr_]))], start=False, skip=True)
                mm.then_inc(ev_ready, 1)

            def d_down(g, j):
                pr = TAIL if j == SJ - 1 else P
                pe.wait_ge(cL_ready, SJ * g + j + 1)
                pe.wait_ge(sL_ready, SJ * g + j + 1)
                if j == 0:
                    pe.wait_ge(w_mixed, 1 + 4 * g)
                    pe.wait_ge(d_done, 1 + 2 * g)
                wd = tuple(w[0:pr] for w in w1_tile(j, 6 * P, D))
                wa = tuple(w[0:pr] for w in w1_tile(j, 6 * P + D, P))
                ends = dict(start=(j == 0), stop=(j == SJ - 1), skip=True)
                three(bank[2][:, 0:512], [(wa, (dsH[0:pr, j % 2], dsL[0:pr, j % 2]))], **ends)
                three(bank[2][:, 512:1024], [(wa, (dcH[0:pr, j % 2], dcL[0:pr, j % 2]))], **ends)
                for b in range(BG):
                    tok = slice(b * P, (b + 1) * P)
                    mm = three(DN[:, b * D:(b + 1) * D], [((dsH[0:pr, j % 2, tok], dsL[0:pr, j % 2, tok]), wd)],
                               start=(j == 0 and b % 2 == 0), stop=False, skip=True)
                mm.then_inc(ddown_done, 1)

            def d_adapt(g):
                pe.wait_ge(wsL_ready, g + 1)
                wb = (w1H[:, 2 * D:3 * D], w1L[:, 2 * D:3 * D])
                for b in range(BG):
                    tok = slice(b * P, (b + 1) * P)
                    mm = three(DN[:, b * D:(b + 1) * D], [((dwH[:, tok], dwL[:, tok]), wb)], start=False, skip=True)
                mm.then_inc(dn_ready, 1)

            def d_tiles(g, more):
                for j in range(1, SJ):
                    d_base(g, j)
                    d_delta(g, j - 1)
                    if j >= 2:
                        d_down(g, j - 2)
                d_delta(g, SJ - 1)
                if more:
                    pe.wait_ge(dsilu_ready, NE * g + at_ev[SJ - 2, 1] + 1)
                    pe.wait_ge(dscaled_ready, NE * g + at_ev[SJ - 2, 1] + 1)
                    d_adapters_in(g + 1)
                d_down(g, SJ - 2)
                d_down(g, SJ - 1)
                if more:
                    d_base(g + 1, 0)
                d_adapt(g)

            for h in range(2, NH0):
                a_conv(G - 1, h)
                if PHASES > 1:
                    if h == 9:
                        b_turn(0)
                    if h == 11:
                        b_logits(0)
            a_sum(G - 1)
            if PHASES > 1:
                b_spread(0)
            if PHASES > 1:
                pe.wait_ge(wL_ready, J0)
                b_gate_up(0, 0)
                with pe.Fori(0, G - 1) as g:
                    b_tiles(g, True)
                b_tiles(G - 1, False)
            if PHASES > 2:
                pe.wait_ge(b_done, 1 + 2 * G)
                c_scores(0, 0)
                c_scores(0, 1)
                c_turn_p(0, 0)
                with pe.Fori(0, G - 1) as g:
                    c_steps(g, True)
                c_steps(G - 1, False)
            if PHASES > 3:
                pe.wait_ge(c_done, B)
                pe.wait_ge(w1L_ready, W1K)
                d_choose()
                pe.wait_ge(dM_ready, 2 * G)
                d_adapters_in(0)
                d_base(0, 0)
                with pe.Fori(0, G - 1) as g:
                    d_tiles(g, True)
                d_tiles(G - 1, False)


def kernel(**inputs):
    import numpy as np
    import concourse.bacc as bacc
    from concourse.bass_utils import run_bass_kernel_spmd

    a = {k: np.asarray(v) for k, v in inputs.items()}

    def halves(w):
        return w.reshape(DT, P, -1).transpose(1, 0, 2)

    def padded(w, n, axis):
        pad = [(0, 0)] * w.ndim
        pad[axis] = (0, n - w.shape[axis])
        return np.pad(w, pad)

    def expert_cols(w):
        w = w.transpose(1, 0, 2).reshape(D, P, EJ).transpose(0, 2, 1)
        return halves(w.reshape(D, -1)).reshape(P, DT, EJ, P)

    def plain_cols(w):
        return halves(padded(w, SJ * P, 1)).reshape(P, DT, SJ, P)

    def rows(w):
        return padded(w, SJ * P, 0).reshape(SJ, P, -1).transpose(1, 0, 2)

    gate0 = np.concatenate([expert_cols(a["L0_ffn_Wg"]), plain_cols(a["L0_ffn_Sg"])], 2)
    up0 = np.concatenate([expert_cols(a["L0_ffn_Wu"]), plain_cols(a["L0_ffn_Su"])], 2)
    down0 = np.concatenate([a["L0_ffn_Wd"].reshape(P, EJ, D), rows(a["L0_ffn_Sd"])], 1)
    tiles = lambda w: w.transpose(2, 0, 1, 3).reshape(w.shape[2], P, -1)
    w0 = np.concatenate([tiles(gate0), tiles(up0), down0.transpose(1, 0, 2)], 2)
    wr = halves(padded(np.concatenate([a["L0_ffn_Wr"], a["L0_ffn_Wsg"]], 1), NR, 1)).reshape(P, -1)
    er_rows = lambda w: w.reshape(P, -1)
    up1, gate1 = plain_cols(a["L1_ffn_w_up"].T), plain_cols(a["L1_ffn_w_gate"].T)
    b_up = padded(er_rows(a["L1_ffn_up_B"].transpose(0, 2, 1)), SJ * P, 1).reshape(P, SJ, P).transpose(1, 0, 2)
    b_gate = padded(er_rows(a["L1_ffn_gate_B"].transpose(0, 2, 1)), SJ * P, 1).reshape(P, SJ, P).transpose(1, 0, 2)
    down1 = rows(a["L1_ffn_w_down"].T).transpose(1, 0, 2)
    a_down = rows(er_rows(a["L1_ffn_down_A"]).T).transpose(1, 0, 2)
    w1_tiles = np.concatenate([tiles(up1), tiles(gate1), b_up, b_gate, down1, a_down], 2)
    ab = np.concatenate([halves(er_rows(a["L1_ffn_up_A"]).T).reshape(P, -1),
                         halves(er_rows(a["L1_ffn_gate_A"]).T).reshape(P, -1),
                         er_rows(a["L1_ffn_down_B"].transpose(0, 2, 1))], 1)
    w1 = np.concatenate([ab, w1_tiles.transpose(1, 0, 2).reshape(P, -1)], 1).reshape(P, W1K, W1C).transpose(1, 0, 2)
    ctx_one = np.concatenate([a["ctx_2048"].reshape(B, P, HEADS, HD), np.ones((B, P, HEADS, 1), np.float32)], 3)
    gw = halves(a["L1_ffn_gate_w"].T).reshape(P, -1)
    filt = np.lib.stride_tricks.sliding_window_view(np.pad(a["L0_xattn_k"], ((0, 0), (P, 0))), 2 * P, 1)
    filt = filt[:, P:0:-1].transpose(1, 0, 2)
    ctx_t = a["ctx_2048"].reshape(G, BG, P, DT, P).transpose(0, 4, 3, 1, 2).reshape(G, P, DT * BG, P)
    ctx_half = ctx_t.reshape(G, P, DT * BG, 2, P // 2).transpose(0, 3, 1, 2, 4)
    arrays = {
        "x": a["x"], "ctx_nat": a["ctx_2048"], "ctx_half": ctx_half,
        "ctx_t": ctx_t, "ctx_one": ctx_one, "filt": filt, "bias": a["fside_S2_0"],
        "gates": np.concatenate([a["g_xattn"], a["g_ffn"]]), "w0": w0, "wr": wr, "w1": w1, "gw": gw,
        "ramp": np.arange(E, 0, -1).astype(np.float32),
    }
    arrays = {k: np.ascontiguousarray(v) for k, v in arrays.items()}
    nc = bacc.Bacc("TRN2", target_bir_lowering=False, num_devices=1)
    args = [nc.dram_tensor("in_" + k, v.shape, mybir.dt.from_np(v.dtype), kind="ExternalInput").ap() for k, v in arrays.items()]
    out = nc.dram_tensor("out", (B, P, D), F32, kind="ExternalOutput").ap()
    flamingo_kernel(nc, *args, out)
    r = run_bass_kernel_spmd(nc, [{"in_" + k: v for k, v in arrays.items()}], core_ids=[0])
    return r.results[0]["out"]
```

```python
from contextlib import ExitStack

import concourse.bass as bass
from concourse import mybir

F32 = mybir.dt.float32
F32R = mybir.dt.float32r
BF16 = mybir.dt.bfloat16
I32 = mybir.dt.int32
ALU = mybir.AluOpType
ACT = mybir.ActivationFunctionType
AX_X = mybir.AxisListType.X

P = 128
B = 16
D = 256
DT = D // P
G = 4
BG = B // G
NT = BG * P
NH0, I0 = 16, 8
HALF, QUARTER = I0 // 2, I0 // 4
E = 8
RANK = 16
F0, FS = 176, 704
EJ = E * F0 // P
SJ = -(-FS // P)
TAIL = FS - (SJ - 1) * P
J0 = EJ + SJ
W0T = 4 * P + D
W1T = 4 * P + 2 * P + D + P
W1X = 4 * P + D
W1N = W1X + SJ * W1T
W1K = 8
W1C = W1N // W1K
NR = E + 2
HEADS, HD = 16, 16
HH = P // HD
VA = HD + 1
OS = 32
EPS = 1e-5
MASKED = -10000.0
FAR = -1e30
LORA_ALPHA = 2.0
NEWTONS = 3
RSQRT_GUESS = 0x5F3759DF
NORM_A = 4
LEAD = 3
TURN_A, BIAS_A = 6, 8
TOEP_H = 4
TURN_AT = (4, 5, 6, 7)


class Count:

    def __init__(self, sem):
        self.sem, self.base, self.n = sem, 0, 0

    def mark(self, ins):
        ins.then_inc(self.sem, 1)
        self.n += 1

    def value(self):
        return self.base + self.n

    def enter(self, g, per, start):
        self.base, self.n = g * per + start, 0

    def leave(self, per, rounds, start):
        assert self.n == per, (self.n, per)
        self.base, self.n = start + per * rounds, 0


class Steps:

    def __init__(self, write=None, count=0):
        self.write, self.count, self.at = write, count, 0

    def take(self, n):
        for i in range(self.at, min(self.at + n, self.count)):
            self.write(i)
        self.at = min(self.at + n, self.count)

    def take_all(self):
        self.take(self.count)

    def left(self):
        return self.at < self.count


def flamingo_kernel(nc, x, ctx_nat, ctx_half, ctx_t, ctx_one, filt, bias, gates, w0, wr, w1, gw, ramp_in, out):
    es = ExitStack()
    with es:
        sb = lambda name, shape, dt=F32: es.enter_context(nc.sbuf_tensor(name, shape, dt))
        sem = lambda name: es.enter_context(nc.semaphore(name))
        bank = [es.enter_context(nc.psum_tensor(f"bank{i}", [P, 1024], F32)) for i in range(4)]

        X = sb("X", [P, B, D])
        ident = sb("ident", [P, P])
        identb = sb("identb", [P, P], BF16)
        ones_blk = sb("ones_blk", [P, NH0, I0])
        neg = sb("neg", [P, 4, P], BF16)
        bias_c = sb("bias_c", [P, 1])
        gate_in = sb("gate_in", [P, 4])
        gate = sb("gate", [P, 4])
        ramp = sb("ramp", [P, E])
        wr_sb = sb("wr_sb", [P, DT, NR])
        gw_sb = sb("gw_sb", [P, DT, E])
        st = sb("st", [P, BG, 6])
        mv = sb("mv", [P, BG, 2])
        ve = sb("ve", [P, BG])
        scrap = sb("scrap", [P, 1])
        tmp = sb("tmp", [P, BG])
        rs = sb("rs", [P, BG])
        nb = sb("nb", [P, BG])
        small = sb("small", [P, 384])
        A1 = sb("A1", [P, 17792])
        R1 = sb("R1", [P, 2 * J0 * W0T + 4 * NT + 4 * NT], F32R)

        def carve(t, sizes):
            views, at = [], 0
            for n in sizes:
                views.append(t[:, at:at + n])
                at += n
            return views

        (toep, ctxN, ctxT, vN, vT, kv_, zr_, z4, stg_) = carve(
            A1, [NH0 * 2 * P, BG * D, BG * D, BG * D, BG * D, 1024, 1024, 8 * HALF * P, 2 * W0T])
        toep = toep.rearrange("p (h c) -> p h c", h=NH0)
        ctxN = ctxN.rearrange("p (b d) -> p b d", b=BG)
        vN = vN.rearrange("p (b d) -> p b d", b=BG)
        ctxT = ctxT.rearrange("p (s q t) -> p s q t", s=2, q=8)
        vT = vT.rearrange("p (q t) -> p q t", t=P)
        kv = kv_.rearrange("p (u q i j) -> p u q i j", u=2, q=8, i=I0)
        zr = zr_.rearrange("p (u q i j) -> p u q i j", u=2, q=8, i=I0)
        zh = z4[:, 0:2 * 8 * HALF * I0].rearrange("p (u q i j) -> p u q i j", u=2, q=8, i=HALF)
        z2 = z4[:, 8 * QUARTER * P:].rearrange("p (q i t) -> p q i t", q=8, i=QUARTER)
        stg = stg_.rearrange("p (u n) -> p u n", u=2)
        yb = [bank[0][:, 0:512], bank[0][:, 512:1024]]
        TV, WB, OB = bank[1], bank[2], bank[3]

        nW0 = J0 * W0T
        w0H = R1[:, 0:nW0].rearrange("p (j n) -> p j n", j=J0)
        w0L = R1[:, nW0:2 * nW0].rearrange("p (j n) -> p j n", j=J0)
        r_at = 2 * nW0
        xH = R1[:, r_at:r_at + DT * NT].rearrange("p (k t) -> p k t", k=DT)
        xL = R1[:, r_at + 2 * NT:r_at + 4 * NT].rearrange("p (k t) -> p k t", k=DT)
        hH = R1[:, r_at + 4 * NT:r_at + 6 * NT].rearrange("p (u t) -> p u t", u=2)
        hL = R1[:, r_at + 6 * NT:r_at + 8 * NT].rearrange("p (u t) -> p u t", u=2)

        xn, xT = (A1[:, at:at + BG * D] for at in (NH0 * 2 * P, NH0 * 2 * P + 2 * BG * D))
        xn = xn.rearrange("p (b d) -> p b d", b=BG)
        spread = A1[:, NH0 * 2 * P:NH0 * 2 * P + 2 * NT].rearrange("p (r b t) -> p r b t", r=2, b=BG)
        xT = xT.rearrange("p (k t) -> p k t", k=DT)
        b_silu, b_scaled = (A1[:, i * 2 * NT:(i + 1) * 2 * NT].rearrange("p (u t) -> p u t", u=2) for i in range(2))
        b_h, b_comb = (A1[:, i * 2 * NT:(i + 1) * 2 * NT].rearrange("p (u t) -> p u t", u=2) for i in (2, 3))
        G_, U_ = [bank[0][:, 0:512], bank[1][:, 0:512]], [bank[0][:, 512:1024], bank[1][:, 512:1024]]
        TP, DN = bank[2], bank[3]
        (lg, es_, eq, rk, oh1, oh2, l2) = carve(small, [BG * NR, BG * (E + 1), BG * E, BG * E, BG * E, BG * E, BG * E])
        m1, m2, den, rcp = carve(small[:, 40 + 36 + 160:], [BG, BG, 2 * BG, 2 * BG])
        lg = lg.rearrange("p (b e) -> p b e", b=BG)
        es_ = es_.rearrange("p (b e) -> p b e", b=BG)
        eq, rk, oh1, oh2, l2 = (v.rearrange("p (b e) -> p b e", b=BG) for v in (eq, rk, oh1, oh2, l2))

        E_, PT_ = (A1[:, i * 2048:(i + 1) * 2048].rearrange("p (u h k) -> p u h k", u=2, h=HH) for i in range(2))
        qT = A1[:, 4096:5120].rearrange("p (b k t) -> p b k t", b=BG, k=DT)
        qn = A1[:, 5120:6144].rearrange("p (b d) -> p b d", b=BG)
        kbd_ = A1[:, 7168:15360]
        kbd = kbd_.rearrange("p (r b k h t) -> p r b k h t", r=2, b=2, k=DT, h=HH)
        va = A1[:, 15360:15360 + BG * HEADS * VA].rearrange("p (r b h e) -> p r b h e", r=2, b=2, h=HEADS)
        stg1 = [A1[:, 6144:6144 + W1C], A1[:, 16448:16448 + W1C]]
        otmp = A1[:, 16448 + W1C:16448 + W1C + D].rearrange("p (h e) -> p h e", h=HEADS)
        (mx_, r16, ot_) = carve(small, [2 * HH, HEADS, 2 * P])
        ot = ot_.rearrange("p (c q) -> p c q", c=2)
        mx = mx_.rearrange("p (u h) -> p u h", u=2)
        (cst_, cmv_) = carve(A1[:, 16448 + W1C:], [B * 6, B * 2])
        cst, cmv = (v.rearrange("p (b s) -> p b s", b=B) for v in (cst_, cmv_))
        (cvar, ctmp, crs, cnb) = carve(A1[:, 16448 + W1C + D:], [B] * 4)
        S_, PTP, O_, OT, TQ = bank[0:2], bank[2], bank[3][:, 0:HEADS * OS], bank[3][:, 512:768], bank[3][:, 768:1024]
        w1H, w1L = R1[:, 0:W1N], R1[:, W1N:2 * W1N]

        (dsilu_, dcb_, dxT_, dM2_, dscaled_, dc1_, dc2_, dw_) = carve(
            A1, [2 * NT, G * 2 * NT, G * DT * NT, G * NT, 2 * NT, 2 * NT, 2 * NT, 3 * NT])
        dxT = dxT_.rearrange("p (g k t) -> p g k t", g=G, k=DT)
        dcb = dcb_.rearrange("p (g r t) -> p g r t", g=G, r=2)
        dM1 = R1[:, r_at + 4 * NT:r_at + 8 * NT].rearrange("p (g t) -> p g t", g=G)
        dM2 = dM2_.rearrange("p (g t) -> p g t", g=G)
        dMD = R1[:, 2 * W1N + 18 * NT:2 * W1N + 19 * NT]
        d_tmp = A1[:, 22 * NT:26 * NT]
        dxn = d_tmp.rearrange("p (u b d) -> p u b d", u=2, b=BG)
        dhot = d_tmp.bitcast(BF16).rearrange("p (r b t) -> p r b t", r=2, b=B)
        dsilu, dscaled, dc1, dc2 = (v.rearrange("p (u t) -> p u t", u=2) for v in (dsilu_, dscaled_, dc1_, dc2_))
        (dst_, dmv_, dvar, dtmp, drs, dnb) = carve(dM2_, [B * 6, B * 2, B, B, B, B])
        (dlg_, deq_, dl2_, do1_, do2_, drk, dtop, dctok, cT_) = carve(
            A1[:, 31 * NT:], [B * E, B * E, B * E, B * E, B * E, B, 2 * B, 2 * B, P])
        dstat = dst_.rearrange("p (b s) -> p b s", b=B)
        dmv = dmv_.rearrange("p (b s) -> p b s", b=B)
        dlg, deq, dl2, do1, do2 = (v.rearrange("p (b e) -> p b e", b=B) for v in (dlg_, deq_, dl2_, do1_, do2_))
        cT = cT_[0:2 * B, :]
        d_at = 2 * W1N
        dzH = R1[:, d_at:d_at + 4 * NT].rearrange("p (r t) -> p r t", r=4)
        dzL = R1[:, d_at + 4 * NT:d_at + 8 * NT].rearrange("p (r t) -> p r t", r=4)
        dsH, dsL, dcH, dcL = (R1[:, d_at + i * NT:d_at + (i + 2) * NT].rearrange("p (u t) -> p u t", u=2)
                              for i in (8, 10, 12, 14))
        dwH, dwL = R1[:, d_at + 16 * NT:d_at + 17 * NT], R1[:, d_at + 17 * NT:d_at + 18 * NT]
        dw = dw_.rearrange("p (r t) -> p r t", r=3)
        dz = [dw[:, 0], dw[:, 1], dw[:, 2], dc1[:, 0]]
        assert d_at + 19 * NT <= r_at
        mneg, mtop, msum, mrcp = (small[0:2 * B, 300 + i:301 + i] for i in range(4))

        def w1_tile(j, at, n):
            a0 = W1X + j * W1T + at
            return w1H[:, a0:a0 + n], w1L[:, a0:a0 + n]

        EV = [(0, 0)]
        for j in range(1, SJ):
            EV += [(j, 0), (j - 1, 1)]
        EV.append((SJ - 1, 1))
        NE = len(EV)
        Z_ORDER = (0, 2, 1, 3)
        at_ev = {ev: i for i, ev in enumerate(EV)}

        consts_ready = sem("consts_ready")
        x0_loaded, x1_loaded, xrest_loaded = sem("x0_loaded"), sem("x1_loaded"), sem("xrest_loaded")
        gates_loaded, small_loaded = sem("gates_loaded"), sem("small_loaded")
        toep_loaded = [sem("toep_loaded0"), sem("toep_loaded1")]
        ctxN_loaded = sem("ctxN_loaded")
        ctxT_loaded = [sem("ctxT_loaded0"), sem("ctxT_loaded1")]
        stg_loaded = [sem("stg_loaded0"), sem("stg_loaded1")]
        wH_ready, wL_ready = sem("wH_ready"), sem("wL_ready")
        gate_ready = sem("gate_ready")
        dve_step = sem("dve_step")
        ln_ready, vN_ready = sem("ln_ready"), sem("vN_ready")
        vtp_ready, vT_ready, bvx_ready, w_ready, t_done = (
            sem("vtp_ready"), sem("vT_ready"), sem("bvx_ready"), sem("w_ready"), sem("t_done"))
        zh_ready = sem("zh_ready")
        kv_ready, y_ready, z_ready, z2_ready, o_ready, a_done = (
            sem("kv_ready"), sem("y_ready"), sem("z_ready"), sem("z2_ready"), sem("o_ready"), sem("a_done"))
        xturned, xT_ready, xH_ready, xL_ready = sem("xturned"), sem("xT_ready"), sem("xH_ready"), sem("xL_ready")
        logits_ready, expin_ready, exp_ready, spread_ready, spread_turned, comb_ready = (
            sem("logits_ready"), sem("expin_ready"), sem("exp_ready"), sem("spread_ready"), sem("spread_turned"),
            sem("comb_ready"))
        gu_ready, silu_ready, scaled_ready, h_ready, hH_ready, hL_ready, down_done, b_done = (
            sem("gu_ready"), sem("silu_ready"), sem("scaled_ready"), sem("h_ready"), sem("hH_ready"), sem("hL_ready"),
            sem("down_done"), sem("b_done"))
        kbd_zeroed, qT_turned, qT_ready = sem("kbd_zeroed"), sem("qT_turned"), sem("qT_ready")
        kbd_loaded = [sem("kbd_loaded0"), sem("kbd_loaded1")]
        va_loaded = [sem("va_loaded0"), sem("va_loaded1")]
        stg1_loaded = [sem("stg1_loaded0"), sem("stg1_loaded1")]
        w1H_ready, w1L_ready = sem("w1H_ready"), sem("w1L_ready")
        ot_zeroed, ot_taken, o_turned = sem("ot_zeroed"), sem("ot_taken"), sem("o_turned")
        scores_ready, shifted, exp_done, p_turned, pT_ready, pv_done, o_read, c_done = (
            sem("scores_ready"), sem("shifted"), sem("exp_done"), sem("p_turned"), sem("pT_ready"), sem("pv_done"),
            sem("o_read"), sem("c_done"))
        d_logits, tops_ready, tops_turned, topmax_ready, cexp_ready, c_ready, c_back, ctok_ready = (
            sem("d_logits"), sem("tops_ready"), sem("tops_turned"), sem("topmax_ready"), sem("cexp_ready"),
            sem("c_ready"), sem("c_back"), sem("ctok_ready"))
        hot_ready = [sem("hot_ready0"), sem("hot_ready1")]
        dM_turned, dM_ready, dMD_ready = sem("dM_turned"), sem("dM_ready"), sem("dMD_ready")
        dcb_turned, dcb_ready = sem("dcb_turned"), [sem("dcb_ready0"), sem("dcb_ready1")]
        z_psum, zm_ready, zH_ready, zL_ready = sem("z_psum"), sem("zm_ready"), sem("zH_ready"), sem("zL_ready")
        ev_ready, dsilu_ready, dscaled_ready, ch_ready, sum_ready = (
            sem("ev_ready"), sem("dsilu_ready"), sem("dscaled_ready"), sem("ch_ready"), sem("sum_ready"))
        cH_ready, cL_ready, sH_ready, sL_ready, ddown_done = (
            sem("cH_ready"), sem("cL_ready"), sem("sH_ready"), sem("sL_ready"), sem("ddown_done"))
        w_mixed, w_sum, wsH_ready, wsL_ready, dn_ready, d_done = (
            sem("w_mixed"), sem("w_sum"), sem("wsH_ready"), sem("wsL_ready"), sem("dn_ready"), sem("d_done"))
        out_stored = sem("out_stored")

        block = es.enter_context(nc.Block())
        SPLIT_AT = (5, 10, 15)
        CH = 4

        @block.sync
        def _(sp):
            sp.dma_start(X[:, 0:BG, :], x[0:BG].rearrange("b p d -> p b d")).then_inc(x0_loaded, 16)
            sp.dma_start(gate_in[:], gates.partition_broadcast(P)).then_inc(gates_loaded, 16)
            sp.dma_start(bias_c[:], bias.rearrange("(p a) -> p a", a=1)).then_inc(gates_loaded, 16)
            for s in range(2):
                sp.dma_start(ctxT[:, s], ctx_half[0, s]).then_inc(ctxT_loaded[s], 16)
            sp.dma_start(X[:, BG:2 * BG, :], x[BG:2 * BG].rearrange("b p d -> p b d")).then_inc(x1_loaded, 16)
            sp.dma_start(toep[:, 0:TOEP_H], filt[:, 0:TOEP_H]).then_inc(toep_loaded[0], 16)
            sp.dma_start(ctxN, ctx_nat[0:BG].rearrange("b p d -> p b d")).then_inc(ctxN_loaded, 16)
            sp.dma_start(toep[:, TOEP_H:], filt[:, TOEP_H:]).then_inc(toep_loaded[1], 16)
            sp.dma_start(X[:, 2 * BG:B, :], x[2 * BG:B].rearrange("b p d -> p b d")).then_inc(xrest_loaded, 16)
            sp.dma_start(ramp[:], ramp_in.partition_broadcast(P)).then_inc(small_loaded, 16)
            sp.dma_start(wr_sb[:], wr.rearrange("p (k n) -> p k n", k=DT)).then_inc(small_loaded, 16)
            sp.dma_start(gw_sb[:], gw.rearrange("p (k n) -> p k n", k=DT)).then_inc(small_loaded, 16)

            def weights(c, first=False):
                u = c[1] % 2
                n = c[0] * CH + c[1]
                if not first:
                    sp.wait_ge(wL_ready, n - 1)
                sp.dma_start(stg[:, u, :], w0[n]).then_inc(stg_loaded[u], 16)

            weights((0, 0), True)
            weights((0, 1), True)

            def loads(g, n_chunks, more):
                if more:
                    sp.wait_ge(t_done, g + 1)
                    sp.dma_start(ctxN, ctx_nat[bass.ds((g + 1) * BG, BG)].rearrange("b p d -> p b d")
                                 ).then_inc(ctxN_loaded, 16)
                for c in range(n_chunks):
                    weights((g, c + 2))
                    if more and c % 2:
                        s = c // 2
                        sp.wait_ge(z_ready, 1 + NH0 * g + NH0 // 2 * (s + 1))
                        sp.dma_start(ctxT[:, s], ctx_half[bass.ds(g + 1, 1), s].rearrange("a p q t -> (a p) q t")
                                     ).then_inc(ctxT_loaded[s], 16)
            with sp.Fori(0, G - 1) as g:
                loads(g, CH, True)
            loads(G - 1, J0 - CH * (G - 1) - 2, False)
            sp.wait_ge(a_done, 1 + 2 * G)

            def keys(g, r):
                src = ctx_t[bass.ds(g, 1)].rearrange("a p (k b) t -> (a p) b k t", k=DT)
                for h in range(HH):
                    for b in range(2):
                        sp.dma_start(kbd[h * HD:(h + 1) * HD, r, b, :, h, :],
                                     src[h * HD:(h + 1) * HD, 2 * r + b, :, :]).then_inc(kbd_loaded[r], 16)

            def values(g, r):
                sp.dma_start(va[:, r], ctx_one[bass.ds(g * BG + 2 * r, 2)].rearrange("b p h e -> p b h e")
                             ).then_inc(va_loaded[r], 16)

            def weights1(g, r):
                if not isinstance(g, int) or g > 0:
                    sp.wait_ge(w1L_ready, 2 * g + r - 1)
                sp.dma_start(stg1[r], w1[bass.ds(2 * g + r, 1)].rearrange("a p n -> (a p) n")
                             ).then_inc(stg1_loaded[r], 16)

            sp.wait_ge(kbd_zeroed, J0 - 1)
            for r in range(2):
                keys(0, r)
                values(0, r)
            sp.wait_ge(b_done, 1 + 2 * G)
            for r in range(2):
                weights1(0, r)
            with sp.Fori(0, G - 1) as g:
                for r in range(2):
                    sp.wait_ge(scores_ready, 8 * g + 4 * r + 4)
                    keys(g + 1, r)
                    weights1(g + 1, r)
                    sp.wait_ge(pv_done, 1 + 8 * g + 4 * r + 4)
                    values(g + 1, r)
            sp.wait_ge(c_done, B)
            with sp.Fori(0, G) as g:
                sp.wait_ge(d_done, 1 + 2 * (g + 1))
                sp.dma_start(out[bass.ds(g * BG, BG)].rearrange("b p d -> p b d"), X[:, bass.ds(g * BG, BG), :]
                             ).then_inc(out_stored, 16)
            sp.wait_ge(out_stored, 16 * G)

        @block.gpsimd
        def _(pool):
            for counted in (y_ready, z_ready, zh_ready, z2_ready, o_ready, a_done, h_ready, down_done, b_done,
                            o_read, pv_done, ch_ready, ddown_done, w_mixed, dn_ready, d_done):
                pool.sem_inc(counted, 1)
            c = Count(consts_ready)
            c.mark(nc.gpsimd.memset(ident[:], 0.0))
            c.mark(nc.gpsimd.memset(ones_blk[:], 1.0))
            c.mark(nc.gpsimd.memset(neg[:], 0.0))
            pool.wait_ge(consts_ready, 3)
            c.mark(nc.gpsimd.affine_select(out=ident[:], in_=ident[:], compare_op=ALU.not_equal, fill=1.0, base=0,
                                           pattern=[[-1, P]], channel_multiplier=1))
            c.mark(nc.gpsimd.affine_select(out=ones_blk[:], in_=ones_blk[:], compare_op=ALU.is_ge, fill=0.0, base=0,
                                           pattern=[[-I0, NH0], [0, I0]], channel_multiplier=1))
            c.mark(nc.gpsimd.affine_select(out=neg[:], in_=neg[:], compare_op=ALU.is_ge, fill=FAR, base=0,
                                           pattern=[[0, 4], [-1, P]], channel_multiplier=1))
            pool.wait_ge(consts_ready, 6)
            c.mark(nc.gpsimd.affine_select(out=ones_blk[:], in_=ones_blk[:], compare_op=ALU.is_ge, fill=0.0,
                                           base=I0 - 1, pattern=[[I0, NH0], [0, I0]], channel_multiplier=-1))
            c.mark(nc.gpsimd.tensor_copy(identb[:], ident[:]))

            def split_low(g, c):
                n = g * CH + c
                pool.wait_ge(wH_ready, n + 1)
                nc.gpsimd.tensor_tensor(w0L[:, bass.ds(n, 1), :], stg[:, c % 2:c % 2 + 1, :],
                                        w0H[:, bass.ds(n, 1), :].bitcast(F32), ALU.subtract).then_inc(wL_ready, 1)

            def a_add(g, h):
                u = h % 2
                pool.wait_ge(z_ready, 1 + NH0 * g + h + 1)
                pool.wait_ge(z2_ready, 1 + NH0 * g + max(h - 1, 0))
                nc.gpsimd.tensor_tensor(zh[:, u], zr[:, u, :, 0:HALF, :], zr[:, u, :, HALF:, :], ALU.add
                                        ).then_inc(zh_ready, 1)
                pool.wait_ge(zh_ready, 1 + NH0 * g + h + 1)
                if h == 0:
                    pool.wait_ge(o_ready, 1 + 2 * g)
                nc.gpsimd.tensor_tensor(z2[:, :, :, h * I0:(h + 1) * I0], zh[:, u, :, 0:QUARTER, :],
                                        zh[:, u, :, QUARTER:, :], ALU.add).then_inc(z2_ready, 1)

            def a_adds(g):
                for c in range(CH - len(SPLIT_AT)):
                    split_low(g, c)
                for h in range(NH0):
                    a_add(g, h)
                    if h in SPLIT_AT:
                        split_low(g, CH - len(SPLIT_AT) + SPLIT_AT.index(h))
            with pool.Fori(0, G - 1) as g:
                a_adds(g)
            a_adds(G - 1)
            for c in range(CH, J0 - CH * (G - 1)):
                split_low(G - 1, c)

            pool.wait_ge(h_ready, 1 + J0 * (G - 1))
            for j in range(J0 - 1):
                nc.gpsimd.memset(kbd_[:, j * 512:(j + 1) * 512], 0.0).then_inc(kbd_zeroed, 1)

            def split_low1(g, r):
                n = 2 * g + r
                pool.wait_ge(w1H_ready, n + 1)
                dst = bass.ds(n * W1C, W1C)
                nc.gpsimd.tensor_tensor(w1L[:, dst], stg1[r], w1H[:, dst].bitcast(F32), ALU.subtract
                                        ).then_inc(w1L_ready, 1)
            with pool.Fori(0, G) as g:
                for r in range(2):
                    split_low1(g, r)

            def d_difference(g):
                nc.gpsimd.tensor_tensor(dMD, dM2[:, bass.ds(g, 1)], dM1[:, bass.ds(g, 1)].bitcast(F32),
                                        ALU.subtract).then_inc(dMD_ready, 1)
            pool.wait_ge(dM_ready, 2 * G)
            d_difference(0)
            with pool.Fori(0, G - 1) as g:
                pool.wait_ge(zm_ready, 4 * (g + 1))
                d_difference(g + 1)

        @block.scalar
        def _(act):
            act.wait_ge(gates_loaded, 32)
            nc.scalar.activation(gate[:], gate_in[:], ACT.Tanh).then_inc(gate_ready, 1)

            def normed(g, b, dst, phase):
                if b == 0:
                    act.wait_ge(ln_ready, G * phase + g + 1)
                nc.scalar.activation(dst[:, b:b + 1, :], X[:, bass.ds(g * BG + b, 1), :], ACT.Identity,
                                     bias=nb[:, b:b + 1], scale=rs[:, b:b + 1]).then_inc(vN_ready, 1)

            def a_prep(g, first=False):
                if not first:
                    act.wait_ge(t_done, g)
                for b in range(BG):
                    normed(g, b, vN, 0)

            def a_turned(g, first=False):
                act.wait_ge(vtp_ready, g + 1)
                if not first:
                    act.wait_ge(kv_ready, NH0 * g)
                for k in range(DT):
                    nc.scalar.activation(vT[:, k * BG:(k + 1) * BG, :], TV[:, k * NT:(k + 1) * NT], ACT.Copy
                                         ).then_inc(vT_ready, 1)

            def split_high(g, c):
                n = g * CH + c
                act.wait_ge(stg_loaded[c % 2], (g * (CH // 2) + c // 2 + 1) * 16)
                nc.scalar.activation(w0H[:, bass.ds(n, 1), :], stg[:, c % 2:c % 2 + 1, :], ACT.Copy
                                     ).then_inc(wH_ready, 1)

            a_prep(0, True)
            a_turned(0, True)
            with act.Fori(0, G - 1) as g:
                split_high(g, 0)
                split_high(g, 1)
                a_prep(g + 1)
                for c in range(2, CH):
                    split_high(g, c)
                a_turned(g + 1)

            def c_norm_one(g, b):
                if b == 0:
                    act.wait_ge(ln_ready, 2 * G + (1 if isinstance(g, int) and g == 0 else 2))
                t = bass.ds(g * BG + b, 1)
                nc.scalar.activation(qn[:, b:b + 1, :], X[:, t, :], ACT.Identity, bias=cnb[:, t], scale=crs[:, t]
                                     ).then_inc(vN_ready, 1)

            def b_norm(g, b):
                if b == 0:
                    if isinstance(g, int) and g == 0:
                        act.wait_ge(t_done, G)
                    else:
                        act.wait_ge(spread_turned, g)
                normed(g, b, xn, 1)

            def b_turned(g):
                act.wait_ge(xturned, g + 1)
                if not (isinstance(g, int) and g == 0):
                    act.wait_ge(xL_ready, 2 * g)
                nc.scalar.activation(xT, TP[:].rearrange("p (k t) -> p k t", k=DT), ACT.Copy).then_inc(xT_ready, 1)

            def b_exp(g):
                act.wait_ge(expin_ready, g + 1)
                nc.scalar.activation(es_, es_, ACT.Exp).then_inc(exp_ready, 1)

            def b_high_x(g):
                act.wait_ge(xT_ready, g + 1)
                for k in range(DT):
                    nc.scalar.activation(xH[:, k], xT[:, k], ACT.Copy).then_inc(xH_ready, 1)

            def b_take_comb(g):
                act.wait_ge(spread_turned, g + 1)
                nc.scalar.activation(b_comb, TP[:].rearrange("p (r t) -> p r t", r=2), ACT.Copy).then_inc(comb_ready, 1)

            def b_silu_of(g, j, first=False):
                pr = TAIL if j == J0 - 1 else P
                act.wait_ge(gu_ready, J0 * g + j + 1)
                if not first:
                    act.wait_ge(h_ready, 1 + J0 * g + j - 1)
                nc.scalar.activation(b_silu[0:pr, j % 2], G_[j % 2][0:pr], ACT.Silu).then_inc(silu_ready, 1)

            def b_high(g, j):
                pr = TAIL if j == J0 - 1 else P
                act.wait_ge(h_ready, 1 + J0 * g + j + 1)
                if j >= 2:
                    act.wait_ge(down_done, 1 + J0 * g + j - 1)
                else:
                    act.wait_ge(down_done, 1 + J0 * g)
                nc.scalar.activation(hH[0:pr, j % 2], b_h[0:pr, j % 2], ACT.Copy).then_inc(hH_ready, 1)

            def b_tiles(g, more):
                for j in range(1, J0):
                    b_silu_of(g, j)
                    b_high(g, j - 1)
                    if more and j == J0 - 1:
                        act.wait_ge(gu_ready, J0 * (g + 1))
                        b_high_x(g + 1)
                    if more and 6 <= j < 10:
                        b_norm(g + 1, j - 6)
                    if more and j == 11:
                        b_turned(g + 1)
                    if more and j == 14:
                        b_exp(g + 1)
                    if not more and 10 <= j < 14:
                        c_norm_one(0, j - 10)
                if more:
                    act.wait_ge(scaled_ready, J0 * (g + 1))
                    b_take_comb(g + 1)
                b_high(g, J0 - 1)
                if more:
                    b_silu_of(g + 1, 0)

            for c in range(J0 - CH * (G - 1)):
                split_high(G - 1, c)
                if c == 0:
                    for b in range(BG):
                        b_norm(0, b)
                if c == 1:
                    b_turned(0)
                if c == 3:
                    b_exp(0)
            act.wait_ge(a_done, 1 + 2 * G)
            b_high_x(0)
            b_take_comb(0)
            b_silu_of(0, 0, True)
            with act.Fori(0, G - 1) as g:
                b_tiles(g, True)
            b_tiles(G - 1, False)

            def c_high(g, r):
                n = 2 * g + r
                act.wait_ge(stg1_loaded[r], 16 * (g + 1))
                nc.scalar.activation(w1H[:, bass.ds(n * W1C, W1C)], stg1[r], ACT.Copy).then_inc(w1H_ready, 1)

            def c_exp(g, k):
                n = 8 * g + k
                act.wait_ge(shifted, n + 1)
                nc.scalar.activation(E_[:, k % 2], E_[:, k % 2], ACT.Exp).then_inc(exp_done, 1)

            def c_evac(g, k):
                n = 8 * g + k
                act.wait_ge(p_turned, n + 1)
                if isinstance(n, int) and n < 2:
                    pass
                else:
                    act.wait_ge(pv_done, 1 + n - 1)
                nc.scalar.activation(PT_[:, k % 2], PTP[:].rearrange("p (h k) -> p h k", h=HH), ACT.Copy
                                     ).then_inc(pT_ready, 1)

            def c_take_q(g, b):
                act.wait_ge(qT_turned, BG * g + b + 1)
                act.wait_ge(scores_ready, 8 * (g - 1) + 2 * b + 2)
                nc.scalar.activation(qT[:, b], TQ.rearrange("p (k t) -> p k t", k=DT), ACT.Copy).then_inc(qT_ready, 1)

            def c_take_ot(g, k):
                act.wait_ge(pv_done, 1 + 8 * g + k + 1)
                nc.scalar.activation(ot_, OT, ACT.Copy).then_inc(ot_taken, 1)

            def d_norm(g):
                if g == 0:
                    act.wait_ge(scores_ready, 8 * G)
                act.wait_ge(ln_ready, 2 * G + (3 if g < G - 1 else 4))
                if g >= 2:
                    act.wait_ge(xturned, G + g - 1)
                for b in range(BG):
                    t = g * BG + b
                    nc.scalar.activation(dxn[:, g % 2, b], X[:, t], ACT.Identity, bias=dnb[:, t:t + 1],
                                         scale=drs[:, t:t + 1]).then_inc(vN_ready, 1)

            def c_steps(g, more):
                for k in range(8):
                    if more and k in TURN_AT:
                        c_take_q(g + 1, TURN_AT.index(k))
                    if k < 7 or more:
                        c_evac(g + (k + 1) // 8, (k + 1) % 8)
                    c_take_ot(g, k)
                    if k < 6 or more:
                        c_exp(g + (k + 2) // 8, (k + 2) % 8)
                    if more and k < BG:
                        if k == 0:
                            act.wait_ge(qT_turned, BG * (g + 1))
                        c_norm_one(g + 1, k)
                    if k in (1, 5):
                        c_high(g, k // 4)
                if not more:
                    d_norm(0)
                    d_norm(1)

            act.wait_ge(qT_turned, BG)
            for b in range(BG):
                nc.scalar.activation(qT[:, b], bank[2][:, b * D:(b + 1) * D].rearrange("p (k t) -> p k t", k=DT),
                                     ACT.Copy).then_inc(qT_ready, 1)
            c_exp(0, 0)
            c_exp(0, 1)
            c_evac(0, 0)
            with act.Fori(0, G - 1) as g:
                c_steps(g, True)
            c_steps(G - 1, False)

            def d_choose():
                act.wait_ge(w1L_ready, W1K - 1)
                for g in range(2):
                    act.wait_ge(xturned, G + g + 1)
                    nc.scalar.activation(dxT[:, g], bank[g][:].rearrange("p (k t) -> p k t", k=DT), ACT.Copy
                                         ).then_inc(xT_ready, 1)
                d_norm(2)
                act.wait_ge(xT_ready, G + 1)
                d_high_x(0)
                d_norm(3)
                act.wait_ge(topmax_ready, 1)
                nc.scalar.activation(cT, bank[2][0:2 * B, 512:512 + P], ACT.Exp, bias=mneg, accum_out=msum
                                     ).then_inc(cexp_ready, 1)
                d_take_masks(0)
                act.wait_ge(c_ready, 1)
                nc.scalar.activation(cT, cT, ACT.Copy, scale=mrcp).then_inc(cexp_ready, 1)
                for g in range(1, G):
                    d_take_masks(g)
                d_take_weights(0)
                d_high_z(0)
                d_take_weights(2)

            def d_take_weights(g):
                act.wait_ge(dcb_turned, g + 1)
                nc.scalar.activation(dcb[:, g], bank[3][:].rearrange("p (r t) -> p r t", r=2), ACT.Copy
                                     ).then_inc(dcb_ready[0], 1)

            def d_take_masks(g):
                act.wait_ge(dM_turned, g + 1)
                for r, dst in enumerate((dM1, dM2)):
                    nc.scalar.activation(dst[:, g], bank[g % 2][:, r * 512:(r + 1) * 512], ACT.Copy
                                         ).then_inc(dM_ready, 1)

            def d_high_x(g):
                for k in range(DT):
                    nc.scalar.activation(xH[:, k], dxT[:, bass.ds(g, 1), k], ACT.Copy).then_inc(xH_ready, 1)

            def d_high_z(g):
                for n, r in enumerate(Z_ORDER):
                    act.wait_ge(zm_ready, 4 * g + n + 1)
                    nc.scalar.activation(dzH[:, r], dz[r], ACT.Copy).then_inc(zH_ready, 1)

            def d_silu(g, j, k, first=False):
                i = at_ev[j, k]
                pr = TAIL if j == SJ - 1 else P
                act.wait_ge(ev_ready, NE * g + i + 1)
                if not first:
                    act.wait_ge(ch_ready, 1 + NE * g + i - 1)
                nc.scalar.activation(dsilu[0:pr, i % 2], U_[j % 2][0:pr], ACT.Silu).then_inc(dsilu_ready, 1)

            def d_high_first(g, j, first=False):
                pr = TAIL if j == SJ - 1 else P
                act.wait_ge(ch_ready, 1 + NE * g + at_ev[j, 0] + 1)
                if not first:
                    act.wait_ge(ddown_done, 1 + SJ * g + j - 1)
                nc.scalar.activation(dcH[0:pr, j % 2], dc1[0:pr, j % 2], ACT.Copy).then_inc(cH_ready, 1)

            def d_high_sum(g, j):
                pr = TAIL if j == SJ - 1 else P
                act.wait_ge(sum_ready, SJ * g + j + 1)
                nc.scalar.activation(dsH[0:pr, j % 2], dc2[0:pr, j % 2], ACT.Copy).then_inc(sH_ready, 1)

            def d_first(g, first=False):
                d_silu(g, 0, 0, first)
                d_high_first(g, 0, first)
                d_silu(g, 1, 0)
                d_silu(g, 0, 1)
                d_high_first(g, 1)
                d_high_sum(g, 0)

            def d_tiles(g, more):
                for j in range(2, SJ):
                    d_silu(g, j, 0)
                    d_silu(g, j - 1, 1)
                    if more and j == SJ - 1:
                        act.wait_ge(ev_ready, NE * g + at_ev[SJ - 1, 0] + 1)
                        d_high_x(g + 1)
                    d_high_first(g, j)
                    d_high_sum(g, j - 1)
                d_silu(g, SJ - 1, 1)
                d_high_sum(g, SJ - 1)
                if more:
                    d_high_z(g + 1)
                act.wait_ge(w_sum, g + 1)
                act.wait_ge(dn_ready, 1 + g)
                nc.scalar.activation(dwH, dw[:, 2], ACT.Copy).then_inc(wsH_ready, 1)
                if more:
                    d_first(g + 1)

            d_choose()
            d_first(0, True)
            with act.Fori(0, G - 1) as g:
                d_tiles(g, True)
            d_tiles(G - 1, False)

        @block.vector
        def _(dve):
            step = Count(dve_step)

            def link(ins):
                step.mark(ins)
                dve.wait_ge(dve_step, step.value())

            def norm_step(i, n, x, st, mv, ve, tmp, rs, nb, gain):
                if i < n:
                    step.mark(nc.vector.bn_stats(st[:, i, :], x(i)))
                    return
                i -= n
                if i == 0 or i > n:
                    dve.wait_ge(dve_step, step.value())
                if i == 0:
                    step.mark(nc.vector.memset(scrap[:], 0.0))
                elif i <= n:
                    step.mark(nc.vector.bn_aggr(mv[:, i - 1, :], st[:, i - 1, :]))
                elif i == n + 1:
                    step.mark(nc.vector.tensor_scalar(ve, mv[:, :, 1], EPS, None, ALU.add))
                elif i == n + 2:
                    step.mark(nc.vector.tensor_scalar(rs.bitcast(I32), ve.bitcast(I32), 1, None,
                                                      ALU.logical_shift_right))
                elif i == n + 3:
                    step.mark(nc.vector.tensor_scalar(rs.bitcast(I32), rs.bitcast(I32), -1, RSQRT_GUESS,
                                                      ALU.mult, ALU.add))
                elif i < n + 4 + 4 * NEWTONS:
                    newton, part = divmod(i - n - 4, 4)
                    if part == 0:
                        step.mark(nc.vector.tensor_tensor(tmp, rs, rs, ALU.mult))
                    elif part == 1:
                        step.mark(nc.vector.tensor_tensor(tmp, tmp, ve, ALU.mult))
                    elif part == 2:
                        step.mark(nc.vector.tensor_scalar(tmp, tmp, -0.5, 1.5, ALU.mult, ALU.add))
                    elif newton == NEWTONS - 1 and gain is not None:
                        step.mark(nc.vector.scalar_tensor_tensor(out=rs, in0=rs, scalar=gain, in1=tmp,
                                                                 op0=ALU.mult, op1=ALU.mult))
                    else:
                        step.mark(nc.vector.tensor_tensor(rs, rs, tmp, ALU.mult))
                else:
                    nc.vector.scalar_tensor_tensor(out=nb, in0=mv[:, :, 0], scalar=-1.0, in1=rs,
                                                   op0=ALU.mult, op1=ALU.mult).then_inc(ln_ready, 1)

            def norm_steps(n, *args):
                return Steps(lambda i: norm_step(i, n, *args), 2 * n + 5 + 4 * NEWTONS)

            def group_norm(g, gain):
                return norm_steps(BG, lambda b: X[:, bass.ds(g * BG + b, 1), :], st, mv, ve[:], tmp[:], rs[:], nb[:],
                                  gain)
            N_STATS = 2 * BG + 4 + 4 * NEWTONS

            def a_kv(g, h, first=False):
                u = h % 2
                t0 = h * I0
                c = ctxT[:, h // 8, :, t0 % 64:t0 % 64 + I0]
                if not first:
                    dve.wait_ge(y_ready, 1 + NH0 * g + h - 1)
                nc.vector.tensor_tensor(
                    kv[:, u], vT[:, :, t0:t0 + I0].unsqueeze(3).to_broadcast([P, 8, I0, I0]),
                    c.unsqueeze(2).to_broadcast([P, 8, I0, I0]), ALU.mult).then_inc(kv_ready, 1)

            def a_z(g, h, first=False):
                u = h % 2
                t0 = h * I0
                c = ctxT[:, h // 8, :, t0 % 64:t0 % 64 + I0]
                dve.wait_ge(y_ready, 1 + NH0 * g + h + 1)
                if not first:
                    dve.wait_ge(zh_ready, NH0 * g + h)
                nc.vector.tensor_tensor(
                    zr[:, u], yb[u].rearrange("p (q i j) -> p q i j", q=8, i=I0),
                    c.unsqueeze(3).to_broadcast([P, 8, I0, I0]), ALU.mult).then_inc(z_ready, 1)

            def a_bias(g):
                dve.wait_ge(vtp_ready, g + 1)
                dve.wait_ge(ctxN_loaded, 16 * (g + 1))
                nc.vector.scalar_tensor_tensor(out=vN, in0=vN, scalar=bias_c[:, 0:1], in1=ctxN,
                                               op0=ALU.mult, op1=ALU.mult).then_inc(bvx_ready, 1)

            def a_skip(g):
                dve.wait_ge(w_ready, g + 1)
                Xg = X[:, bass.ds(g * BG, BG), :]
                link(nc.vector.tensor_tensor(vN, WB[:].rearrange("p (b d) -> p b d", b=BG), ctxN, ALU.mult))
                nc.vector.tensor_tensor(Xg, Xg, vN, ALU.add).then_inc(t_done, 1)

            def a_finish(g):
                for k in range(2):
                    dve.wait_ge(o_ready, 1 + 2 * g + 1 + k)
                    if k == 0:
                        dve.wait_ge(t_done, g + 1)
                    Xg = X[:, bass.ds(g * BG + 2 * k, 2), :]
                    nc.vector.tensor_tensor(Xg, Xg, OB[:, k * 512:(k + 1) * 512].rearrange("p (b d) -> p b d", b=2),
                                            ALU.add).then_inc(a_done, 1)

            def a_heads(g, more):
                norm = Steps()
                route = Steps() if more else group_route(0)
                for h in range(LEAD, NH0 + LEAD if more else NH0):
                    if h < NH0:
                        a_z(g, h)
                    else:
                        a_z(g + 1, h - NH0)
                    if more and h == NORM_A:
                        dve.wait_ge(vN_ready, BG * (g + 2))
                        if not isinstance(g, int):
                            norm = group_norm(g + 2, gate[:, 0:1])
                        elif more:
                            norm = group_norm(0, None)
                    beside = norm if norm.left() else route if h > 8 else Steps()
                    beside.take(1 if more else 2)
                    if h + 2 < NH0:
                        if h + 2 == NH0 // 2:
                            dve.wait_ge(ctxT_loaded[1], 16 * (g + 1))
                        a_kv(g, h + 2)
                    elif more:
                        if h + 2 == NH0:
                            dve.wait_ge(vT_ready, 2 * (g + 2))
                            dve.wait_ge(ctxT_loaded[0], 16 * (g + 2))
                        a_kv(g + 1, h + 2 - NH0)
                    beside.take(1 if more else 2)
                    if more and h == BIAS_A:
                        a_bias(g + 1)
                    if more and h == NH0:
                        a_skip(g + 1)
                route.take_all()
                norm.take_all()

            N_TOPS = 11

            def tops_step(i, lg, eq, rk, l2, m1, m2, dst1, dst2):
                n = lg.shape[1]
                wide = lambda v: v.unsqueeze(2).to_broadcast([P, n, E])
                order = ramp[:].unsqueeze(1).to_broadcast([P, n, E])
                src, mx, dst = (lg, m1, dst1) if i < 5 else (l2, m2, dst2)
                dve.wait_ge(dve_step, step.value())
                if i in (0, 6):
                    step.mark(nc.vector.tensor_reduce(mx, src, AX_X, ALU.max))
                elif i in (1, 7):
                    step.mark(nc.vector.tensor_tensor(eq, src, wide(mx), ALU.is_equal))
                elif i in (2, 8):
                    step.mark(nc.vector.tensor_tensor(eq, eq, order, ALU.mult))
                elif i in (3, 9):
                    step.mark(nc.vector.tensor_reduce(rk, eq, AX_X, ALU.max))
                elif i in (4, 10):
                    step.mark(nc.vector.tensor_tensor(dst, order, wide(rk), ALU.is_equal))
                else:
                    step.mark(nc.vector.scalar_tensor_tensor(out=l2, in0=dst1, scalar=FAR, in1=lg,
                                                             op0=ALU.mult, op1=ALU.add))

            def route_step(i, g):
                tops = (lg[:, :, 0:E], eq, rk[:, :, 0], l2, m1, m2, oh1, oh2)
                if i == 0:
                    dve.wait_ge(logits_ready, g + 1)
                    step.mark(nc.vector.tensor_copy(lg, TP[:, 0:BG * NR].rearrange("p (b e) -> p b e", b=BG)))
                elif i < 6:
                    tops_step(i - 1, *tops)
                elif i == 6:
                    step.mark(nc.vector.tensor_tensor(es_[:, :, 0:E], lg[:, :, 0:E],
                                                      m1.unsqueeze(2).to_broadcast([P, BG, E]), ALU.subtract))
                elif i == 7:
                    dve.wait_ge(dve_step, step.value())
                    nc.vector.tensor_scalar(es_[:, :, E], lg[:, :, E], -1.0, None, ALU.mult).then_inc(expin_ready, 1)
                elif i < 14:
                    tops_step(i - 3, *tops)
                elif i == 21:
                    nc.vector.tensor_copy(spread[:, 1], rcp[:, BG:].unsqueeze(2).to_broadcast([P, BG, P])
                                          ).then_inc(spread_ready, 1)
                elif i == 15:
                    dve.wait_ge(exp_ready, g + 1)
                    step.mark(nc.vector.tensor_reduce(den[:, 0:BG], es_[:, :, 0:E], AX_X, ALU.add))
                else:
                    dve.wait_ge(dve_step, step.value())
                    if i == 14:
                        step.mark(nc.vector.tensor_tensor(oh1, oh1, oh2, ALU.add))
                    elif i == 16:
                        step.mark(nc.vector.tensor_scalar(den[:, BG:], es_[:, :, E], 1.0, None, ALU.add))
                    elif i == 17:
                        step.mark(nc.vector.reciprocal(rcp, den))
                    elif i == 18:
                        step.mark(nc.vector.tensor_tensor(oh1, oh1, es_[:, :, 0:E], ALU.mult))
                    elif i == 19:
                        step.mark(nc.vector.tensor_tensor(
                            oh1, oh1, rcp[:, 0:BG].unsqueeze(2).to_broadcast([P, BG, E]), ALU.mult))
                    else:
                        step.mark(nc.vector.tensor_copy(spread[:, 0].rearrange("p b (e r) -> p b e r", e=E),
                                                        oh1.unsqueeze(3).to_broadcast([P, BG, E, RANK])))

            def group_route(g):
                return Steps(lambda i: route_step(i, g), 22)
            N_ROUTE = 20

            def b_low_x(g):
                for k in range(DT):
                    dve.wait_ge(xH_ready, 2 * g + k + 1)
                    nc.vector.tensor_tensor(xL[:, k], xT[:, k], xH[:, k].bitcast(F32), ALU.subtract
                                            ).then_inc(xL_ready, 1)

            def b_hidden(g, j, beside=Steps()):
                pr = TAIL if j == J0 - 1 else P
                dve.wait_ge(gu_ready, J0 * g + j + 1)
                if j == 0:
                    dve.wait_ge(comb_ready, g + 1)
                nc.vector.tensor_tensor(b_scaled[0:pr, j % 2], U_[j % 2][0:pr], b_comb[0:pr, 0 if j < EJ else 1],
                                        ALU.mult).then_inc(scaled_ready, 1)
                beside.take(2)
                dve.wait_ge(silu_ready, J0 * g + j + 1)
                dve.wait_ge(scaled_ready, J0 * g + j + 1)
                nc.vector.tensor_tensor(b_h[0:pr, j % 2], b_silu[0:pr, j % 2], b_scaled[0:pr, j % 2], ALU.mult
                                        ).then_inc(h_ready, 1)

            def b_low(g, j):
                pr = TAIL if j == J0 - 1 else P
                dve.wait_ge(hH_ready, J0 * g + j + 1)
                nc.vector.tensor_tensor(hL[0:pr, j % 2], b_h[0:pr, j % 2], hH[0:pr, j % 2].bitcast(F32), ALU.subtract
                                        ).then_inc(hL_ready, 1)

            def c_norm(lo, hi):
                return norm_steps(hi - lo, lambda b: X[:, lo + b], cst[:, lo:hi], cmv[:, lo:hi], cvar[:, lo:hi],
                                  ctmp[:, lo:hi], crs[:, lo:hi], cnb[:, lo:hi], HD ** -0.5)

            def b_tiles(g, more):
                if more:
                    norm, route = group_norm(g + 1, None), group_route(g + 1)
                else:
                    norm, route = c_norm(0, B - BG), Steps()
                    dve.wait_ge(b_done, 1 + 2 * (G - 1))
                for j in range(1, J0):
                    beside = norm if norm.left() else route if j > 11 else Steps()
                    b_hidden(g, j, beside)
                    beside.take(1)
                    if more and j == J0 - 1:
                        route.take_all()
                    b_low(g, j - 1)
                    beside.take(2)
                if more:
                    b_low_x(g + 1)
                b_low(g, J0 - 1)
                if more:
                    b_hidden(g + 1, 0)

            def b_finish(g):
                dve.wait_ge(down_done, 1 + J0 * (g + 1))
                for k in range(2):
                    Xg = X[:, bass.ds(g * BG + 2 * k, 2), :]
                    nc.vector.scalar_tensor_tensor(
                        out=Xg, in0=DN[:, k * 512:(k + 1) * 512].rearrange("p (b d) -> p b d", b=2),
                        scalar=gate[:, 2:3], in1=Xg, op0=ALU.mult, op1=ALU.add).then_inc(b_done, 1)

            def c_shift(g, k, beside=Steps()):
                n = 8 * g + k
                u = k % 2
                dve.wait_ge(scores_ready, n + 1)
                S = S_[u][:].rearrange("p (h k) -> p h k", h=HH)
                step.mark(nc.vector.tensor_reduce(mx[:, u], S, AX_X, ALU.max))
                found = step.value()
                beside.take(2)
                dve.wait_ge(dve_step, found)
                step.mark(nc.vector.tensor_scalar(mx[:, u], mx[:, u], MASKED, None, ALU.max))
                found = step.value()
                beside.take(2)
                dve.wait_ge(dve_step, found)
                if not (isinstance(n, int) and n < 2):
                    dve.wait_ge(p_turned, n - 1)
                nc.vector.scalar_tensor_tensor(out=E_[:, u], in0=S, scalar=MASKED,
                                               in1=mx[:, u].unsqueeze(2).to_broadcast([P, HH, P]),
                                               op0=ALU.max, op1=ALU.subtract).then_inc(shifted, 1)

            def c_finish(g, b):
                t = BG * g + b
                dve.wait_ge(o_turned, 2 * t + 2)
                O = O_.rearrange("p (h e) -> p h e", h=HEADS)
                link(nc.vector.reciprocal(r16, O[:, :, HD]))
                nc.vector.scalar_tensor_tensor(out=otmp, in0=O[:, :, 0:HD], scalar=gate[:, 1:2],
                                               in1=r16.unsqueeze(2).to_broadcast([P, HEADS, HD]),
                                               op0=ALU.mult, op1=ALU.mult).then_inc(o_read, 1)
                dve.wait_ge(o_read, 1 + t + 1)
                Xt = X[:, bass.ds(t, 1), :]
                nc.vector.tensor_tensor(Xt, Xt, otmp.rearrange("p h e -> p (h e)").unsqueeze(1), ALU.add
                                        ).then_inc(c_done, 1)

            def d_norm(lo, hi):
                return norm_steps(hi - lo, lambda b: X[:, lo + b], dstat[:, lo:hi], dmv[:, lo:hi], dvar[:, lo:hi],
                                  dtmp[:, lo:hi], drs[:, lo:hi], dnb[:, lo:hi], None)

            last_norm = d_norm(B - BG, B)

            def c_steps(g, more):
                norm = Steps()
                if not more:
                    dve.wait_ge(c_done, B - BG)
                for k in range(8):
                    if k and (k < 6 or more):
                        c_shift(g + (k + 2) // 8, (k + 2) % 8, norm)
                    norm.take(4)
                    if not more:
                        if k == 1:
                            norm = d_norm(0, B - BG)
                        if k == 6:
                            norm.take_all()
                        if k == 7:
                            dve.wait_ge(c_done, B - 1)
                            last_norm.take(BG - 1)
                    if k and k % 2 == 0:
                        c_finish(g, k // 2 - 1)
                if more:
                    c_shift(g + 1, 2)
                c_finish(g, BG - 1)

            def d_take_x(g):
                dve.wait_ge(xturned, G + g + 1)
                nc.vector.tensor_copy(dxT[:, g], bank[g % 2][:].rearrange("p (k t) -> p k t", k=DT)
                                      ).then_inc(xT_ready, 1)

            def d_choose():
                last_norm.take_all()
                d_take_x(2)
                d_low_x(0)
                dve.wait_ge(w1L_ready, W1K)
                d_take_x(3)
                dve.wait_ge(d_logits, G)
                link(nc.vector.tensor_copy(dlg, bank[2][:, 0:B * E].rearrange("p (b e) -> p b e", b=B)))
                for i in range(N_TOPS):
                    if i == 7:
                        dve.wait_ge(dve_step, step.value())
                        nc.vector.memset(scrap[:], 0.0).then_inc(tops_ready, 1)
                    tops_step(i, dlg, deq, drk, dl2, dtop[:, 0:B], dtop[:, B:], do1, do2)
                dve.wait_ge(dve_step, step.value())
                for r, hot in enumerate((do1, do2)):
                    ins = nc.vector.tensor_scalar(dhot[:, r].rearrange("p b (e r) -> p b e r", e=E),
                                                  hot.unsqueeze(3).to_broadcast([P, B, E, RANK]), LORA_ALPHA, None,
                                                  ALU.mult)
                    ins.then_inc(hot_ready[r], 1)
                    if r == 0:
                        dve.wait_ge(tops_turned, 1)
                        link(nc.vector.tensor_reduce(mtop, bank[2][0:2 * B, 512:512 + P], AX_X, ALU.max))
                        nc.vector.tensor_scalar(mneg, mtop, -1.0, None, ALU.mult).then_inc(topmax_ready, 1)
                dve.wait_ge(cexp_ready, 1)
                nc.vector.reciprocal(mrcp, msum).then_inc(c_ready, 1)
                dve.wait_ge(c_back, 1)
                nc.vector.tensor_copy(dctok, bank[2][:, 512 + P:512 + P + 2 * B]).then_inc(ctok_ready, 1)
                d_take_weights(1)
                d_split_z(0)
                d_take_weights(3)
                dve.wait_ge(dcb_ready[0], 2)
                dve.wait_ge(dcb_ready[1], 2)

            def d_take_weights(g):
                dve.wait_ge(dcb_turned, g + 1)
                nc.vector.tensor_copy(dcb[:, g], bank[2][:].rearrange("p (r t) -> p r t", r=2)
                                      ).then_inc(dcb_ready[1], 1)

            def d_low_x(g):
                for k in range(DT):
                    dve.wait_ge(xH_ready, 2 * (G + g) + k + 1)
                    nc.vector.tensor_tensor(xL[:, k], dxT[:, bass.ds(g, 1), k], xH[:, k].bitcast(F32), ALU.subtract
                                            ).then_inc(xL_ready, 1)

            def d_split_z(g):
                dve.wait_ge(dMD_ready, g + 1)
                for n, r in enumerate(Z_ORDER):
                    dve.wait_ge(z_psum, 2 * g + n % 2 + 1)
                    m = (dM1[:, bass.ds(g, 1)] if r % 2 == 0 else dMD).bitcast(F32)
                    nc.vector.tensor_tensor(dz[r], (U_, G_)[r // 2][0], m, ALU.mult).then_inc(zm_ready, 1)
                for n, r in enumerate(Z_ORDER):
                    dve.wait_ge(zH_ready, 4 * g + n + 1)
                    nc.vector.tensor_tensor(dzL[:, r], dz[r], dzH[:, r].bitcast(F32), ALU.subtract
                                            ).then_inc(zL_ready, 1)

            def d_rows(g, j, k):
                i = at_ev[j, k]
                pr = TAIL if j == SJ - 1 else P
                dst = (dc1, dc2)[k]
                dve.wait_ge(ev_ready, NE * g + i + 1)
                nc.vector.tensor_tensor(dscaled[0:pr, i % 2], G_[j % 2][0:pr], dcb[0:pr, bass.ds(g, 1), k], ALU.mult
                                        ).then_inc(dscaled_ready, 1)
                dve.wait_ge(dsilu_ready, NE * g + i + 1)
                dve.wait_ge(dscaled_ready, NE * g + i + 1)
                nc.vector.tensor_tensor(dst[0:pr, j % 2], dscaled[0:pr, i % 2], dsilu[0:pr, i % 2], ALU.mult
                                        ).then_inc(ch_ready, 1)
                if k == 1:
                    dve.wait_ge(ch_ready, 1 + NE * g + i + 1)
                    nc.vector.tensor_tensor(dc2[0:pr, j % 2], dc2[0:pr, j % 2], dc1[0:pr, j % 2], ALU.add
                                            ).then_inc(sum_ready, 1)

            def d_low_first(g, j):
                pr = TAIL if j == SJ - 1 else P
                dve.wait_ge(cH_ready, SJ * g + j + 1)
                nc.vector.tensor_tensor(dcL[0:pr, j % 2], dc1[0:pr, j % 2], dcH[0:pr, j % 2].bitcast(F32),
                                        ALU.subtract).then_inc(cL_ready, 1)

            def d_low_sum(g, j):
                pr = TAIL if j == SJ - 1 else P
                dve.wait_ge(sH_ready, SJ * g + j + 1)
                nc.vector.tensor_tensor(dsL[0:pr, j % 2], dc2[0:pr, j % 2], dsH[0:pr, j % 2].bitcast(F32),
                                        ALU.subtract).then_inc(sL_ready, 1)

            def d_mix(g):
                dve.wait_ge(ddown_done, 1 + SJ * (g + 1))
                nc.vector.tensor_tensor(dw[:, 1], bank[2][:, 512:1024], dM1[:, bass.ds(g, 1)].bitcast(F32), ALU.mult
                                        ).then_inc(w_mixed, 1)
                nc.vector.tensor_copy(dw[:, 2], bank[2][:, 512:1024]).then_inc(w_mixed, 1)
                dve.wait_ge(w_mixed, 1 + 4 * g + 2)
                nc.vector.tensor_tensor(dw[:, 0], bank[2][:, 0:512], dw[:, 2], ALU.subtract).then_inc(w_mixed, 1)
                dve.wait_ge(w_mixed, 1 + 4 * g + 3)
                nc.vector.tensor_tensor(dw[:, 0], dw[:, 0], dM2[:, bass.ds(g, 1)], ALU.mult).then_inc(w_mixed, 1)
                dve.wait_ge(w_mixed, 1 + 4 * g + 4)
                nc.vector.tensor_tensor(dw[:, 2], dw[:, 0], dw[:, 1], ALU.add).then_inc(w_sum, 1)
                dve.wait_ge(wsH_ready, g + 1)
                nc.vector.tensor_tensor(dwL, dw[:, 2], dwH.bitcast(F32), ALU.subtract).then_inc(wsL_ready, 1)

            def d_finish(g):
                dve.wait_ge(dn_ready, 1 + g + 1)
                for k in range(2):
                    Xg = X[:, bass.ds(g * BG + 2 * k, 2), :]
                    nc.vector.scalar_tensor_tensor(
                        out=Xg, in0=DN[:, k * 512:(k + 1) * 512].rearrange("p (b d) -> p b d", b=2),
                        scalar=gate[:, 3:4], in1=Xg, op0=ALU.mult, op1=ALU.add).then_inc(d_done, 1)

            def d_first(g):
                d_rows(g, 0, 0)
                d_low_first(g, 0)
                d_rows(g, 1, 0)
                d_rows(g, 0, 1)
                d_low_first(g, 1)
                d_low_sum(g, 0)

            def d_tiles(g, more):
                for j in range(2, SJ):
                    d_rows(g, j, 0)
                    d_rows(g, j - 1, 1)
                    if more and j == SJ - 1:
                        d_low_x(g + 1)
                    d_low_first(g, j)
                    d_low_sum(g, j - 1)
                d_rows(g, SJ - 1, 1)
                d_low_sum(g, SJ - 1)
                if more:
                    dve.wait_ge(dn_ready, 1 + g)
                    d_split_z(g + 1)
                    dve.wait_ge(zL_ready, 4 * (g + 2))
                d_mix(g)
                if more:
                    d_first(g + 1)
                d_finish(g)

            dve.wait_ge(x0_loaded, 16)
            dve.wait_ge(gate_ready, 1)
            group_norm(0, gate[:, 0:1]).take_all()
            dve.wait_ge(x1_loaded, 16)
            norm = group_norm(1, gate[:, 0:1])
            norm.take(2 * BG + 1)
            dve.wait_ge(vN_ready, BG)
            norm.take_all()
            dve.wait_ge(vT_ready, 2)
            dve.wait_ge(ctxT_loaded[0], 16)
            for h in range(2):
                a_kv(0, h, True)
            a_bias(0)
            for h in range(LEAD):
                a_z(0, h, h < 2)
                a_kv(0, h + 2)
                if h == 1:
                    a_skip(0)
            dve.wait_ge(xrest_loaded, 16)
            dve.wait_ge(small_loaded, 16 * 3)
            per = N_STATS + 1
            start = step.value()
            with dve.Fori(0, G - 2) as g:
                step.enter(g, per, start)
                a_heads(g, True)
                a_finish(g)
            step.leave(per, G - 2, start)
            a_heads(G - 2, True)
            a_finish(G - 2)
            a_heads(G - 1, False)
            a_finish(G - 1)
            b_low_x(0)
            b_hidden(0, 0)
            per = N_STATS + N_ROUTE
            start = step.value()
            with dve.Fori(0, G - 1) as g:
                step.enter(g, per, start)
                b_tiles(g, True)
                b_finish(g)
            step.leave(per, G - 1, start)
            b_tiles(G - 1, False)
            b_finish(G - 1)
            dve.wait_ge(b_done, 1 + 2 * G)
            nc.vector.memset(OT, 0.0).then_inc(ot_zeroed, 1)
            norm = c_norm(B - BG, B)
            norm.take(4)
            c_shift(0, 0)
            norm.take(3)
            c_shift(0, 1, norm)
            c_shift(0, 2, norm)
            norm.take_all()
            per = 2 * 8 + BG
            start = step.value()
            with dve.Fori(0, G - 1) as g:
                step.enter(g, per, start)
                c_steps(g, True)
            step.leave(per, G - 1, start)
            c_steps(G - 1, False)
            dve.wait_ge(c_done, B)
            d_choose()
            d_first(0)
            with dve.Fori(0, G - 1) as g:
                d_tiles(g, True)
            d_tiles(G - 1, False)

        @block.tensor
        def _(pe):
            pe.wait_ge(consts_ready, 8)

            def a_turn(g, first=False):
                pe.wait_ge(vN_ready, BG * (g + 1))
                if not first:
                    pe.wait_ge(vT_ready, 2 * g)
                for k in range(DT):
                    for b in range(BG):
                        mm = nc.tensor.transpose(TV[:, (k * BG + b) * P:(k * BG + b + 1) * P],
                                                 vN[:, b, k * P:(k + 1) * P], ident[:])
                mm.then_inc(vtp_ready, 1)

            def a_block_sums(g, first=False):
                pe.wait_ge(bvx_ready, g + 1)
                if not first:
                    pe.wait_ge(t_done, g)
                ob = ones_blk[:].rearrange("p a b -> p (a b)")
                for k in range(2):
                    mm = nc.tensor.matmul(WB[:, k * 512:(k + 1) * 512], ob, vN[:, 2 * k:2 * k + 2, :],
                                          start=True, stop=True)
                mm.then_inc(w_ready, 1)

            def a_conv(g, h):
                u = h % 2
                pe.wait_ge(toep_loaded[0 if h < TOEP_H else 1], 16)
                pe.wait_ge(kv_ready, NH0 * g + h + 1)
                if h >= 2:
                    pe.wait_ge(z_ready, 1 + NH0 * g + h - 1)
                else:
                    pe.wait_ge(z_ready, 1 + NH0 * g)
                y = yb[u]
                n = BG * I0 * I0
                diag, off = toep[:, h, 0:P], toep[:, h, P:2 * P]
                kv0 = kv[:, u, 0:BG].rearrange("p q i j -> p (q i j)")
                kv1 = kv[:, u, BG:2 * BG].rearrange("p q i j -> p (q i j)")
                nc.tensor.matmul(y[:, 0:n], diag, kv0, start=True, stop=False, skip_group_check=True)
                nc.tensor.matmul(y[:, n:2 * n], diag, kv1, start=False, stop=False, skip_group_check=True)
                nc.tensor.matmul(y[:, n:2 * n], off, kv0, start=False, stop=True, skip_group_check=True
                                 ).then_inc(y_ready, 1)

            def a_sum(g):
                pe.wait_ge(z2_ready, 1 + NH0 * (g + 1))
                pe.wait_ge(a_done, 1 + 2 * g)
                for b in range(BG):
                    for k in range(DT):
                        for i in range(QUARTER):
                            mm = nc.tensor.matmul(OB[:, b * D + k * P:b * D + (k + 1) * P], z2[:, k * BG + b, i, :],
                                                  ident[:], start=(i == 0), stop=(i == QUARTER - 1),
                                                  skip_group_check=True)
                    if b % 2:
                        mm.then_inc(o_ready, 1)

            a_turn(0, True)
            a_conv(0, 0)
            a_conv(0, 1)
            a_block_sums(0, True)
            with pe.Fori(0, G - 1) as g:
                for h in range(2, NH0):
                    a_conv(g, h)
                    if h == TURN_A:
                        a_turn(g + 1)
                    if h == BIAS_A + 2:
                        a_block_sums(g + 1)
                for h in range(2):
                    a_conv(g + 1, h)
                a_sum(g)

            def b_turn(g):
                pe.wait_ge(vN_ready, BG * (G + g + 1))
                if isinstance(g, int) and g == 0:
                    pe.wait_ge(t_done, G)
                else:
                    pe.wait_ge(comb_ready, g)
                for k in range(DT):
                    for b in range(BG):
                        mm = nc.tensor.transpose(TP[:, (k * BG + b) * P:(k * BG + b + 1) * P],
                                                 xn[:, b, k * P:(k + 1) * P], ident[:])
                mm.then_inc(xturned, 1)

            def b_logits(g):
                pe.wait_ge(xT_ready, g + 1)
                for b in range(BG):
                    for k in range(DT):
                        mm = nc.tensor.matmul(TP[:, b * NR:(b + 1) * NR], xT[:, k, b * P:(b + 1) * P], wr_sb[:, k],
                                              start=(k == 0), stop=(k == DT - 1), skip_group_check=True)
                mm.then_inc(logits_ready, 1)

            def b_spread(g):
                pe.wait_ge(spread_ready, g + 1)
                for r in range(2):
                    for b in range(BG):
                        mm = nc.tensor.transpose(TP[:, (r * BG + b) * P:(r * BG + b + 1) * P], spread[:, r, b],
                                                 ident[:])
                mm.then_inc(spread_turned, 1)

            def b_gate_up(g, j):
                pr = TAIL if j == J0 - 1 else P
                if j == 0:
                    pe.wait_ge(xL_ready, 2 * (g + 1))
                if j >= 2:
                    pe.wait_ge(silu_ready, J0 * g + j - 1)
                else:
                    pe.wait_ge(h_ready, 1 + J0 * g)
                for at, dst in ((0, G_[j % 2]), (2 * P, U_[j % 2])):
                    if j >= 2 and at:
                        pe.wait_ge(scaled_ready, J0 * g + j - 1)
                    n = 0
                    for wX, mX in ((w0H, xH), (w0L, xH), (w0H, xL)):
                        for k in range(DT):
                            mm = nc.tensor.matmul(dst[0:pr], wX[:, j, at + k * P:at + k * P + pr], mX[:, k],
                                                  start=(n == 0), stop=(n == 5))
                            n += 1
                mm.then_inc(gu_ready, 1)

            def b_down(g, j):
                pr = TAIL if j == J0 - 1 else P
                if j == 0:
                    pe.wait_ge(b_done, 1 + 2 * g)
                pe.wait_ge(hL_ready, J0 * g + j + 1)
                for b in range(BG):
                    n = 0
                    for hX, wX in ((hH, w0H), (hH, w0L), (hL, w0H)):
                        mm = nc.tensor.matmul(DN[:, b * D:(b + 1) * D], hX[0:pr, j % 2, b * P:(b + 1) * P],
                                              wX[0:pr, j, 4 * P:], start=(j == 0 and n == 0 and b % 2 == 0),
                                              stop=(j == J0 - 1 and n == 2), skip_group_check=True)
                        n += 1
                mm.then_inc(down_done, 1)

            def b_tiles(g, more):
                for j in range(1, J0):
                    b_gate_up(g, j)
                    if j >= 2:
                        b_down(g, j - 2)
                    if more and j == 10:
                        b_turn(g + 1)
                    if more and j == 12:
                        b_logits(g + 1)
                    if not more and j == 15:
                        pe.wait_ge(vN_ready, BG * (2 * G + 1))
                        for b in range(BG):
                            for k in range(DT):
                                mm = nc.tensor.transpose(bank[2][:, b * D + k * P:b * D + (k + 1) * P],
                                                         qn[:, b, k * P:(k + 1) * P], ident[:])
                            mm.then_inc(qT_turned, 1)
                if more:
                    b_spread(g + 1)
                b_down(g, J0 - 2)
                if more:
                    b_gate_up(g + 1, 0)
                b_down(g, J0 - 1)

            def c_scores(g, k):
                n = 8 * g + k
                r, b, kk = k // 4, k // 2, k % 2
                pe.wait_ge(qT_ready, BG * g + b + 1)
                pe.wait_ge(kbd_loaded[r], 16 * 2 * HH * (g + 1))
                if not (isinstance(n, int) and n < 2):
                    pe.wait_ge(shifted, n - 1)
                for c in range(2):
                    S = S_[k % 2][:, c * 512:(c + 1) * 512]
                    nc.tensor.matmul(S, qT[:, b, kk], kbd[:, r, b % 2, kk, 4 * c:4 * c + 4, :], start=True, stop=False)
                    mm = nc.tensor.matmul(S, identb[:], neg[:], start=False, stop=True)
                mm.then_inc(scores_ready, 1)

            def c_turn_p(g, k):
                n = 8 * g + k
                pe.wait_ge(exp_done, n + 1)
                if not (isinstance(n, int) and n == 0):
                    pe.wait_ge(pT_ready, n)
                for h in range(HH):
                    mm = nc.tensor.transpose(PTP[:, h * P:(h + 1) * P], E_[:, k % 2, h], ident[:])
                mm.then_inc(p_turned, 1)

            def c_values(g, k):
                n = 8 * g + k
                r, b, kk = k // 4, k // 2, k % 2
                pe.wait_ge(pT_ready, n + 1)
                pe.wait_ge(va_loaded[r], 16 * (g + 1))
                for h in range(HH):
                    c, i = h // 4, h % 4
                    mm = nc.tensor.matmul(OT[i * OS:i * OS + VA, c * P:(c + 1) * P], va[:, r, b % 2, kk * HH + h],
                                          PT_[:, k % 2, h], start=True, stop=True, skip_group_check=True)
                mm.then_inc(pv_done, 1)

            def c_turn_o(g, k):
                n = 8 * g + k
                b, kk = k // 2, k % 2
                pe.wait_ge(ot_taken, n + 1)
                if kk == 0:
                    pe.wait_ge(o_read, 1 + BG * g + b)
                for c in range(2):
                    mm = nc.tensor.transpose(O_[:, (2 * kk + c) * P:(2 * kk + c + 1) * P], ot[:, c], ident[:])
                mm.then_inc(o_turned, 1)

            def c_turn_q(g, b):
                pe.wait_ge(vN_ready, BG * (2 * G + g) + b + 1)
                pe.wait_ge(qT_ready, BG * g + b)
                for k in range(DT):
                    mm = nc.tensor.transpose(TQ[:, k * P:(k + 1) * P], qn[:, b, k * P:(k + 1) * P], ident[:])
                mm.then_inc(qT_turned, 1)

            def d_turn(g):
                pe.wait_ge(vN_ready, BG * (3 * G + g + 1))
                if g >= 2:
                    pe.wait_ge(xT_ready, G + g - 1)
                for k in range(DT):
                    for b in range(BG):
                        mm = nc.tensor.transpose(bank[g % 2][:, (k * BG + b) * P:(k * BG + b + 1) * P],
                                                 dxn[:, g % 2, b, k * P:(k + 1) * P], ident[:])
                mm.then_inc(xturned, 1)

            def c_steps(g, more):
                for k in range(8):
                    if k and (k < 6 or more):
                        c_scores(g + (k + 2) // 8, (k + 2) % 8)
                    if more and k in TURN_AT:
                        pe.wait_ge(ot_taken, 8 * g + k)
                        c_turn_q(g + 1, TURN_AT.index(k))
                    if k < 7 or more:
                        c_turn_p(g + (k + 1) // 8, (k + 1) % 8)
                    if k:
                        c_turn_o(g, k - 1)
                    if more and k in TURN_AT:
                        pe.wait_ge(qT_ready, BG * (g + 1) + TURN_AT.index(k) + 1)
                    c_values(g, k)
                if more:
                    c_scores(g + 1, 2)
                c_turn_o(g, 7)
                if not more:
                    pe.wait_ge(shifted, 8 * G)
                    d_turn(0)
                    d_turn(1)

            def three(dst, pairs, start=True, stop=True, skip=False):
                prods = [(a[0], m[0]) for a, m in pairs] + [(a[1], m[0]) for a, m in pairs] + [
                    (a[0], m[1]) for a, m in pairs]
                for n, (a, m) in enumerate(prods):
                    mm = nc.tensor.matmul(dst, a, m, start=start and n == 0, stop=stop and n == len(prods) - 1,
                                          skip_group_check=skip)
                return mm

            def d_router(g):
                pe.wait_ge(xT_ready, G + g + 1)
                for b in range(BG):
                    t = g * BG + b
                    for k in range(DT):
                        mm = nc.tensor.matmul(bank[2][:, t * E:(t + 1) * E], dxT[:, g, k, b * P:(b + 1) * P],
                                              gw_sb[:, k], start=(k == 0), stop=(k == DT - 1), skip_group_check=True)
                mm.then_inc(d_logits, 1)

            def d_masks(g):
                for r in range(2):
                    pe.wait_ge(hot_ready[r], 1)
                    if r == 0 and g >= 2:
                        pe.wait_ge(dM_ready, 2 * (g - 1))
                    for b in range(BG):
                        mm = nc.tensor.matmul(bank[g % 2][:, (r * BG + b) * P:(r * BG + b + 1) * P],
                                              dhot[:, r, g * BG + b], identb[:], start=True, stop=True,
                                              skip_group_check=True)
                mm.then_inc(dM_turned, 1)

            def d_weights(g):
                if g >= 2:
                    pe.wait_ge(dcb_ready[g % 2], 1)
                for r in range(2):
                    for b in range(BG):
                        q = r * B + g * BG + b
                        mm = nc.tensor.matmul(bank[3 - g % 2][:, (r * BG + b) * P:(r * BG + b + 1) * P],
                                              dctok[:, q:q + 1].to_broadcast([P, P]), ident[:], start=True, stop=True,
                                              skip_group_check=True)
                mm.then_inc(dcb_turned, 1)

            def d_choose():
                d_router(0)
                d_router(1)
                d_turn(2)
                d_router(2)
                d_turn(3)
                d_router(3)
                pe.wait_ge(tops_ready, 1)
                nc.tensor.transpose(bank[2][0:2 * B, 512:512 + P], dtop, ident[:]).then_inc(tops_turned, 1)
                d_masks(0)
                d_masks(1)
                pe.wait_ge(cexp_ready, 2)
                nc.tensor.matmul(bank[2][:, 512 + P:512 + P + 2 * B], cT, ident[0:2 * B, 0:2 * B], start=True,
                                 stop=True, skip_group_check=True).then_inc(c_back, 1)
                d_masks(2)
                d_masks(3)
                pe.wait_ge(ctok_ready, 1)
                d_weights(0)
                d_weights(1)
                pe.wait_ge(dM_ready, 2 * G)
                d_adapters_in(0)
                d_weights(2)
                d_weights(3)

            def d_adapters_in(g):
                pe.wait_ge(xL_ready, 2 * (G + g + 1))
                for r, dst in enumerate((U_[0], G_[0])):
                    a = [((w1H[:, r * D + k * P:r * D + (k + 1) * P], w1L[:, r * D + k * P:r * D + (k + 1) * P]),
                          (xH[:, k], xL[:, k])) for k in range(DT)]
                    three(dst, a).then_inc(z_psum, 1)

            def d_base(g, j):
                pr = TAIL if j == SJ - 1 else P
                if j >= 2:
                    pe.wait_ge(dsilu_ready, NE * g + at_ev[j - 2, 1] + 1)
                else:
                    pe.wait_ge(zm_ready, 4 * (g + 1))
                if j == 0:
                    pe.wait_ge(zL_ready, 4 * g + 2)
                for at, dst, zr_ in ((0, U_[j % 2], 0), (2 * P, G_[j % 2], 2)):
                    if j >= 2 and zr_ == 2:
                        pe.wait_ge(dscaled_ready, NE * g + at_ev[j - 2, 1] + 1)
                    a = [(tuple(w[:, 0:pr] for w in w1_tile(j, at + k * P, P)), (xH[:, k], xL[:, k]))
                         for k in range(DT)]
                    lora = tuple(w[:, 0:pr] for w in w1_tile(j, 4 * P + at // 2, P))
                    mm = three(dst[0:pr], a + [(lora, (dzH[:, zr_], dzL[:, zr_]))], skip=True)
                mm.then_inc(ev_ready, 1)

            def d_delta(g, j):
                pr = TAIL if j == SJ - 1 else P
                if j == 0:
                    pe.wait_ge(zL_ready, 4 * (g + 1))
                pe.wait_ge(dsilu_ready, NE * g + at_ev[j, 0] + 1)
                pe.wait_ge(dscaled_ready, NE * g + at_ev[j, 0] + 1)
                for at, dst, zr_ in ((0, U_[j % 2], 1), (P, G_[j % 2], 3)):
                    lora = tuple(w[:, 0:pr] for w in w1_tile(j, 4 * P + at, P))
                    mm = three(dst[0:pr], [(lora, (dzH[:, zr_], dzL[:, zr_]))], start=False, skip=True)
                mm.then_inc(ev_ready, 1)

            def d_down(g, j):
                pr = TAIL if j == SJ - 1 else P
                pe.wait_ge(cL_ready, SJ * g + j + 1)
                pe.wait_ge(sL_ready, SJ * g + j + 1)
                if j == 0:
                    pe.wait_ge(w_mixed, 1 + 4 * g)
                    pe.wait_ge(d_done, 1 + 2 * g)
                wd = tuple(w[0:pr] for w in w1_tile(j, 6 * P, D))
                wa = tuple(w[0:pr] for w in w1_tile(j, 6 * P + D, P))
                ends = dict(start=(j == 0), stop=(j == SJ - 1), skip=True)
                three(bank[2][:, 0:512], [(wa, (dsH[0:pr, j % 2], dsL[0:pr, j % 2]))], **ends)
                three(bank[2][:, 512:1024], [(wa, (dcH[0:pr, j % 2], dcL[0:pr, j % 2]))], **ends)
                for b in range(BG):
                    tok = slice(b * P, (b + 1) * P)
                    mm = three(DN[:, b * D:(b + 1) * D], [((dsH[0:pr, j % 2, tok], dsL[0:pr, j % 2, tok]), wd)],
                               start=(j == 0 and b % 2 == 0), stop=False, skip=True)
                mm.then_inc(ddown_done, 1)

            def d_adapt(g):
                pe.wait_ge(wsL_ready, g + 1)
                wb = (w1H[:, 2 * D:3 * D], w1L[:, 2 * D:3 * D])
                for b in range(BG):
                    tok = slice(b * P, (b + 1) * P)
                    mm = three(DN[:, b * D:(b + 1) * D], [((dwH[:, tok], dwL[:, tok]), wb)], start=False, skip=True)
                mm.then_inc(dn_ready, 1)

            def d_tiles(g, more):
                for j in range(2, SJ):
                    d_base(g, j)
                    d_delta(g, j - 1)
                    d_down(g, j - 2)
                d_delta(g, SJ - 1)
                if more:
                    pe.wait_ge(dsilu_ready, NE * g + at_ev[SJ - 2, 1] + 1)
                    pe.wait_ge(dscaled_ready, NE * g + at_ev[SJ - 2, 1] + 1)
                    d_adapters_in(g + 1)
                d_down(g, SJ - 2)
                d_down(g, SJ - 1)
                if more:
                    d_base(g + 1, 0)
                    d_base(g + 1, 1)
                d_adapt(g)
                if more:
                    d_delta(g + 1, 0)

            for h in range(2, NH0):
                a_conv(G - 1, h)
                if h == 4:
                    b_turn(0)
                if h == 7:
                    b_logits(0)
            a_sum(G - 1)
            b_spread(0)
            pe.wait_ge(wL_ready, J0)
            b_gate_up(0, 0)
            with pe.Fori(0, G - 1) as g:
                b_tiles(g, True)
            b_tiles(G - 1, False)
            pe.wait_ge(h_ready, 1 + J0 * G)
            c_scores(0, 0)
            c_scores(0, 1)
            pe.wait_ge(qT_ready, BG)
            c_turn_p(0, 0)
            c_scores(0, 2)
            pe.wait_ge(ot_zeroed, 1)
            with pe.Fori(0, G - 1) as g:
                c_steps(g, True)
            c_steps(G - 1, False)
            pe.wait_ge(w1L_ready, W1K)
            d_choose()
            d_base(0, 0)
            d_base(0, 1)
            d_delta(0, 0)
            with pe.Fori(0, G - 1) as g:
                d_tiles(g, True)
            d_tiles(G - 1, False)


def kernel(**inputs):
    import numpy as np
    import concourse.bacc as bacc
    from concourse.bass_utils import run_bass_kernel_spmd

    a = {k: np.asarray(v) for k, v in inputs.items()}

    def halves(w):
        return w.reshape(DT, P, -1).transpose(1, 0, 2)

    def padded(w, n, axis):
        pad = [(0, 0)] * w.ndim
        pad[axis] = (0, n - w.shape[axis])
        return np.pad(w, pad)

    def expert_cols(w):
        w = w.transpose(1, 0, 2).reshape(D, P, EJ).transpose(0, 2, 1)
        return halves(w.reshape(D, -1)).reshape(P, DT, EJ, P)

    def plain_cols(w):
        return halves(padded(w, SJ * P, 1)).reshape(P, DT, SJ, P)

    def rows(w):
        return padded(w, SJ * P, 0).reshape(SJ, P, -1).transpose(1, 0, 2)

    gate0 = np.concatenate([expert_cols(a["L0_ffn_Wg"]), plain_cols(a["L0_ffn_Sg"])], 2)
    up0 = np.concatenate([expert_cols(a["L0_ffn_Wu"]), plain_cols(a["L0_ffn_Su"])], 2)
    down0 = np.concatenate([a["L0_ffn_Wd"].reshape(P, EJ, D), rows(a["L0_ffn_Sd"])], 1)
    tiles = lambda w: w.transpose(2, 0, 1, 3).reshape(w.shape[2], P, -1)
    w0 = np.concatenate([tiles(gate0), tiles(up0), down0.transpose(1, 0, 2)], 2)
    wr = halves(padded(np.concatenate([a["L0_ffn_Wr"], a["L0_ffn_Wsg"]], 1), NR, 1)).reshape(P, -1)
    er_rows = lambda w: w.reshape(P, -1)
    up1, gate1 = plain_cols(a["L1_ffn_w_up"].T), plain_cols(a["L1_ffn_w_gate"].T)
    b_up = padded(er_rows(a["L1_ffn_up_B"].transpose(0, 2, 1)), SJ * P, 1).reshape(P, SJ, P).transpose(1, 0, 2)
    b_gate = padded(er_rows(a["L1_ffn_gate_B"].transpose(0, 2, 1)), SJ * P, 1).reshape(P, SJ, P).transpose(1, 0, 2)
    down1 = rows(a["L1_ffn_w_down"].T).transpose(1, 0, 2)
    a_down = rows(er_rows(a["L1_ffn_down_A"]).T).transpose(1, 0, 2)
    w1_tiles = np.concatenate([tiles(up1), tiles(gate1), b_up, b_gate, down1, a_down], 2)
    ab = np.concatenate([halves(er_rows(a["L1_ffn_up_A"]).T).reshape(P, -1),
                         halves(er_rows(a["L1_ffn_gate_A"]).T).reshape(P, -1),
                         er_rows(a["L1_ffn_down_B"].transpose(0, 2, 1))], 1)
    w1 = np.concatenate([ab, w1_tiles.transpose(1, 0, 2).reshape(P, -1)], 1).reshape(P, W1K, W1C).transpose(1, 0, 2)
    ctx_one = np.concatenate([a["ctx_2048"].reshape(B, P, HEADS, HD), np.ones((B, P, HEADS, 1), np.float32)], 3)
    gw = halves(a["L1_ffn_gate_w"].T).reshape(P, -1)
    filt = np.lib.stride_tricks.sliding_window_view(np.pad(a["L0_xattn_k"], ((0, 0), (P, 0))), 2 * P, 1)
    filt = filt[:, P:0:-1].transpose(1, 0, 2)
    ctx_t = a["ctx_2048"].reshape(G, BG, P, DT, P).transpose(0, 4, 3, 1, 2).reshape(G, P, DT * BG, P)
    ctx_half = ctx_t.reshape(G, P, DT * BG, 2, P // 2).transpose(0, 3, 1, 2, 4)
    arrays = {
        "x": a["x"], "ctx_nat": a["ctx_2048"], "ctx_half": ctx_half,
        "ctx_t": ctx_t, "ctx_one": ctx_one, "filt": filt, "bias": a["fside_S2_0"],
        "gates": np.concatenate([a["g_xattn"], a["g_ffn"]]), "w0": w0, "wr": wr, "w1": w1, "gw": gw,
        "ramp": np.arange(E, 0, -1).astype(np.float32),
    }
    arrays = {k: np.ascontiguousarray(v) for k, v in arrays.items()}
    nc = bacc.Bacc("TRN2", target_bir_lowering=False, num_devices=1)
    args = [nc.dram_tensor("in_" + k, v.shape, mybir.dt.from_np(v.dtype), kind="ExternalInput").ap() for k, v in arrays.items()]
    out = nc.dram_tensor("out", (B, P, D), F32, kind="ExternalOutput").ap()
    flamingo_kernel(nc, *args, out)
    r = run_bass_kernel_spmd(nc, [{"in_" + k: v for k, v in arrays.items()}], core_ids=[0])
    return r.results[0]["out"]
```
